# Optimizing a Trainium2 kernel written in Bass

```python
import numpy as np
import jax
import jax.numpy as jnp

def _softmax(x, axis=-1):
    return jax.nn.softmax(x, axis=axis)

def _gelu(x):
    return jax.nn.gelu(x, approximate=True)

def _silu(x):
    return jax.nn.silu(x)

def _sigmoid(x):
    return jax.nn.sigmoid(x)

def _layernorm(x, axis=-1, eps=1e-05):
    m = jnp.mean(x, axis=axis, keepdims=True)
    v = jnp.var(x, axis=axis, keepdims=True)
    return (x - m) / jnp.sqrt(v + eps)

def _scatter_add(tgt, idx, src, axis=0):
    return tgt.at[idx].add(src)

def _segment_sum(src, seg, n):
    return jax.ops.segment_sum(src, seg, n)
kernel_name = 'mk_gnn_resnorm_d2_gnn_r8_6d0a05'

def setup_inputs(seed: int=0):
    np.random.seed(seed)
    _w = jnp.asarray

    def _rec_inputs():
        import jax
        import jax.numpy as jnp
        _gk = jax.random.key(seed)
        x = -0.000202 + 1 * jax.random.normal(jax.random.fold_in(_gk, 1), (50000, 16), jnp.float32)
        _s = jax.random.randint(jax.random.fold_in(_gk, 2), (400000,), 0, 50000, jnp.int32)
        _d = jax.random.randint(jax.random.fold_in(_gk, 3), (400000,), 0, 50000, jnp.int32)
        _loop = jnp.arange(50000, dtype=jnp.int32)
        src = jnp.concatenate([_s, _d, _loop])
        dst = jnp.concatenate([_d, _s, _loop])
        _o = jnp.argsort(dst, stable=True)
        src = src[_o]
        dst = dst[_o]
        edge_type_6 = jax.random.randint(jax.random.fold_in(_gk, 13), (850000,), 0, 6, jnp.int32)
        edge_type_8 = jax.random.randint(jax.random.fold_in(_gk, 14), (850000,), 0, 8, jnp.int32)
        return (x, src, dst, edge_type_6, edge_type_8)
    x, src, dst, edge_type_6, edge_type_8 = _rec_inputs()

    def _L0_gnn_setup():
        import jax, jax.numpy as jnp
        import numpy as np
        N = 6250
        E_RAND = 200000
        IN = 8
        OUT = 8
        B = 16
        T = 5
        key = jax.random.key(seed)
        k1, k2, k3, k4, k5, k6 = jax.random.split(key, 6)
        x = jax.random.normal(k1, (N * IN, B), jnp.float32)
        loops = jnp.arange(N, dtype=jnp.int32)
        src = jnp.concatenate([loops, jax.random.randint(k2, (E_RAND,), 0, N, jnp.int32)])
        dst = jnp.concatenate([loops, jax.random.randint(k3, (E_RAND,), 0, N, jnp.int32)])
        edge_types = jnp.concatenate([jnp.ones(N, jnp.int32), jax.random.randint(k4, (E_RAND,), 2, T + 1, jnp.int32)])
        bound = 1.0 / np.sqrt(IN)
        W = jax.random.uniform(k5, (T, OUT, IN), jnp.float32, -bound, bound)
        Bv = jax.random.uniform(k6, (T, OUT), jnp.float32, -bound, bound)
        return dict(x=x, W=W, Bv=Bv, src=src, dst=dst, edge_types=edge_types)
    _L0_gnn_all = _L0_gnn_setup()
    _L0_gnn_in = {k: v for k, v in _L0_gnn_all.items() if k in ('W', 'Bv')}
    del _L0_gnn_all

    def _L1_gnn_setup():
        import jax, jax.numpy as jnp
        import numpy as np
        NUM_ENTITIES = 12500
        NUM_RELATIONS = 8
        NUM_CLASSES = 16
        HIDDEN = 16
        NUM_EDGES = 400000

        def rgcn_conv(x, src, dst, edge_type, W, root, bias):
            num_nodes = x.shape[0]
            x_src = x[src]
            msg = jnp.zeros((src.shape[0], W.shape[2]), x.dtype)
            for r in range(NUM_RELATIONS):
                msg = msg + jnp.where((edge_type == r)[:, None], x_src @ W[r], jnp.zeros((), x.dtype))
            cnt = jnp.zeros((num_nodes, NUM_RELATIONS), x.dtype).at[dst, edge_type].add(1.0)
            norm = 1.0 / jnp.maximum(cnt[dst, edge_type], 1.0)
            agg = jax.ops.segment_sum(msg * norm[:, None], dst, num_segments=num_nodes)
            return agg + x @ root + bias
        key = jax.random.key(seed)
        ks = jax.random.split(key, 9)
        s = 1.0 / np.sqrt(HIDDEN)
        edge_index = jax.random.randint(ks[0], (2, NUM_EDGES), 0, NUM_ENTITIES, dtype=jnp.int32)
        edge_type = jax.random.randint(ks[1], (NUM_EDGES,), 0, NUM_RELATIONS, dtype=jnp.int32)
        return {'embed': jax.random.normal(ks[2], (NUM_ENTITIES, HIDDEN), jnp.float32), 'W1': jax.random.normal(ks[3], (NUM_RELATIONS, HIDDEN, HIDDEN), jnp.float32) * s, 'root1': jax.random.normal(ks[4], (HIDDEN, HIDDEN), jnp.float32) * s, 'b1': jnp.zeros((HIDDEN,), jnp.float32), 'W2': jax.random.normal(ks[5], (NUM_RELATIONS, HIDDEN, NUM_CLASSES), jnp.float32) * s, 'root2': jax.random.normal(ks[6], (HIDDEN, NUM_CLASSES), jnp.float32) * s, 'b2': jnp.zeros((NUM_CLASSES,), jnp.float32), 'edge_index': edge_index, 'edge_type': edge_type}
    _L1_gnn_all = _L1_gnn_setup()
    _L1_gnn_in = {k: v for k, v in _L1_gnn_all.items() if k in ('W1', 'root1', 'b1', 'W2', 'root2', 'b2')}
    del _L1_gnn_all
    return {'x': x, 'src': src, 'dst': dst, 'edge_type_6': edge_type_6, 'edge_type_8': edge_type_8, 'L0_gnn_W': _L0_gnn_in['W'], 'L0_gnn_Bv': _L0_gnn_in['Bv'], 'L1_gnn_W1': _L1_gnn_in['W1'], 'L1_gnn_root1': _L1_gnn_in['root1'], 'L1_gnn_b1': _L1_gnn_in['b1'], 'L1_gnn_W2': _L1_gnn_in['W2'], 'L1_gnn_root2': _L1_gnn_in['root2'], 'L1_gnn_b2': _L1_gnn_in['b2']}

def reference(x, src, dst, edge_type_6, edge_type_8, L0_gnn_W, L0_gnn_Bv, L1_gnn_W1, L1_gnn_root1, L1_gnn_b1, L1_gnn_W2, L1_gnn_root2, L1_gnn_b2):
    import jax
    import jax.numpy as jnp

    def _L0_gnn_ref(x, W, Bv, src, dst, edge_types):
        import jax, jax.numpy as jnp
        import numpy as np
        N = 6250
        E_RAND = 200000
        IN = 8
        OUT = 8
        B = 16
        T = 5
        T_, OUT_, IN_ = W.shape
        Nn = x.shape[0] // IN_
        xr = x.reshape(Nn, IN_, -1)
        Wg = W[edge_types - 1]
        msg = jnp.einsum('eoi,eib->eob', Wg, xr[src])
        y = jax.ops.segment_sum(msg, dst, num_segments=Nn)
        yb = jax.ops.segment_sum(Bv[edge_types - 1], dst, num_segments=Nn)
        y = y + yb[:, :, None]
        return y.reshape(Nn * OUT_, -1)

    def _L1_gnn_ref(embed, W1, root1, b1, W2, root2, b2, edge_index, edge_type):
        import jax, jax.numpy as jnp
        import numpy as np
        NUM_ENTITIES = 12500
        NUM_RELATIONS = 8
        NUM_CLASSES = 16
        HIDDEN = 16
        NUM_EDGES = 400000

        def rgcn_conv(x, src, dst, edge_type, W, root, bias):
            num_nodes = x.shape[0]
            x_src = x[src]
            msg = jnp.zeros((src.shape[0], W.shape[2]), x.dtype)
            for r in range(NUM_RELATIONS):
                msg = msg + jnp.where((edge_type == r)[:, None], x_src @ W[r], jnp.zeros((), x.dtype))
            cnt = jnp.zeros((num_nodes, NUM_RELATIONS), x.dtype).at[dst, edge_type].add(1.0)
            norm = 1.0 / jnp.maximum(cnt[dst, edge_type], 1.0)
            agg = jax.ops.segment_sum(msg * norm[:, None], dst, num_segments=num_nodes)
            return agg + x @ root + bias
        src, dst = (edge_index[0], edge_index[1])
        h = rgcn_conv(embed, src, dst, edge_type, W1, root1, b1)
        h = jax.nn.relu(h)
        h = rgcn_conv(h, src, dst, edge_type, W2, root2, b2)
        return jax.nn.log_softmax(h, axis=1)
    edge_index = jnp.stack([src, dst])
    x = _layernorm(x + _L0_gnn_ref(x, L0_gnn_W, L0_gnn_Bv, src, dst, edge_type_6), axis=-1)
    x = _layernorm(x + _L1_gnn_ref(x, L1_gnn_W1, L1_gnn_root1, L1_gnn_b1, L1_gnn_W2, L1_gnn_root2, L1_gnn_b2, edge_index, edge_type_8), axis=-1)
    return x

_drawn_inputs = setup_inputs


def setup_inputs(seed=0):
    import zlib

    import numpy as np

    out = dict(_drawn_inputs(seed))
    spreads = {'L1_gnn_b1': (0.0, 0.1), 'L1_gnn_b2': (0.0, 0.418)}
    factors = {'L0_gnn_Bv': 8.0}
    for name, (base, spread) in spreads.items():
        noise = np.random.default_rng([zlib.crc32(name.encode()), seed]).standard_normal(out[name].shape)
        drawn = base * np.exp(spread * noise) if base else spread * noise
        out[name] = jnp.asarray(drawn.astype(out[name].dtype))
    for name, factor in factors.items():
        out[name] = (out[name] * factor).astype(out[name].dtype)
    return out
```

```python
import concourse.bass as bass
from concourse import mybir
from contextlib import ExitStack

F32 = mybir.dt.float32
BF16 = mybir.dt.bfloat16
I32 = mybir.dt.int32
ALU = mybir.AluOpType
ACT = mybir.ActivationFunctionType
AX = mybir.AxisListType

P = 128
FEAT = 16
NODES1 = 50000
EDGES = 850000
CH = 8
NODES0 = NODES1 // CH
ROW0 = CH * FEAT
TYPES0 = 5
RELS = 8
EPS = 1e-5

WIN = 64
COLS = 6656
WINS = COLS // WIN
LAST_VALID = EDGES - (P - 1) * COLS
LEAD = WIN

TILES = -(-NODES0 // P)
TAIL = NODES0 - (TILES - 1) * P
NWIN = 56
NWINS = TILES * CH // NWIN
TPW = NWIN // CH

BP, BC = 125, 68
BLOCK = BP * BC
BLOCKS = EDGES // BLOCK
HALF = ROW0 // 2
assert WINS % 2 == 0 and BLOCKS * BLOCK == EDGES and BLOCKS % 2 == 0 and NWINS * NWIN == TILES * CH
assert TILES % 2 == 1 and NWINS == 7


class Steps:

    def __init__(self, eng, sem, done=0):
        self.eng, self.sem, self.n, self.done = eng, sem, 0, done

    def __call__(self, ins):
        ins.then_inc(self.sem, 1)
        self.n += 1

    def wait(self):
        self.eng.wait_ge(self.sem, self.done + self.n)


class Scope:

    def __init__(self, nc, ctx, prefix):
        self.nc, self.ctx, self.prefix = nc, ctx, prefix

    def sb(self, name, shape, dt=F32):
        return self.ctx.enter_context(self.nc.sbuf_tensor(f"{self.prefix}_{name}", shape, dt))

    def ps(self, name, shape):
        return self.ctx.enter_context(self.nc.psum_tensor(f"{self.prefix}_{name}", shape, F32))

    def sem(self, name):
        return self.ctx.enter_context(self.nc.semaphore(f"{self.prefix}_{name}"))

    def block(self):
        return self.ctx.enter_context(self.nc.Block())


def stage_edges(nc, env):
    with ExitStack() as ctx:
        s = Scope(nc, ctx, "ed")
        dst_f = s.sb("dst_f", [P, COLS])
        typ = s.sb("typ", [P, COLS], I32)
        typ8 = dst_f[:, :].bitcast(I32)
        before = s.sb("before", [P, 1], I32)
        after = s.sb("after", [P, 1], I32)
        firsts = s.sb("firsts", [P, 2])
        flag = s.sb("flag", [P, 4])
        wide = s.sb("wide", [P, 2, P])
        lead = s.sb("lead", [1, LEAD])
        fix_base = s.sb("fix_base", [P, 1], I32)
        wide_ps = s.ps("wide_ps", [P, 2, P])
        padded, dst_in, type6_in, src_in, type8_in, small_in = map(
            s.sem, ("padded", "dst_in", "type6_in", "src_in", "type8_in", "small_in"))
        dst_used, type6_used, flags_done, stored0, stored, iotas = map(
            s.sem, ("dst_used", "type6_used", "flags_done", "stored0", "stored", "iotas"))
        idx0_ready, wide_ready, turned, step = map(s.sem, ("idx0_ready", "wide_ready", "turned", "step"))
        block = s.block()
        rows = P - 1
        split = rows * COLS

        def load(eng, to, frm, landed):
            eng.dma_start(to[0:rows, :], frm[0:split].rearrange("(p c) -> p c", p=rows)).then_inc(landed, 16)
            eng.dma_start(to[rows:P, 0:LAST_VALID],
                          frm[split:EDGES].rearrange("(p c) -> p c", p=1)).then_inc(landed, 16)

        @block.sync
        def _(sp):
            sp.wait_ge(padded, 2)
            load(sp, typ, env.dst, dst_in)
            load(sp, env.idx1, env.src, src_in)
            sp.wait_ge(dst_used, 1)
            load(sp, typ, env.type6, type6_in)
            sp.wait_ge(flags_done, 1)
            sp.dma_start(env.dst_d[LEAD:LEAD + P * COLS].rearrange("(p c) -> p c", c=COLS),
                         dst_f[:, :]).then_inc(stored, 16)
            sp.dma_start(env.dst_d[0:LEAD].rearrange("(a b) -> a b", a=1), lead[:, :]).then_inc(stored, 16)
            sp.wait_ge(stored, 32)
            sp.wait_ge(padded, 3)
            load(sp, typ8, env.type8, type8_in)
            sp.wait_ge(idx0_ready, 1)
            sp.dma_start(env.idx0_d.rearrange("(p c) -> p c", c=COLS), typ[:, :]).then_inc(stored0, 16)
            sp.wait_ge(stored0, 16)

        @block.scalar
        def _(act):
            act.wait_ge(padded, 2)
            act.dma_start(before[1:P, :], env.dst[0:rows * COLS].rearrange("(p c) -> p c", c=COLS)
                          [:, COLS - 1:COLS]).then_inc(small_in, 16)
            act.dma_start(after[0:rows - 1, :], env.dst[COLS:split].rearrange("(p c) -> p c", c=COLS)
                          [:, 0:1]).then_inc(small_in, 16)
            act.dma_start(after[rows - 1:rows, :], env.dst[split:split + 1].rearrange("(p c) -> p c", c=1)
                          ).then_inc(small_in, 16)
            act.dma_start(env.ident[:, :], env.eye).then_inc(small_in, 16)
            act.dma_start(env.block_first[0:1, 1:BLOCKS], env.dst[BLOCK:EDGES].rearrange("(k e) -> e k", e=BLOCK)
                          [0:1, :]).then_inc(small_in, 16)
            act.wait_ge(small_in, 80)

        @block.gpsimd
        def _(pool):
            nc.gpsimd.iota(fix_base[:, :], pattern=[[0, 1]], base=-1, channel_multiplier=COLS).then_inc(iotas, 1)
            nc.gpsimd.iota(env.rel_id[:, :], pattern=[[1, RELS]], base=0, channel_multiplier=0,
                           allow_small_or_imprecise_dtypes=True).then_inc(iotas, 1)

        @block.tensor
        def _(pe):
            pe.wait_ge(small_in, 80)
            pe.wait_ge(wide_ready, 2)
            for j in range(2):
                nc.tensor.transpose(wide_ps[:, j, :], wide[:, j, :], env.ident[:, :]).then_inc(turned, 1)

        @block.vector
        def _(dve):
            st = Steps(dve, step)
            tmp = env.norm
            nc.vector.memset(before[:, :], -1)
            nc.vector.memset(after[:, :], NODES1)
            nc.vector.memset(typ[:, LAST_VALID:], NODES1).then_inc(padded, 1)
            nc.vector.memset(env.idx1[:, LAST_VALID:], 0).then_inc(padded, 1)
            nc.vector.memset(lead[:, :], -1.0)
            nc.vector.memset(env.block_first[:, 0:1], 0)
            dve.wait_ge(dst_in, 32)
            st(nc.vector.tensor_copy(dst_f[:, :], typ[:, :]))
            st.wait()
            st(nc.vector.memset(typ[:, LAST_VALID:], 0))
            st.wait()
            dve.sem_inc(dst_used, 1)
            st(nc.vector.tensor_tensor(env.keep[:, 1:COLS], dst_f[:, 1:COLS], dst_f[:, 0:COLS - 1], ALU.is_equal))
            st(nc.vector.memset(env.keep[:, 0:1], 1.0))
            st(nc.vector.memset(env.keep[:, COLS:COLS + 1], 1.0))
            st(nc.vector.tensor_scalar(env.in_first[:, :], dst_f[:, :], dst_f[:, 0:1], None, ALU.is_equal))
            st(nc.vector.tensor_scalar(env.in_last[:, :], dst_f[:, :], dst_f[:, COLS - 1:COLS], None, ALU.is_equal))
            dve.wait_ge(small_in, 80)
            st(nc.vector.tensor_tensor(flag[:, 0:1], dst_f[:, 0:1], before[:, :], ALU.is_equal))
            st(nc.vector.tensor_tensor(flag[:, 1:2], dst_f[:, 0:1], dst_f[:, COLS - 1:COLS], ALU.is_equal))
            st(nc.vector.tensor_copy(env.firsts[:, 0:1], dst_f[:, 0:1]))
            st(nc.vector.tensor_copy(env.firsts[:, 1:2], after[:, :]))
            st.wait()
            nc.vector.memset(env.firsts[0:1, 0:1], -1.0)
            dve.sem_inc(flags_done, 1)
            st(nc.vector.tensor_reduce(flag[:, 2:3], env.in_first[:, :], AX.X, ALU.add))
            for j in range(2):
                nc.vector.tensor_copy(wide[:, j, :], flag[:, j:j + 1].to_broadcast([P, P])).then_inc(wide_ready, 1)
            st.wait()
            dve.wait_ge(iotas, 2)
            st(nc.vector.tensor_tensor(env.fix_idx[:, :], fix_base[:, :], flag[:, 2:3], ALU.add))
            dve.wait_ge(turned, 2)
            st(nc.vector.tensor_copy(env.cont_row[:, :], wide_ps[:, 0, :]))
            st(nc.vector.memset(env.pass_row[:, :], 0.0))
            st(nc.vector.memset(env.back_row[:, :], 0.0))
            st.wait()
            st(nc.vector.tensor_tensor(env.pass_row[:, 1:P], env.cont_row[:, 1:P], wide_ps[:, 1, 0:P - 1], ALU.mult))
            st(nc.vector.tensor_tensor(env.back_row[:, 0:P - 1], env.cont_row[:, 1:P], wide_ps[:, 1, 1:P], ALU.mult))
            dve.wait_ge(type6_in, 32)
            st(nc.vector.tensor_scalar(tmp[:, :], typ[:, :], 0.0, float(TYPES0), ALU.is_equal, ALU.mult))
            st.wait()
            st(nc.vector.scalar_tensor_tensor(tmp[:, :], typ[:, :], -1.0, tmp[:, :], ALU.add, ALU.add))
            dve.wait_ge(src_in, 32)
            st.wait()
            st(nc.vector.tensor_scalar(typ[:, :], env.idx1[:, :], float(NODES0 - 1), float(TYPES0), ALU.min, ALU.mult))
            st.wait()
            nc.vector.tensor_tensor(typ[:, :], typ[:, :], tmp[:, :], ALU.add).then_inc(idx0_ready, 1)
            dve.wait_ge(stored, 32)
            st(nc.vector.memset(typ8[:, LAST_VALID:], 0))
            st.wait()
            dve.sem_inc(padded, 1)
            dve.wait_ge(type8_in, 32)
            st(nc.vector.scalar_tensor_tensor(env.idx1[:, :], env.idx1[:, :], float(RELS), typ8,
                                              ALU.mult, ALU.add))
            st(nc.vector.tensor_copy(env.rel[:, :], typ8))
            st.wait()


def stage_norm(nc, env):
    with ExitStack() as ctx:
        s = Scope(nc, ctx, "no")
        count = s.sb("count", [P, COLS])
        mine = s.sb("mine", [P, COLS], BF16)
        part = s.sb("part", [P, COLS], BF16)
        ends = s.sb("ends", [P, 2, RELS])
        carry_in = s.sb("carry_in", [RELS, 2, P])
        carry_row = s.sb("carry_row", [RELS, 2, P])
        carry = s.sb("carry", [P, 2, RELS])
        ends_ps = s.ps("ends_ps", [RELS, 2, P])
        carry_ps = s.ps("carry_ps", [P, 2, RELS])
        fill = BLOCK * HALF // P
        zeros = s.sb("zeros", [P, fill])
        zeroed, filled = map(s.sem, ("zeroed", "filled"))
        summed, turned, rows_ready, returned = map(s.sem, ("summed", "turned", "rows_ready", "returned"))
        step1, step2, step3 = map(s.sem, ("step1", "step2", "step3"))
        block = s.block()

        @block.scalar
        def _(act):
            act.wait_ge(zeroed, 1)
            with act.Fori(0, BLOCKS) as k:
                first_dst = act.value_load(env.block_first[0:1, bass.ds(k, 1)])
                with act.If(first_dst >= NODES0):
                    for h in range(2):
                        act.dma_start(env.sums0[h].rearrange("e f -> (e f)")[bass.ds(k * (BLOCK * HALF), BLOCK * HALF)]
                                      .rearrange("(p c) -> p c", p=P), zeros[:, :]).then_inc(filled, 16)
                with act.If(first_dst < NODES0):
                    act.sem_inc(filled, 32)
            act.wait_ge(filled, 32 * BLOCKS)

        @block.tensor
        def _(pe):
            pe.wait_ge(summed, RELS)
            for j in range(2):
                nc.tensor.transpose(ends_ps[:, j, :], ends[:, j, :], env.ident[:, :]).then_inc(turned, 1)
            pe.wait_ge(rows_ready, 2)
            for j in range(2):
                nc.tensor.transpose(carry_ps[:, j, :], carry_row[:, j, :],
                                    env.ident[0:RELS, 0:RELS]).then_inc(returned, 1)

        @block.vector
        def _(dve):
            nc.vector.memset(zeros[:, :], 0.0).then_inc(zeroed, 1)
            per = 5
            with dve.Fori(0, RELS) as r:
                st = Steps(dve, step1, r * per)
                mask = mine[:, :]
                rel = env.rel_id[:, bass.ds(r, 1)]
                st(nc.vector.tensor_scalar(mask, env.rel[:, :], rel, None, ALU.is_equal))
                for j, seg in enumerate((env.in_first, env.in_last)):
                    st.wait()
                    st(nc.vector.tensor_tensor(part[:, :], mask, seg[:, :], ALU.mult))
                    st.wait()
                    st(nc.vector.tensor_reduce(ends[:, j, bass.ds(r, 1)], part[:, :], AX.X, ALU.add))
                st.wait()
                dve.sem_inc(summed, 1)
                assert st.n == per
            st = Steps(dve, step2)
            st(nc.vector.memset(carry_in[:, :, :], 0.0))
            st(nc.vector.memset(env.norm[:, :], -1.0))
            dve.wait_ge(turned, 2)
            st.wait()
            st(nc.vector.tensor_tensor(carry_in[:, 0, 1:P], env.cont_row[0:RELS, 1:P], ends_ps[:, 1, 0:P - 1], ALU.mult))
            st(nc.vector.tensor_tensor(carry_in[:, 1, 0:P - 1], env.cont_row[0:RELS, 1:P], ends_ps[:, 0, 1:P], ALU.mult))
            st.wait()
            nc.vector.tensor_tensor_scan(carry_row[:, 0, :], env.pass_row[0:RELS, :], carry_in[:, 0, :], 0.0,
                                         ALU.mult, ALU.add).then_inc(rows_ready, 1)
            nc.vector.tensor_tensor_scan(carry_row[:, 1, ::-1], env.back_row[0:RELS, ::-1], carry_in[:, 1, ::-1], 0.0,
                                         ALU.mult, ALU.add).then_inc(rows_ready, 1)
            dve.wait_ge(returned, 2)
            st(nc.vector.tensor_copy(carry[:, :, :], carry_ps[:, :, :]))
            st.wait()
            per = 7
            with dve.Fori(0, RELS) as r:
                st = Steps(dve, step3, r * per)
                mask = mine[:, :]
                st(nc.vector.tensor_scalar(mask, env.rel[:, :], env.rel_id[:, bass.ds(r, 1)], None, ALU.is_equal))
                st.wait()
                for j in range(2):
                    way = slice(None, None, 1 - 2 * j)
                    keep = env.keep[:, j:COLS + j]
                    st(nc.vector.tensor_tensor_scan(count[:, way], keep[:, way], mask[:, way],
                                                    carry[:, j, bass.ds(r, 1)], ALU.mult, ALU.add))
                    st.wait()
                    st(nc.vector.tensor_tensor(count[:, :], count[:, :], mask, ALU.mult))
                    st.wait()
                    st(nc.vector.tensor_tensor(env.norm[:, :], env.norm[:, :], count[:, :], ALU.add))
                    st.wait()
                assert st.n == per
            st = Steps(dve, step2, 6)
            st.n = -2
            st(nc.vector.tensor_scalar_max(env.norm[:, :], env.norm[:, :], 1.0))
            dve.wait_ge(step2, 6)
            nc.vector.reciprocal(env.norm[:, :], env.norm[:, :])


def stage_rank(nc, env):
    slots = TILES * CH
    with ExitStack() as ctx:
        s = Scope(nc, ctx, "rk")
        node_i = s.sb("node_i", [P, slots], I32)
        node = s.sb("node", [P, slots])
        tile_base = s.sb("tile_base", [P, TILES])
        in_tile = s.sb("in_tile", [P, CH, P], F32)
        first_t = s.sb("first_t", [P, TILES])
        samples = s.sb("samples", [P, WINS])
        shifted = s.sb("shifted", [P, WINS])
        pick = s.sb("pick", [P, WINS + 1])
        reached = s.sb("reached", [P, 2, CH, P])
        below = s.sb("below", [P, CH, WINS])
        part_no = s.sb("part_no", [P, slots])
        win_no = s.sb("win_no", [P, slots])
        win_idx = s.sb("win_idx", [P, slots], I32)
        idx_win = s.sb("idx_win", [P, 2, NWIN], I32)
        got = s.sb("got", [P, 2, NWIN, WIN])
        cmp = s.sb("cmp", [P, NWIN, WIN])
        n_le = s.sb("n_le", [P, slots])
        n_eq = s.sb("n_eq", [P, slots])
        picked = [s.ps(f"picked{b}", [P, 2, 4, P]) for b in range(2)]
        iotas, loaded, pick_ready, reached_ready, picked_done, picked_used = map(
            s.sem, ("iotas", "loaded", "pick_ready", "reached_ready", "picked_done", "picked_used"))
        prep, step, step2, idx_ready, claimed, step3, step4, stored = map(
            s.sem, ("prep", "step", "step2", "idx_ready", "claimed", "step3", "step4", "stored"))
        landed = [s.sem(f"landed{b}") for b in range(2)]
        block = s.block()
        dst_rows = env.dst_d.rearrange("(r c) -> r c", c=WIN)

        @block.sync
        def _(sp):
            src = dst_rows[1:1 + P * WINS, 0:1].rearrange("(p j) c -> p (j c)", j=WINS)
            sp.wait_ge(prep, 1)
            sp.dma_start(samples[:, :], src).then_inc(loaded, 16)
            sp.dma_start(shifted[1:P, :], src[0:P - 1, :]).then_inc(loaded, 16)
            sp.wait_ge(step4, 4)
            sp.dma_start(env.end_d[0:(TILES - 1) * P * CH].rearrange("(t n o) -> n t o", n=P, o=CH),
                         env.end_idx[:, 0:(TILES - 1) * CH].rearrange("n (t o) -> n t o", o=CH)).then_inc(stored, 16)
            sp.dma_start(env.some_d[0:(TILES - 1) * P * CH].rearrange("(t n o) -> n t o", n=P, o=CH),
                         env.has_edge[:, 0:(TILES - 1) * CH].rearrange("n (t o) -> n t o", o=CH)).then_inc(stored, 16)
            sp.wait_ge(stored, 32)
            for to, frm in ((env.end0, env.end_d), (env.some0, env.some_d)):
                sp.dma_start(to[:, 0:TILES - 1], frm[0:(TILES - 1) * P].rearrange("(t n) -> n t", n=P)).then_inc(stored, 16)
                sp.dma_start(to[0:TAIL, TILES - 1:TILES],
                             frm[(TILES - 1) * P:NODES0].rearrange("(n t) -> n t", t=1)).then_inc(stored, 16)
            sp.wait_ge(stored, 96)

        @block.gpsimd
        def _(pool):
            nc.gpsimd.iota(node_i[:, :], pattern=[[P * CH, TILES], [1, CH]], base=0,
                           channel_multiplier=CH).then_inc(iotas, 1)
            nc.gpsimd.iota(tile_base[:, :], pattern=[[P * CH, TILES]], base=0, channel_multiplier=0,
                           allow_small_or_imprecise_dtypes=True).then_inc(iotas, 1)
            nc.gpsimd.iota(in_tile[:, :, :], pattern=[[1, CH], [CH, P]], base=0, channel_multiplier=0,
                           allow_small_or_imprecise_dtypes=True).then_inc(iotas, 1)

            def window(b, ready):
                pool.wait_ge(idx_ready, ready)
                pool.sem_inc(claimed, 1)
                for j in range(NWIN):
                    pool.indirect_dma_start(
                        out=got[:, b, j, :], out_offset=None, in_=dst_rows,
                        in_offset=bass.IndirectOffsetOnAxis(ap=idx_win[:, b, j:j + 1], axis=0)
                    ).then_inc(landed[b], 16)

            window(0, 1)
            with pool.Fori(0, NWINS // 2) as i:
                window(1, i * 2 + 2)
                window(0, i * 2 + 3)

        @block.tensor
        def _(pe):
            def tile(b, ready, free):
                pe.wait_ge(reached_ready, ready)
                if free is not None:
                    pe.wait_ge(picked_used, free)
                for o in range(CH):
                    last = nc.tensor.matmul(picked[b][:, o // 4, o % 4, 0:WINS + 1], reached[:, b, o, :],
                                            pick[:, :], start=True, stop=True)
                last.then_inc(picked_done, 1)

            pe.wait_ge(pick_ready, 1)
            tile(0, 1, None)
            tile(1, 2, None)
            with pe.Fori(1, TILES // 2) as i:
                tile(0, i * 2 + 1, i * 2 - 1)
                tile(1, i * 2 + 2, i * 2)
            tile(0, TILES, TILES - 2)

        @block.vector
        def _(dve):
            st = Steps(dve, step)
            nc.vector.memset(shifted[0:1, :], 0.0).then_inc(prep, 1)
            st(nc.vector.memset(env.end0[:, :], 0))
            st(nc.vector.memset(env.some0[:, :], 0.0))
            dve.wait_ge(iotas, 3)
            st(nc.vector.tensor_copy(node[:, :], node_i[:, :]))
            st(nc.vector.tensor_scalar(first_t[:, :], tile_base[:, :], -1.0, env.firsts[:, 0:1], ALU.mult, ALU.add))
            dve.wait_ge(loaded, 32)
            st(nc.vector.tensor_tensor(pick[:, 0:WINS], samples[:, :], shifted[:, :], ALU.subtract))
            st(nc.vector.memset(pick[:, WINS:WINS + 1], 1.0))
            st.wait()
            dve.sem_inc(pick_ready, 1)

            def reach(b, t):
                nc.vector.tensor_scalar(reached[:, b, :, :], in_tile[:, :, :], first_t[:, bass.ds(t, 1)], None,
                                        ALU.is_ge).then_inc(reached_ready, 1)

            per = 3

            def count(b, t, done):
                dve.wait_ge(picked_done, t + 1)
                st2 = Steps(dve, step2, t * per)
                at = bass.ds(t * CH, CH)
                st2(nc.vector.tensor_tensor(
                    below[:, :, :].rearrange("n (a c) j -> n a c j", a=2), picked[b][:, :, :, 0:WINS],
                    node[:, at].rearrange("n (a c) -> n a c", a=2).unsqueeze(3).to_broadcast([P, 2, 4, WINS]),
                    ALU.is_le))
                st2(nc.vector.tensor_copy(part_no[:, at].rearrange("n (a c) -> n a c", a=2),
                                          picked[b][:, :, :, WINS]))
                st2.wait()
                dve.sem_inc(picked_used, 1)
                st2(nc.vector.tensor_reduce(win_no[:, at], below[:, :, :], AX.X, ALU.add))
                st2.wait()
                assert st2.n == per

            reach(0, 0)
            reach(1, 1)
            with dve.Fori(0, TILES // 2 - 1) as i:
                for b in range(2):
                    count(b, i * 2 + b, None)
                    reach(b, i * 2 + b + 2)
            count(0, TILES - 3, None)
            reach(0, TILES - 1)
            count(1, TILES - 2, None)
            count(0, TILES - 1, None)

            st3 = Steps(dve, step3)
            st3(nc.vector.tensor_scalar(win_no[:, :], win_no[:, :], -1.0, 0.0, ALU.add, ALU.max))
            st3(nc.vector.tensor_scalar(part_no[:, :], part_no[:, :], -1.0, float(WINS), ALU.add, ALU.mult))
            st3.wait()
            st3(nc.vector.tensor_tensor(part_no[:, :], part_no[:, :], win_no[:, :], ALU.add))
            st3.wait()
            st3(nc.vector.tensor_scalar(win_idx[:, :], part_no[:, :], float(LEAD // WIN), None, ALU.add))
            st3.wait()
            for b in range(2):
                nc.vector.tensor_copy(idx_win[:, b, :], win_idx[:, b * NWIN:(b + 1) * NWIN]).then_inc(idx_ready, 1)

            base = 4
            per_w = 4

            def compare(b, w, arrived, more):
                dve.wait_ge(landed[b], arrived)
                st4 = Steps(dve, step3, base + w * per_w)
                at = bass.ds(w * NWIN, NWIN)
                want = node[:, at].unsqueeze(2).to_broadcast([P, NWIN, WIN])
                for op, to in ((ALU.is_le, n_le), (ALU.is_equal, n_eq)):
                    st4(nc.vector.tensor_tensor(cmp[:, :, :], got[:, b, :, :], want, op))
                    st4.wait()
                    st4(nc.vector.tensor_reduce(to[:, at], cmp[:, :, :], AX.X, ALU.add))
                    st4.wait()
                if more:
                    nc.vector.tensor_copy(idx_win[:, b, :],
                                          win_idx[:, bass.ds((w + 2) * NWIN, NWIN)]).then_inc(idx_ready, 1)
                assert st4.n == per_w

            full = 16 * NWIN
            with dve.Fori(0, NWINS // 2 - 1) as i:
                for b in range(2):
                    compare(b, i * 2 + b, (i + 1) * full, True)
            compare(0, NWINS - 3, (NWINS // 2) * full, True)
            compare(1, NWINS - 2, (NWINS // 2) * full, False)
            compare(0, NWINS - 1, (NWINS // 2 + 1) * full, False)
            st5 = Steps(dve, step4)
            st5(nc.vector.tensor_scalar(n_le[:, :], n_le[:, :], -1.0, None, ALU.add))
            st5(nc.vector.tensor_scalar(env.has_edge[:, :], n_eq[:, :], 1.0, None, ALU.min))
            st5.wait()
            st5(nc.vector.scalar_tensor_tensor(n_le[:, :], part_no[:, :], float(WIN), n_le[:, :], ALU.mult, ALU.add))
            st5.wait()
            st5(nc.vector.tensor_tensor(env.end_idx[:, :], n_le[:, :], env.has_edge[:, :], ALU.mult))


def stage_table(nc, env, name, x_sb, weights, bias, table, types, root):
    width = TYPES0 * ROW0 if root is None else CH * RELS * FEAT
    pieces = [(a, min(a + 512, width)) for a in range(0, width, 512)]
    if root is not None:
        pieces.append((width, width + ROW0))
    total = pieces[-1][1]
    biased = len(pieces) if root is None else 1
    with ExitStack() as ctx:
        s = Scope(nc, ctx, name)
        mix = s.sb("mix", [P, total])
        rep = s.sb("rep", [P, 160])
        slot = s.sb("slot", [P, CH])
        lane = s.sb("lane", [P, FEAT])
        bias_in = s.sb("bias_in", [P, TYPES0 * CH])
        bias_w = s.sb("bias_w", [P, width if root is None else ROW0])
        xt = s.sb("xt", [P, 2, P])
        x_turned = s.sb("x_turned", [P, 2, P])
        out = s.sb("out", [P, 2, width])
        turn_ps = [s.ps(f"turn_ps{b}", [P, 512]) for b in range(2)]
        mul_ps = [s.ps(f"mul_ps{b}", [P, len(pieces), 512]) for b in range(2)]
        loaded, mix_ready, staged, turned, back, multiplied, out_a, out_b, step, zeroed = map(
            s.sem, ("loaded", "mix_ready", "staged", "turned", "back", "multiplied", "out_a", "out_b", "step",
                    "zeroed"))
        stored = [s.sem(f"stored{b}") for b in range(2)]
        block = s.block()
        flat = table.rearrange("(n r) f -> n (r f)", n=NODES0)
        n_loads = 0
        if root is None:
            w_dram, b_dram = weights, bias
        else:
            (w_dram, root_dram), b_dram = weights, bias

        @block.sync
        def _(sp):
            if root is None:
                sp.wait_ge(zeroed, 1)
                sp.dma_start(x_sb[:, 0:TILES - 1, :], env.x[0:(TILES - 1) * P * CH, :]
                             .rearrange("(t n o) b -> n t (o b)", n=P, o=CH)).then_inc(loaded, 16)
                sp.dma_start(x_sb[0:TAIL, TILES - 1, :], env.x[(TILES - 1) * P * CH:NODES1, :]
                             .rearrange("(n o) b -> n (o b)", o=CH)).then_inc(loaded, 16)
                for i in range(CH):
                    sp.dma_start(rep[i * FEAT:(i + 1) * FEAT, 0:TYPES0 * CH],
                                 w_dram[i:i + 1, :].to_broadcast([FEAT, TYPES0 * CH])).then_inc(loaded, 16)
                sp.dma_start(bias_in[:, :], b_dram.rearrange("(a t) o -> a (t o)", a=1)
                             .to_broadcast([P, TYPES0 * CH])).then_inc(loaded, 16)
            else:
                for i in range(CH):
                    sp.dma_start(rep[i * FEAT:(i + 1) * FEAT, 0:RELS * FEAT].rearrange("b (r c) -> b r c", c=FEAT),
                                 w_dram.rearrange("r b c -> b r c")).then_inc(loaded, 16)
                    sp.dma_start(rep[i * FEAT:(i + 1) * FEAT, RELS * FEAT:(RELS + 1) * FEAT],
                                 root_dram).then_inc(loaded, 16)
                sp.dma_start(bias_in[:, 0:FEAT], b_dram.rearrange("(a c) -> a c", a=1)
                             .to_broadcast([P, FEAT])).then_inc(loaded, 16)

            def store(b, t, done, rows, at):
                sp.wait_ge(out_a, done)
                sp.wait_ge(out_b, done)
                sp.dma_start(flat[at, :], out[0:rows, b, :]).then_inc(stored[b], 16)

            with sp.Fori(0, TILES // 2) as i:
                for b in range(2):
                    store(b, None, i * 2 + b + 1, P, bass.ds((i * 2 + b) * P, P))
            store(0, None, TILES, TAIL, slice((TILES - 1) * P, NODES0))
            sp.wait_ge(stored[0], 16 * (TILES // 2 + 1))
            sp.wait_ge(stored[1], 16 * (TILES // 2))

        all_loaded = 16 * (2 + CH + 1) if root is None else 16 * (2 * CH + 1)

        @block.tensor
        def _(pe):
            pe.wait_ge(mix_ready, 1)

            def tile(b, n, read):
                if read is not None:
                    pe.wait_ge(out_a, read)
                    pe.wait_ge(out_b, read)
                pe.wait_ge(staged, n)
                nc.tensor.transpose(turn_ps[b][:, 0:P], xt[:, b, :], env.ident[:, :]).then_inc(turned, 1)
                pe.wait_ge(back, n)
                for j, (a, z) in enumerate(pieces):
                    last = nc.tensor.matmul(mul_ps[b][:, j, 0:z - a], x_turned[:, b, :], mix[:, a:z],
                                            start=True, stop=True)
                last.then_inc(multiplied, 1)

            tile(0, 1, None)
            tile(1, 2, None)
            with pe.Fori(1, TILES // 2) as i:
                for b in range(2):
                    tile(b, i * 2 + b + 1, i * 2 + b - 1)
            tile(0, TILES, TILES - 2)

        @block.scalar
        def _(act):
            def tile(b, n, free):
                act.wait_ge(multiplied, n)
                if free is not None:
                    act.wait_ge(stored[b], free)
                if root is None:
                    act.wait_ge(out_b, n)
                    act.sem_inc(out_a, 1)
                else:
                    nc.scalar.copy(out[:, b, 512:1024], mul_ps[b][:, 1, :]).then_inc(out_a, 1)

            tile(0, 1, None)
            tile(1, 2, None)
            with act.Fori(1, TILES // 2) as i:
                for b in range(2):
                    tile(b, i * 2 + b + 1, i * 16)
            tile(0, TILES, (TILES // 2) * 16)

        @block.vector
        def _(dve):
            st = Steps(dve, step)
            if root is None:
                nc.vector.memset(x_sb[:, TILES - 1, :], 0.0).then_inc(zeroed, 1)
            eye = env.ident[:, :].rearrange("p (o b) -> p o b", b=FEAT)
            st(nc.vector.tensor_reduce(slot[:, :], eye, AX.X, ALU.add))
            st(nc.vector.tensor_reduce(lane[:, :], env.ident[:, :].rearrange("p (o b) -> p b o", b=FEAT), AX.X, ALU.add))
            dve.wait_ge(loaded, all_loaded)
            st.wait()
            if root is None:
                m = mix[:, :].rearrange("p (k b) -> p k b", b=FEAT)
                st(nc.vector.tensor_tensor(m, rep[:, 0:TYPES0 * CH].unsqueeze(2).to_broadcast([P, TYPES0 * CH, FEAT]),
                                           lane[:, :].unsqueeze(1).to_broadcast([P, TYPES0 * CH, FEAT]), ALU.mult))
                st(nc.vector.tensor_copy(bias_w[:, :].rearrange("p (k b) -> p k b", b=FEAT),
                                         bias_in[:, :].unsqueeze(2).to_broadcast([P, TYPES0 * CH, FEAT])))
            else:
                for o in range(CH):
                    st(nc.vector.tensor_scalar(mix[:, o * P:(o + 1) * P], rep[:, 0:P], slot[:, o:o + 1], None, ALU.mult))
                    st(nc.vector.tensor_scalar(mix[:, width + o * FEAT:width + (o + 1) * FEAT], rep[:, P:P + FEAT],
                                               slot[:, o:o + 1], None, ALU.mult))
                st(nc.vector.tensor_copy(bias_w[:, :].rearrange("p (k b) -> p k b", b=FEAT),
                                         bias_in[:, 0:FEAT].unsqueeze(1).to_broadcast([P, CH, FEAT])))
            st.wait()
            dve.sem_inc(mix_ready, 1)

            def tile(b, t, n, free):
                nc.vector.tensor_copy(xt[:, b, :], x_sb[:, t, :]).then_inc(staged, 1)
                dve.wait_ge(turned, n)
                nc.vector.tensor_copy(x_turned[:, b, :], turn_ps[b][:, 0:P]).then_inc(back, 1)
                dve.wait_ge(multiplied, n)
                if free is not None:
                    dve.wait_ge(stored[b], free)
                if root is None:
                    for j, (a, z) in enumerate(pieces):
                        last = nc.vector.tensor_tensor(out[:, b, a:z], mul_ps[b][:, j, 0:z - a], bias_w[:, a:z], ALU.add)
                    last.then_inc(out_b, 1)
                else:
                    nc.vector.tensor_tensor(root[:, t, :], mul_ps[b][:, 2, 0:ROW0], bias_w[:, :], ALU.add)
                    nc.vector.tensor_copy(out[:, b, 0:512], mul_ps[b][:, 0, :]).then_inc(out_b, 1)

            tile(0, 0, 1, None)
            tile(1, 1, 2, None)
            with dve.Fori(1, TILES // 2) as i:
                for b in range(2):
                    tile(b, bass.ds(i * 2 + b, 1), i * 2 + b + 1, i * 16)
            tile(0, TILES - 1, TILES, (TILES // 2) * 16)


def stage_sum0(nc, env):
    with ExitStack() as ctx:
        s = Scope(nc, ctx, "s0")
        rows = s.sb("rows", [BP, 2, BC, ROW0])
        idx = s.sb("idx", [BP, 2, BC], I32)
        dst = s.sb("dst", [BP, 2, BC + 1])
        keep = s.sb("keep", [BP, BC])
        first = s.sb("first", [BP, BC])
        flag = s.sb("flag", [BP, 2])
        wide = s.sb("wide", [BP, 2, P])
        cont = s.sb("cont", [P, BP])
        through = s.sb("through", [P, BP])
        passed = s.sb("passed", [P, BP])
        last = s.sb("last", [P, BP + 1])
        carry_in = s.sb("carry_in", [P, BP])
        carry_row = s.sb("carry_row", [P, BP])
        carry = s.sb("carry", [BP, P])
        wide_ps = s.ps("wide_ps", [P, 2, P])
        last_ps = s.ps("last_ps", [P, P])
        carry_ps = s.ps("carry_ps", [P, P])
        wide_ready, wide_turned, scanned, last_turned, carry_ready, carry_back, summed, claimed = map(
            s.sem, ("wide_ready", "wide_turned", "scanned", "last_turned", "carry_ready", "carry_back",
                    "summed", "claimed"))
        start, step, finished = map(s.sem, ("start", "step", "finished"))
        loaded = [s.sem(f"loaded{b}") for b in range(2)]
        landed = [s.sem(f"landed{b}") for b in range(2)]
        stored = [s.sem(f"stored{b}") for b in range(2)]
        block = s.block()

        def each_block(eng, body):
            def one(b, i, k):
                first_dst = eng.value_load(env.block_first[0:1, bass.ds(k, 1)] if not isinstance(k, int)
                                           else env.block_first[0:1, k:k + 1])
                with eng.If(first_dst < NODES0):
                    body(b, i, k)
            one(0, 0, 0)
            one(1, 0, 1)
            with eng.Fori(1, BLOCKS // 2) as i:
                for b in range(2):
                    one(b, i, i * 2 + b)

        @block.sync
        def _(sp):
            def body(b, i, k):
                if not isinstance(k, int):
                    sp.wait_ge(stored[b], i * 32)
                at = k * BLOCK
                sp.dma_start(idx[:, b, :], env.idx0_d[bass.ds(at, BLOCK)].rearrange("(p c) -> p c", c=BC)
                             ).then_inc(loaded[b], 16)
                sp.dma_start(dst[:, b, 1:BC + 1], env.dst_d[bass.ds(at + LEAD, BLOCK)]
                             .rearrange("(p c) -> p c", c=BC)).then_inc(loaded[b], 16)
                sp.dma_start(dst[:, b, 0:1], env.dst_d[bass.ds(at + LEAD - 1, BLOCK)]
                             .rearrange("(p c) -> p c", c=BC)[:, 0:1]).then_inc(loaded[b], 16)
            each_block(sp, body)

        @block.gpsimd
        def _(pool):
            def body(b, i, k):
                pool.wait_ge(loaded[b], (i + 1) * 48)
                pool.sem_inc(claimed, 1)
                for c in range(BC):
                    pool.indirect_dma_start(
                        out=rows[:, b, c, :], out_offset=None, in_=env.table0,
                        in_offset=bass.IndirectOffsetOnAxis(ap=idx[:, b, c:c + 1], axis=0)
                    ).then_inc(landed[b], 16)
            each_block(pool, body)

        @block.tensor
        def _(pe):
            def body(b, i, k):
                pe.wait_ge(wide_ready, k + 1)
                for j in range(2):
                    mm = nc.tensor.transpose(wide_ps[:, j, 0:BP], wide[:, j, :], env.ident[0:BP, 0:BP])
                mm.then_inc(wide_turned, 1)
                pe.wait_ge(scanned, k + 1)
                nc.tensor.transpose(last_ps[:, 0:BP], rows[:, b, BC - 1, :], env.ident[0:BP, 0:BP]
                                    ).then_inc(last_turned, 1)
                pe.wait_ge(carry_ready, k + 1)
                nc.tensor.transpose(carry_ps[0:BP, :], carry_row[:, :], env.ident[:, :]).then_inc(carry_back, 1)
            each_block(pe, body)

        @block.scalar
        def _(act):
            def body(b, i, k):
                act.wait_ge(summed, k + 1)
                for h in range(2):
                    act.dma_start(env.sums0[h][bass.ds(k * BLOCK, BLOCK) if not isinstance(k, int)
                                               else slice(k * BLOCK, (k + 1) * BLOCK), :]
                                  .rearrange("(p c) f -> p c f", c=BC),
                                  rows[:, b, :, h * HALF:(h + 1) * HALF]).then_inc(stored[b], 16)
                act.wait_ge(stored[b], (i + 1) * 32)
                act.sem_inc(finished, 1)
            each_block(act, body)

        @block.vector
        def _(dve):
            nc.vector.memset(last[:, 0:1], 0.0).then_inc(start, 1)
            dve.wait_ge(start, 1)
            per = 14 + 1

            def body(b, i, k):
                st = Steps(dve, step, k * per)
                dve.wait_ge(loaded[b], (i + 1) * 48)
                st(nc.vector.tensor_tensor(keep[:, :], dst[:, b, 1:BC + 1], dst[:, b, 0:BC], ALU.is_equal))
                st(nc.vector.tensor_scalar(first[:, :], dst[:, b, 1:BC + 1], dst[:, b, 1:2], None, ALU.is_equal))
                st(nc.vector.tensor_tensor(flag[:, 1:2], dst[:, b, 1:2], dst[:, b, BC:BC + 1], ALU.is_equal))
                st.wait()
                st(nc.vector.tensor_copy(wide[:, 0, :], keep[:, 0:1].to_broadcast([BP, P])))
                st(nc.vector.tensor_copy(wide[:, 1, :], flag[:, 1:2].to_broadcast([BP, P])))
                st.wait()
                dve.sem_inc(wide_ready, 1)
                dve.wait_ge(wide_turned, k + 1)
                st(nc.vector.tensor_copy(cont[:, :], wide_ps[:, 0, 0:BP]))
                st(nc.vector.tensor_copy(through[:, :], wide_ps[:, 1, 0:BP]))
                st(nc.vector.memset(passed[:, 0:1], 0.0))
                st.wait()
                st(nc.vector.tensor_tensor(passed[:, 1:BP], cont[:, 1:BP], through[:, 0:BP - 1], ALU.mult))
                dve.wait_ge(landed[b], (i + 1) * (16 * BC))
                for f in range(ROW0):
                    one = nc.vector.tensor_tensor_scan(rows[:, b, :, f], keep[:, :], rows[:, b, :, f], 0.0,
                                                       ALU.mult, ALU.add)
                one.then_inc(scanned, 1)
                dve.wait_ge(last_turned, k + 1)
                st(nc.vector.tensor_copy(last[:, 1:BP + 1], last_ps[:, 0:BP]))
                st.wait()
                st(nc.vector.tensor_tensor(carry_in[:, :], cont[:, :], last[:, 0:BP], ALU.mult))
                st.wait()
                nc.vector.tensor_tensor_scan(carry_row[:, :], passed[:, :], carry_in[:, :], 0.0,
                                             ALU.mult, ALU.add).then_inc(carry_ready, 1)
                dve.wait_ge(carry_ready, k + 1)
                st(nc.vector.scalar_tensor_tensor(last[:, 0:1], carry_row[:, BP - 1:BP], through[:, BP - 1:BP],
                                                  last[:, BP:BP + 1], ALU.mult, ALU.add))
                dve.wait_ge(carry_back, k + 1)
                st(nc.vector.tensor_copy(carry[:, :], carry_ps[0:BP, :]))
                st.wait()
                for c in range(BC):
                    one = nc.vector.scalar_tensor_tensor(rows[:, b, c, :], carry[:, :], first[:, c:c + 1],
                                                         rows[:, b, c, :], ALU.mult, ALU.add)
                st(one)
                st.wait()
                dve.sem_inc(summed, 1)
                assert st.n == 14, st.n
            per = 14
            each_block(dve, body)


def layer_norm(nc, st, x, sq, mean, var, slots, act_root):
    stat = lambda t: t.unsqueeze(2).to_broadcast([P, slots, FEAT])
    st(nc.vector.tensor_reduce(mean, x, AX.X, ALU.add))
    st.wait()
    st(nc.vector.tensor_scalar(mean, mean, 1.0 / FEAT, None, ALU.mult))
    st.wait()
    st(nc.vector.tensor_tensor(x, x, stat(mean), ALU.subtract))
    st.wait()
    st(nc.vector.tensor_tensor(sq, x, x, ALU.mult))
    st.wait()
    st(nc.vector.tensor_reduce(var, sq, AX.X, ALU.add))
    st.wait()
    st(nc.vector.tensor_scalar(var, var, 1.0 / FEAT, EPS, ALU.mult, ALU.add))
    st.wait()
    act_root()
    st(nc.vector.reciprocal(var, var))
    st.wait()
    st(nc.vector.tensor_tensor(x, x, stat(var), ALU.mult))
    st.wait()


def stage_nodes0(nc, env):
    slots = TILES * CH
    with ExitStack() as ctx:
        s = Scope(nc, ctx, "n0")
        total = s.sb("total", [P, TILES, ROW0])
        mean = s.sb("mean", [P, slots])
        var = s.sb("var", [P, slots])
        landed, step, var_ready, rooted = map(s.sem, ("landed", "step", "var_ready", "rooted"))
        block = s.block()

        @block.gpsimd
        def _(pool):
            for t in range(TILES):
                for h in range(2):
                    pool.indirect_dma_start(
                        out=total[:, t, h * HALF:(h + 1) * HALF], out_offset=None, in_=env.sums0[h],
                        in_offset=bass.IndirectOffsetOnAxis(ap=env.end0[:, t:t + 1], axis=0)
                    ).then_inc(landed, 16)
            pool.wait_ge(landed, 16 * 2 * TILES)

        @block.scalar
        def _(act):
            act.wait_ge(var_ready, 1)
            nc.scalar.activation(var[:, :], var[:, :], ACT.Sqrt).then_inc(rooted, 1)

        @block.vector
        def _(dve):
            st = Steps(dve, step)
            dve.wait_ge(landed, 16 * 2 * TILES)
            st(nc.vector.tensor_tensor(total[:, :, :], total[:, :, :],
                                       env.some0[:, :].unsqueeze(2).to_broadcast([P, TILES, ROW0]), ALU.mult))
            st.wait()
            st(nc.vector.tensor_tensor(env.x_sb[:, :, :], env.x_sb[:, :, :], total[:, :, :], ALU.add))
            st.wait()

            def root():
                dve.sem_inc(var_ready, 1)
                dve.wait_ge(rooted, 1)
            layer_norm(nc, st, env.x_sb[:, :, :].rearrange("p t (o b) -> p (t o) b", b=FEAT),
                       total[:, :, :].rearrange("p t (o b) -> p (t o) b", b=FEAT),
                       mean[:, :], var[:, :], slots, root)


def stage_sum1(nc, env, name, table, sums):
    with ExitStack() as ctx:
        s = Scope(nc, ctx, name)
        rows = s.sb("rows", [P, 2, WIN, FEAT])
        idx = s.sb("idx", [P, 2, WIN], I32)
        so_far = s.sb("so_far", [P, FEAT])
        idx_ready, claimed, summed, step, start = map(s.sem, ("idx_ready", "claimed", "summed", "step", "start"))
        landed = [s.sem(f"landed{b}") for b in range(2)]
        stored = [s.sem(f"stored{b}") for b in range(2)]
        block = s.block()
        out = sums.rearrange("(p c) f -> p c f", p=P)

        @block.gpsimd
        def _(pool):
            with pool.Fori(0, WINS // 2) as i:
                for b in range(2):
                    pool.wait_ge(idx_ready, i * 2 + b + 1)
                    pool.sem_inc(claimed, 1)
                    for c in range(WIN):
                        pool.indirect_dma_start(
                            out=rows[:, b, c, :], out_offset=None, in_=table,
                            in_offset=bass.IndirectOffsetOnAxis(ap=idx[:, b, c:c + 1], axis=0)
                        ).then_inc(landed[b], 16)

        @block.sync
        def _(sp):
            with sp.Fori(0, WINS // 2) as i:
                for b in range(2):
                    sp.wait_ge(summed, i * 2 + b + 1)
                    sp.dma_start(out[:, bass.ds((i * 2 + b) * WIN, WIN), :], rows[:, b, :, :]).then_inc(stored[b], 16)
            for b in range(2):
                sp.wait_ge(stored[b], 16 * (WINS // 2))

        @block.vector
        def _(dve):
            nc.vector.memset(so_far[:, :], 0.0).then_inc(start, 1)
            for b in range(2):
                nc.vector.tensor_copy(idx[:, b, :], env.idx1[:, b * WIN:(b + 1) * WIN]).then_inc(idx_ready, 1)
            dve.wait_ge(start, 1)
            per = 3

            def window(b, i, more):
                w = i * 2 + b
                st = Steps(dve, step, w * per)
                dve.wait_ge(landed[b], (i + 1) * (16 * WIN))
                scale = env.norm[:, bass.ds(w * WIN, WIN)].unsqueeze(2).to_broadcast([P, WIN, FEAT])
                st(nc.vector.tensor_tensor(rows[:, b, :, :], rows[:, b, :, :], scale, ALU.mult))
                st.wait()
                for f in range(FEAT):
                    one = nc.vector.tensor_tensor_scan(rows[:, b, :, f], env.keep[:, bass.ds(w * WIN, WIN)],
                                                       rows[:, b, :, f], so_far[:, f:f + 1], ALU.mult, ALU.add)
                st(one)
                st.wait()
                dve.sem_inc(summed, 1)
                st(nc.vector.tensor_copy(so_far[:, :], rows[:, b, WIN - 1, :]))
                st.wait()
                if more:
                    dve.wait_ge(stored[b], (i + 1) * 16)
                    nc.vector.tensor_copy(idx[:, b, :], env.idx1[:, bass.ds((w + 2) * WIN, WIN)]
                                          ).then_inc(idx_ready, 1)
                assert st.n == per
            with dve.Fori(0, WINS // 2 - 1) as i:
                for b in range(2):
                    window(b, i, True)
            for b in range(2):
                window(b, WINS // 2 - 1, False)


def stage_nodes1(nc, env, name, sums, root, last_stage):
    slots = TILES * CH
    with ExitStack() as ctx:
        s = Scope(nc, ctx, name)
        ends = s.sb("ends", [P, 2, FEAT])
        carry_in = s.sb("carry_in", [FEAT, P])
        carry_row = s.sb("carry_row", [FEAT, P])
        idx = s.sb("idx", [P, 2, NWIN], I32)
        got = s.sb("got", [P, 2, NWIN, FEAT])
        big = s.sb("big", [P, slots, FEAT] if last_stage else [P, 1, FEAT])
        stat1 = s.sb("stat1", [P, slots])
        stat2 = s.sb("stat2", [P, slots])
        last_ps = s.ps("last_ps", [FEAT, P])
        carry_ps = s.ps("carry_ps", [P, FEAT])
        ends_in, fix_in, turned, carry_ready, carry_back, fixed, patched = map(
            s.sem, ("ends_in", "fix_in", "turned", "carry_ready", "carry_back", "fixed", "patched"))
        idx_ready, claimed, added, step, step2, step3, asked, answered, stored = map(
            s.sem, ("idx_ready", "claimed", "added", "step", "step2", "step3", "asked", "answered", "stored"))
        landed = [s.sem(f"landed{b}") for b in range(2)]
        block = s.block()
        out3 = root[:, :, :].rearrange("p t (o c) -> p (t o) c", c=FEAT)

        @block.sync
        def _(sp):
            sp.dma_start(ends[:, 1, :], sums.rearrange("(p c) f -> p c f", p=P)[:, COLS - 1, :]).then_inc(ends_in, 16)
            if last_stage:
                sp.wait_ge(asked, 4)
                sp.dma_start(env.out[0:(TILES - 1) * P * CH, :].rearrange("(t n o) b -> n t (o b)", n=P, o=CH),
                             root[:, 0:TILES - 1, :]).then_inc(stored, 16)
                sp.dma_start(env.out[(TILES - 1) * P * CH:NODES1, :].rearrange("(n o) b -> n (o b)", o=CH),
                             root[0:TAIL, TILES - 1, :]).then_inc(stored, 16)
                sp.wait_ge(stored, 32)

        @block.gpsimd
        def _(pool):
            pool.indirect_dma_start(out=ends[:, 0, :], out_offset=None, in_=sums,
                                    in_offset=bass.IndirectOffsetOnAxis(ap=env.fix_idx[:, 0:1], axis=0)
                                    ).then_inc(fix_in, 16)
            pool.wait_ge(fixed, 1)
            pool.indirect_dma_start(out=sums, out_offset=bass.IndirectOffsetOnAxis(ap=env.fix_idx[:, 0:1], axis=0),
                                    in_=ends[:, 0, :], in_offset=None).then_inc(patched, 16)
            pool.wait_ge(patched, 16)

            def window(b, ready):
                pool.wait_ge(idx_ready, ready)
                pool.sem_inc(claimed, 1)
                for j in range(NWIN):
                    pool.indirect_dma_start(
                        out=got[:, b, j, :], out_offset=None, in_=sums,
                        in_offset=bass.IndirectOffsetOnAxis(ap=idx[:, b, j:j + 1], axis=0)
                    ).then_inc(landed[b], 16)
            window(0, 1)
            with pool.Fori(0, NWINS // 2) as i:
                window(1, i * 2 + 2)
                window(0, i * 2 + 3)

        @block.tensor
        def _(pe):
            pe.wait_ge(ends_in, 16)
            nc.tensor.transpose(last_ps[:, :], ends[:, 1, :], env.ident[:, :]).then_inc(turned, 1)
            pe.wait_ge(carry_ready, 1)
            nc.tensor.transpose(carry_ps[:, :], carry_row[:, :], env.ident[0:FEAT, 0:FEAT]).then_inc(carry_back, 1)

        @block.scalar
        def _(act):
            if last_stage:
                act.wait_ge(asked, 1)
                nc.scalar.activation(big[:, :, :], out3, ACT.Exp).then_inc(answered, 1)
                act.wait_ge(asked, 2)
                nc.scalar.activation(stat1[:, :], stat1[:, :], ACT.Ln).then_inc(answered, 1)
                act.wait_ge(asked, 3)
                nc.scalar.activation(stat2[:, :], stat2[:, :], ACT.Sqrt).then_inc(answered, 1)

        @block.vector
        def _(dve):
            st = Steps(dve, step)
            st(nc.vector.memset(carry_in[:, 0:1], 0.0))
            for b in range(2):
                nc.vector.tensor_copy(idx[:, b, :], env.end_idx[:, b * NWIN:(b + 1) * NWIN]).then_inc(idx_ready, 1)
            dve.wait_ge(turned, 1)
            st(nc.vector.tensor_tensor(carry_in[:, 1:P], env.cont_row[0:FEAT, 1:P], last_ps[:, 0:P - 1], ALU.mult))
            st.wait()
            nc.vector.tensor_tensor_scan(carry_row[:, :], env.pass_row[0:FEAT, :], carry_in[:, :], 0.0,
                                         ALU.mult, ALU.add).then_inc(carry_ready, 1)
            dve.wait_ge(carry_back, 1)
            dve.wait_ge(fix_in, 16)
            nc.vector.tensor_tensor(ends[:, 0, :], ends[:, 0, :], carry_ps[:, :], ALU.add).then_inc(fixed, 1)
            per = 3

            def window(b, w, arrived, more):
                dve.wait_ge(landed[b], arrived)
                st2 = Steps(dve, step2, w * per)
                some = env.has_edge[:, bass.ds(w * NWIN, NWIN)].unsqueeze(2).to_broadcast([P, NWIN, FEAT])
                st2(nc.vector.tensor_tensor(got[:, b, :, :], got[:, b, :, :], some, ALU.mult))
                st2.wait()
                to = root[:, bass.ds(w * TPW, TPW), :].rearrange("p t (o c) -> p (t o) c", c=FEAT)
                st2(nc.vector.tensor_tensor(to, to, got[:, b, :, :], ALU.add))
                st2.wait()
                if more:
                    nc.vector.tensor_copy(idx[:, b, :], env.end_idx[:, bass.ds((w + 2) * NWIN, NWIN)]
                                          ).then_inc(idx_ready, 1)
                if last_stage:
                    st2(nc.vector.tensor_reduce(stat1[:, bass.ds(w * NWIN, NWIN)], to, AX.X, ALU.max))
                else:
                    st2(nc.vector.tensor_scalar(to, to, 0.0, None, ALU.max))
                st2.wait()
                assert st2.n == per
            full = 16 * NWIN
            with dve.Fori(0, NWINS // 2 - 1) as i:
                for b in range(2):
                    window(b, i * 2 + b, (i + 1) * full, True)
            window(0, NWINS - 3, (NWINS // 2) * full, True)
            window(1, NWINS - 2, (NWINS // 2) * full, False)
            window(0, NWINS - 1, (NWINS // 2 + 1) * full, False)
            if last_stage:
                st3 = Steps(dve, step3)
                stat = lambda t: t.unsqueeze(2).to_broadcast([P, slots, FEAT])
                st3(nc.vector.tensor_tensor(out3, out3, stat(stat1[:, :]), ALU.subtract))
                st3.wait()
                dve.sem_inc(asked, 1)
                dve.wait_ge(answered, 1)
                st3(nc.vector.tensor_reduce(stat1[:, :], big[:, :, :], AX.X, ALU.add))
                st3.wait()
                dve.sem_inc(asked, 1)
                dve.wait_ge(answered, 2)
                st3(nc.vector.tensor_tensor(out3, out3, stat(stat1[:, :]), ALU.subtract))
                st3.wait()
                st3(nc.vector.tensor_tensor(root[:, :, :], root[:, :, :], env.x_sb[:, :, :], ALU.add))
                st3.wait()

                def take_root():
                    dve.sem_inc(asked, 1)
                    dve.wait_ge(answered, 3)
                layer_norm(nc, st3, out3, big[:, :, :], stat1[:, :], stat2[:, :], slots, take_root)
                dve.sem_inc(asked, 1)


class Env:
    pass


def gnn_layers(nc, x, src, dst, type6, type8, w0, b0, w1, root1, bias1, w2, root2, bias2, eye, out, stop=None):
    env = Env()
    env.x, env.src, env.dst, env.type6, env.type8, env.eye, env.out = x, src, dst, type6, type8, eye, out
    dram = lambda name, shape, dt=F32: nc.dram_tensor(name, shape, dt, kind="Internal").ap()
    env.idx0_d = dram("idx0_d", (P * COLS,), I32)
    env.dst_d = dram("dst_d", (LEAD + P * COLS,))
    env.end_d = dram("end_d", (TILES * P * CH,), I32)
    env.some_d = dram("some_d", (TILES * P * CH,))
    env.table0 = dram("table0", (NODES0 * TYPES0, ROW0))
    env.sums0 = [dram(f"sums0_{h}", (EDGES, HALF)) for h in range(2)]
    table1 = dram("table1", (NODES1 * RELS, FEAT))
    table2 = dram("table2", (NODES1 * RELS, FEAT))
    sums1 = dram("sums1", (P * COLS, FEAT))
    sums2 = dram("sums2", (P * COLS, FEAT))
    with ExitStack() as ctx:
        ctx.enter_context(nc.allow_non_contiguous_dma(reason="single columns of the edge list, a few of them"))
        s = Scope(nc, ctx, "all")
        env.ident = s.sb("ident", [P, P])
        env.idx1 = s.sb("idx1", [P, COLS], I32)
        env.norm = s.sb("norm", [P, COLS])
        env.keep = s.sb("keep", [P, COLS + 1], BF16)
        env.cont_row = s.sb("cont_row", [P, P])
        env.pass_row = s.sb("pass_row", [P, P])
        env.back_row = s.sb("back_row", [P, P])
        env.fix_idx = s.sb("fix_idx", [P, 1], I32)
        env.firsts = s.sb("firsts", [P, 2])
        env.rel_id = s.sb("rel_id", [P, RELS])
        env.block_first = s.sb("block_first", [1, BLOCKS], I32)
        with ExitStack() as early:
            e = Scope(nc, early, "early")
            env.in_first = e.sb("in_first", [P, COLS], BF16)
            env.in_last = e.sb("in_last", [P, COLS], BF16)
            env.rel = e.sb("rel", [P, COLS], BF16)
            stage_edges(nc, env)
            stage_norm(nc, env)
        env.end_idx = s.sb("end_idx", [P, TILES * CH], I32)
        env.has_edge = s.sb("has_edge", [P, TILES * CH])
        env.end0 = s.sb("end0", [P, TILES], I32)
        env.some0 = s.sb("some0", [P, TILES])
        stage_rank(nc, env)
        env.x_sb = s.sb("x_sb", [P, TILES, ROW0])
        stage_table(nc, env, "t0", env.x_sb, w0, b0, env.table0, TYPES0, None)
        stage_sum0(nc, env)
        stage_nodes0(nc, env)
        hidden = s.sb("hidden", [P, TILES, ROW0])
        logits = s.sb("logits", [P, TILES, ROW0])
        stage_table(nc, env, "t1", env.x_sb, (w1, root1), bias1, table1, RELS, hidden)
        stage_sum1(nc, env, "s1", table1, sums1)
        stage_nodes1(nc, env, "n1", sums1, hidden, False)
        stage_table(nc, env, "t2", hidden, (w2, root2), bias2, table2, RELS, logits)
        stage_sum1(nc, env, "s2", table2, sums2)
        stage_nodes1(nc, env, "n2", sums2, logits, True)


def kernel(**inputs):
    import numpy as _np
    import concourse.bacc as _bacc
    from concourse import mybir as _mybir
    from concourse.bass_utils import run_bass_kernel_spmd as _run

    nc = _bacc.Bacc("TRN2", target_bir_lowering=False, num_devices=1)
    names = ["x", "src", "dst", "edge_type_6", "edge_type_8", "L0_gnn_W", "L0_gnn_Bv", "L1_gnn_W1",
             "L1_gnn_root1", "L1_gnn_b1", "L1_gnn_W2", "L1_gnn_root2", "L1_gnn_b2", "eye"]
    arrays, args = {}, []
    for name in names:
        a = _np.eye(P, dtype=_np.float32) if name == "eye" else _np.asarray(inputs[name])
        if name == "L0_gnn_W":
            a = a.transpose(2, 0, 1).reshape(CH, TYPES0 * CH)
        a = _np.ascontiguousarray(a)
        arrays[f"in_{name}_dram"] = a
        args.append(nc.dram_tensor(f"in_{name}_dram", a.shape, _mybir.dt.from_np(a.dtype), kind="ExternalInput").ap())
    args.append(nc.dram_tensor("out_0_dram", (NODES1, FEAT), _mybir.dt.float32, kind="ExternalOutput").ap())
    gnn_layers(nc, *args)
    r = _run(nc, [arrays], core_ids=[0])
    return r.results[0]["out_0_dram"]
```

```python
import concourse.bass as bass
from concourse import mybir
from contextlib import ExitStack

F32 = mybir.dt.float32
BF16 = mybir.dt.bfloat16
I32 = mybir.dt.int32
ALU = mybir.AluOpType
ACT = mybir.ActivationFunctionType
AX = mybir.AxisListType

P = 128
FEAT = 16
NODES1 = 50000
EDGES = 850000
CH = 8
NODES0 = NODES1 // CH
ROW0 = CH * FEAT
TYPES0 = 5
RELS = 8
EPS = 1e-5

WIN = 64
COLS = 6656
WINS = COLS // WIN
LAST_VALID = EDGES - (P - 1) * COLS
RING = 8
LEAD = WIN

TILES = -(-NODES0 // P)
TAIL = NODES0 - (TILES - 1) * P
NWIN = 56
NWINS = TILES * CH // NWIN
TPW = NWIN // CH

BP, BC = 125, 68
BLOCK = BP * BC
BLOCKS = EDGES // BLOCK
ROUNDS = 5
PER_ROUND = BLOCKS // ROUNDS
ROUND = PER_ROUND * BLOCK
assert BLOCKS * BLOCK == EDGES and ROUNDS * PER_ROUND == BLOCKS and PER_ROUND % 2 == 0
assert WINS % RING == 0 and NWINS * NWIN == TILES * CH and NWINS == TPW == 7
assert NODES0 <= TPW * P * CH


class Steps:

    def __init__(self, eng, sem, done=0):
        self.eng, self.sem, self.n, self.done = eng, sem, 0, done

    def __call__(self, ins):
        ins.then_inc(self.sem, 1)
        self.n += 1

    def wait(self):
        self.eng.wait_ge(self.sem, self.done + self.n)


class Scope:

    def __init__(self, nc, ctx, prefix):
        self.nc, self.ctx, self.prefix = nc, ctx, prefix
        self.sems = []
        ctx.callback(self.clear)

    def clear(self):
        if self.sems:
            self.nc.clear_and_free_semaphores(self.sems)
            self.nc.all_engine_barrier()

    def sb(self, name, shape, dt=F32):
        return self.ctx.enter_context(self.nc.sbuf_tensor(f"{self.prefix}_{name}", shape, dt))

    def ps(self, name, shape):
        return self.ctx.enter_context(self.nc.psum_tensor(f"{self.prefix}_{name}", shape, F32))

    def sem(self, name):
        self.sems.append(self.nc.alloc_semaphore(name=f"{self.prefix}_{name}"))
        return self.sems[-1]

    def block(self):
        return self.ctx.enter_context(self.nc.Block())


def stage_edges(nc, env):
    with ExitStack() as ctx:
        s = Scope(nc, ctx, "ed")
        dst_f = s.sb("dst_f", [P, COLS])
        typ = s.sb("typ", [P, COLS], I32)
        typ6 = s.sb("typ6", [P, COLS], I32)
        tmp = s.sb("tmp", [P, COLS])
        before = s.sb("before", [P, 1], I32)
        after = s.sb("after", [P, 1], I32)
        flag = s.sb("flag", [P, 2])
        wide = s.sb("wide", [P, 2, P])
        lead = s.sb("lead", [1, LEAD])
        wide_ps = s.ps("wide_ps", [P, 2, P])
        padded, dst_in, type6_in, src_in, type8_in, small_in, dst_used, idx0_used = map(
            s.sem, ("padded", "dst_in", "type6_in", "src_in", "type8_in", "small_in", "dst_used", "idx0_used"))
        flags_done, stored, iotas, idx0_ready, wide_ready, turned, step = map(
            s.sem, ("flags_done", "stored", "iotas", "idx0_ready", "wide_ready", "turned", "step"))
        block = s.block()
        rows = P - 1
        split = rows * COLS

        def load(eng, to, frm, landed):
            eng.dma_start(to[0:rows, :], frm[0:split].rearrange("(p c) -> p c", p=rows)).then_inc(landed, 16)
            eng.dma_start(to[rows:P, 0:LAST_VALID],
                          frm[split:EDGES].rearrange("(p c) -> p c", p=1)).then_inc(landed, 16)

        @block.sync
        def _(sp):
            sp.wait_ge(padded, 3)
            load(sp, typ, env.dst, dst_in)
            load(sp, typ6, env.type6, type6_in)
            load(sp, env.idx1, env.src, src_in)
            sp.wait_ge(dst_used, 1)
            load(sp, typ, env.type8, type8_in)
            sp.wait_ge(idx0_ready, 1)
            sp.dma_start(env.idx0_d.rearrange("(p c) -> p c", c=COLS), typ6[:, :]).then_inc(stored, 16)
            sp.wait_ge(stored, 48)

        @block.scalar
        def _(act):
            act.wait_ge(padded, 3)
            act.dma_start(before[1:P, :], env.dst[0:rows * COLS].rearrange("(p c) -> p c", c=COLS)
                          [:, COLS - 1:COLS]).then_inc(small_in, 16)
            act.dma_start(after[0:rows - 1, :], env.dst[COLS:split].rearrange("(p c) -> p c", c=COLS)
                          [:, 0:1]).then_inc(small_in, 16)
            act.dma_start(after[rows - 1:rows, :], env.dst[split:split + 1].rearrange("(p c) -> p c", c=1)
                          ).then_inc(small_in, 16)
            act.dma_start(env.ident[:, :], env.eye).then_inc(small_in, 16)
            act.dma_start(env.block_first[0:1, 1:BLOCKS], env.dst[BLOCK:EDGES].rearrange("(k e) -> e k", e=BLOCK)
                          [0:1, :]).then_inc(small_in, 16)
            act.wait_ge(flags_done, 1)
            act.dma_start(env.dst_d[LEAD:LEAD + P * COLS].rearrange("(p c) -> p c", c=COLS),
                          dst_f[:, :]).then_inc(stored, 16)
            act.dma_start(env.dst_d[0:LEAD].rearrange("(a b) -> a b", a=1), lead[:, :]).then_inc(stored, 16)
            act.wait_ge(small_in, 80)

        @block.gpsimd
        def _(pool):
            nc.gpsimd.iota(env.fix_base[:, :], pattern=[[0, 1]], base=-1, channel_multiplier=COLS).then_inc(iotas, 1)
            nc.gpsimd.iota(env.rel_id[:, :], pattern=[[1, RELS]], base=0, channel_multiplier=0,
                           allow_small_or_imprecise_dtypes=True).then_inc(iotas, 1)
            nc.gpsimd.iota(env.round_at[:, :], pattern=[[ROUND // 100, ROUNDS + 1]], base=0, channel_multiplier=0,
                           allow_small_or_imprecise_dtypes=True).then_inc(iotas, 1)
            pool.wait_ge(iotas, 3)

        @block.tensor
        def _(pe):
            pe.wait_ge(small_in, 80)
            pe.wait_ge(wide_ready, 2)
            for j in range(2):
                nc.tensor.transpose(wide_ps[:, j, :], wide[:, j, :], env.ident[:, :]).then_inc(turned, 1)

        @block.vector
        def _(dve):
            st = Steps(dve, step)
            nc.vector.memset(before[:, :], -1)
            nc.vector.memset(after[:, :], NODES1)
            nc.vector.memset(env.block_first[:, 0:1], 0)
            nc.vector.memset(typ[:, LAST_VALID:], NODES1).then_inc(padded, 1)
            nc.vector.memset(typ6[:, LAST_VALID:], 0).then_inc(padded, 1)
            nc.vector.memset(env.idx1[:, LAST_VALID:], 0).then_inc(padded, 1)
            nc.vector.memset(lead[:, :], -1.0)
            dve.wait_ge(dst_in, 32)
            st(nc.vector.tensor_copy(dst_f[:, :], typ[:, :]))
            st.wait()
            nc.vector.memset(typ[:, LAST_VALID:], 0).then_inc(dst_used, 1)
            dve.sem_inc(flags_done, 1)
            st(nc.vector.tensor_tensor(env.keep[:, 1:COLS], dst_f[:, 1:COLS], dst_f[:, 0:COLS - 1], ALU.is_equal))
            st(nc.vector.memset(env.keep[:, 0:1], 1.0))
            dve.wait_ge(small_in, 80)
            st(nc.vector.tensor_tensor(env.keep[:, COLS:COLS + 1], dst_f[:, COLS - 1:COLS], after[:, :], ALU.is_equal))
            st(nc.vector.tensor_tensor(flag[:, 0:1], dst_f[:, 0:1], before[:, :], ALU.is_equal))
            st(nc.vector.tensor_tensor(flag[:, 1:2], dst_f[:, 0:1], dst_f[:, COLS - 1:COLS], ALU.is_equal))
            st(nc.vector.tensor_copy(env.first_dst[:, :], dst_f[:, 0:1]))
            st.wait()
            st(nc.vector.memset(env.first_dst[0:1, :], -1.0))
            for j in range(2):
                nc.vector.tensor_copy(wide[:, j, :], flag[:, j:j + 1].to_broadcast([P, P])).then_inc(wide_ready, 1)
            dve.wait_ge(type6_in, 32)
            st(nc.vector.tensor_scalar(tmp[:, :], typ6[:, :], 0.0, float(TYPES0), ALU.is_equal, ALU.mult))
            st.wait()
            st(nc.vector.scalar_tensor_tensor(tmp[:, :], typ6[:, :], -1.0, tmp[:, :], ALU.add, ALU.add))
            dve.wait_ge(src_in, 32)
            st.wait()
            st(nc.vector.tensor_scalar(typ6[:, :], env.idx1[:, :], float(NODES0 - 1), float(TYPES0), ALU.min, ALU.mult))
            st.wait()
            nc.vector.tensor_tensor(typ6[:, :], typ6[:, :], tmp[:, :], ALU.add).then_inc(idx0_ready, 1)
            dve.wait_ge(turned, 2)
            st(nc.vector.tensor_copy(env.cont_row[:, :], wide_ps[:, 0, :]))
            st(nc.vector.memset(env.pass_row[:, :], 0.0))
            st(nc.vector.memset(env.back_row[:, :], 0.0))
            st.wait()
            st(nc.vector.tensor_tensor(env.pass_row[:, 1:P], env.cont_row[:, 1:P], wide_ps[:, 1, 0:P - 1], ALU.mult))
            st(nc.vector.tensor_tensor(env.back_row[:, 0:P - 1], env.cont_row[:, 1:P], wide_ps[:, 1, 1:P], ALU.mult))
            dve.wait_ge(type8_in, 32)
            st(nc.vector.scalar_tensor_tensor(env.idx1[:, :], env.idx1[:, :], float(RELS), typ[:, :],
                                              ALU.mult, ALU.add))
            st.wait()
            dve.wait_ge(iotas, 3)
            st(nc.vector.tensor_scalar(env.round_at[:, :], env.round_at[:, :], 100.0, None, ALU.mult))
            st.wait()


class Table:

    def __init__(self, nc, env, s, values, weights, table, root_out):
        self.nc, self.env, self.values, self.root_out = nc, env, values, root_out
        s = Scope(nc, s.ctx, s.prefix + "t")
        self.w, self.root, self.width = weights[0], weights[1], CH * RELS * FEAT
        self.mix = s.sb("mix", [P, self.width + ROW0])
        self.rep = s.sb("rep", [P, (RELS + 1) * FEAT])
        self.slot = s.sb("slot", [P, CH])
        self.xt = s.sb("xt", [P, 2, P])
        self.x_turned = s.sb("x_turned", [P, 2, P])
        self.out = s.sb("out", [P, 2, self.width + ROW0])
        self.turn_ps = [s.ps(f"turn_ps{b}", [P, 512]) for b in range(2)]
        self.mul_ps = [s.ps(f"mul_ps{b}", [P, 3, 512]) for b in range(2)]
        self.flat = table.rearrange("(n r) f -> n (r f)", n=NODES0)
        (self.weights_in, self.mix_ready, self.group_ready, self.staged, self.turned, self.back, self.multiplied,
         self.read_out, self.mix_step) = map(s.sem, (
             "weights_in", "mix_ready", "group_ready", "staged", "turned", "back", "multiplied", "read_out",
             "mix_step"))
        self.stored = [s.sem(f"stored{b}") for b in range(2)]

    def load_weights(self, eng):
        for i in range(CH):
            eng.dma_start(self.rep[i * FEAT:(i + 1) * FEAT, 0:RELS * FEAT].rearrange("b (r c) -> b r c", c=FEAT),
                          self.w.rearrange("r b c -> b r c")).then_inc(self.weights_in, 16)
            eng.dma_start(self.rep[i * FEAT:(i + 1) * FEAT, RELS * FEAT:], self.root).then_inc(self.weights_in, 16)

    def make_mix(self, dve):
        nc, st = self.nc, Steps(dve, self.mix_step)
        st(nc.vector.tensor_reduce(self.slot[:, :], self.env.ident[:, :].rearrange("p (o b) -> p o b", b=FEAT),
                                   AX.X, ALU.add))
        dve.wait_ge(self.weights_in, 16 * 2 * CH)
        st.wait()
        for o in range(CH):
            st(nc.vector.tensor_scalar(self.mix[:, o * P:(o + 1) * P], self.rep[:, 0:P],
                                       self.slot[:, o:o + 1], None, ALU.mult))
            at = self.width + o * FEAT
            st(nc.vector.tensor_scalar(self.mix[:, at:at + FEAT], self.rep[:, P:P + FEAT],
                                       self.slot[:, o:o + 1], None, ALU.mult))
        st.wait()
        dve.sem_inc(self.mix_ready, 1)

    @staticmethod
    def previous(g, j):
        n = g * TPW + j + 1
        back = {0: 1, 1: 3}.get(j, 2)
        return None if isinstance(g, int) and n - back <= 0 else n - back

    @staticmethod
    def uses(g, j):
        return g * (TPW // 2 + 1 - j % 2) + j // 2

    def each_group(self, eng, body):
        body(0)
        with eng.Fori(1, TPW - 1) as g:
            body(g)
        body(TPW - 1)

    def pe(self, pe):
        nc = self.nc
        pe.wait_ge(self.mix_ready, 1)

        def turn(g, j):
            pe.wait_ge(self.staged, g * TPW + j + 1)
            nc.tensor.transpose(self.turn_ps[j % 2][:, 0:P], self.xt[:, j % 2, :],
                                self.env.ident[:, :]).then_inc(self.turned, 1)

        def group(g):
            turn(g, 0)
            for j in range(TPW):
                if j + 1 < TPW:
                    turn(g, j + 1)
                before = self.previous(g, j)
                if before is not None:
                    pe.wait_ge(self.read_out, before)
                pe.wait_ge(self.back, g * TPW + j + 1)
                for k, (a, z) in enumerate(((0, 512), (512, 1024), (1024, 1152))):
                    last = nc.tensor.matmul(self.mul_ps[j % 2][:, k, 0:z - a], self.x_turned[:, j % 2, :],
                                            self.mix[:, a:z], start=True, stop=True)
                last.then_inc(self.multiplied, 1)
        self.each_group(pe, group)

    def act(self, act):
        nc = self.nc

        def stage(g, j):
            nc.scalar.copy(self.xt[:, j % 2, :], self.values[:, self.tile(g, j), :]).then_inc(self.staged, 1)

        def turn_back(g, j):
            act.wait_ge(self.turned, g * TPW + j + 1)
            before = self.previous(g, j)
            if before is not None:
                act.wait_ge(self.multiplied, before)
            nc.scalar.copy(self.x_turned[:, j % 2, :], self.turn_ps[j % 2][:, 0:P]).then_inc(self.back, 1)

        def group(g):
            act.wait_ge(self.group_ready, g + 1)
            stage(g, 0)
            stage(g, 1)
            turn_back(g, 0)
            for j in range(TPW):
                if j + 1 < TPW:
                    turn_back(g, j + 1)
                if j + 2 < TPW:
                    stage(g, j + 2)
                act.wait_ge(self.multiplied, g * TPW + j + 1)
                if not (isinstance(g, int) and self.uses(g, j) == 0):
                    act.wait_ge(self.stored[j % 2], self.uses(g, j) * 32)
                nc.scalar.copy(self.out[:, j % 2, 0:512], self.mul_ps[j % 2][:, 0, :])
                nc.scalar.copy(self.out[:, j % 2, 512:1024], self.mul_ps[j % 2][:, 1, :])
                nc.scalar.copy(self.out[:, j % 2, 1024:], self.mul_ps[j % 2][:, 2, 0:ROW0]).then_inc(self.read_out, 1)
        self.each_group(act, group)

    @staticmethod
    def tile(g, j):
        return g * TPW + j if isinstance(g, int) else bass.ds(g * TPW + j, 1)

    def sp(self, sp):
        def group(g):
            for j in range(TPW):
                t = g * TPW + j
                end = isinstance(g, int) and t == TILES - 1
                rows = TAIL if end else P
                at = slice(t * P, t * P + rows) if isinstance(g, int) else bass.ds(t * P, P)
                sp.wait_ge(self.read_out, t + 1)
                sp.dma_start(self.flat[at, :], self.out[0:rows, j % 2, 0:self.width]).then_inc(self.stored[j % 2], 16)
                sp.dma_start(self.root_out[at if not end else slice(t * P, t * P + P), :],
                             self.out[:, j % 2, self.width:]).then_inc(self.stored[j % 2], 16)
        self.each_group(sp, group)
        for b in range(2):
            sp.wait_ge(self.stored[b], 32 * self.uses(TPW, b))


def stage_first(nc, env):
    slots = TILES * CH
    width = TYPES0 * ROW0
    with ExitStack() as ctx:
        s = Scope(nc, ctx, "fi")
        x_sb = s.sb("x_sb", [P, TILES, ROW0])
        mix = s.sb("mix", [P, width])
        rep = s.sb("rep", [P, TYPES0 * CH])
        lane = s.sb("lane", [P, FEAT])
        bias_in = s.sb("bias_in", [P, TYPES0 * CH])
        bias_w = s.sb("bias_w", [P, width])
        xt = s.sb("xt", [P, P])
        x_turned = s.sb("x_turned", [P, P])
        out = s.sb("out", [P, 2, width])
        node_i = s.sb("node_i", [P, slots], I32)
        tile_base = s.sb("tile_base", [P, TILES])
        in_tile = s.sb("in_tile", [P, CH, P])
        first_t = s.sb("first_t", [P, TILES])
        samples = s.sb("samples", [P, WINS])
        shifted = s.sb("shifted", [P, WINS])
        pick = s.sb("pick", [P, WINS + 1])
        reached = s.sb("reached", [P, 2, CH, P])
        below = s.sb("below", [P, CH, WINS])
        win_no = s.sb("win_no", [P, slots])
        turn_ps = s.ps("turn_ps", [P, 512])
        mul_ps = s.ps("mul_ps", [P, 2, 512])
        picked = [s.ps(f"picked{b}", [P, 2, 4, P]) for b in range(2)]
        loaded, samples_in, zeroed, mix_ready, staged, turned, back, multiplied, read_out = map(
            s.sem, ("loaded", "samples_in", "zeroed", "mix_ready", "staged", "turned", "back", "multiplied",
                    "read_out"))
        iotas, prep, pick_ready, reached_ready, picked_done, picked_used, step, tile_step, step3 = map(
            s.sem, ("iotas", "prep", "pick_ready", "reached_ready", "picked_done", "picked_used", "step",
                    "tile_step", "step3"))
        stored = [s.sem(f"stored{b}") for b in range(2)]
        block = s.block()
        flat = env.table0.rearrange("(n r) f -> n (r f)", n=NODES0)
        pairs = TILES // 2

        @block.sync
        def _(sp):
            src = env.dst_rows[1:1 + P * WINS, 0:1].rearrange("(p j) c -> p (j c)", j=WINS)
            sp.wait_ge(zeroed, 2)
            sp.dma_start(samples[:, :], src).then_inc(samples_in, 16)
            sp.dma_start(shifted[1:P, :], src[0:P - 1, :]).then_inc(samples_in, 16)
            load_x(sp, env, x_sb, loaded)

            def store(b, done, rows, at):
                sp.wait_ge(read_out, done)
                sp.dma_start(flat[at, :], out[0:rows, b, :]).then_inc(stored[b], 16)

            with sp.Fori(0, pairs) as i:
                for b in range(2):
                    store(b, i * 2 + b + 1, P, bass.ds((i * 2 + b) * P, P))
            store(0, TILES, TAIL, slice((TILES - 1) * P, NODES0))
            sp.wait_ge(stored[0], 16 * (pairs + 1))
            sp.wait_ge(stored[1], 16 * pairs)

        @block.gpsimd
        def _(pool):
            nc.gpsimd.iota(node_i[:, :], pattern=[[P * CH, TILES], [1, CH]], base=0,
                           channel_multiplier=CH).then_inc(iotas, 1)
            nc.gpsimd.iota(tile_base[:, :], pattern=[[P * CH, TILES]], base=0, channel_multiplier=0,
                           allow_small_or_imprecise_dtypes=True).then_inc(iotas, 1)
            nc.gpsimd.iota(in_tile[:, :, :], pattern=[[1, CH], [CH, P]], base=0, channel_multiplier=0,
                           allow_small_or_imprecise_dtypes=True).then_inc(iotas, 1)

        @block.scalar
        def _(act):
            for i in range(CH):
                act.dma_start(rep[i * FEAT:(i + 1) * FEAT, :],
                              env.w0[i:i + 1, :].to_broadcast([FEAT, TYPES0 * CH])).then_inc(loaded, 16)
            act.dma_start(bias_in[:, :], env.b0.rearrange("(a t) o -> a (t o)", a=1)
                          .to_broadcast([P, TYPES0 * CH])).then_inc(loaded, 16)
            act.wait_ge(loaded, 16 * (CH + 1 + 2))

            def tile(t, n):
                if not isinstance(t, int):
                    act.wait_ge(turned, n - 1)
                nc.scalar.copy(xt[:, :], x_sb[:, t if isinstance(t, int) else bass.ds(t, 1), :]).then_inc(staged, 1)
                act.wait_ge(turned, n)
                if not isinstance(t, int):
                    act.wait_ge(multiplied, n - 1)
                nc.scalar.copy(x_turned[:, :], turn_ps[:, 0:P]).then_inc(back, 1)

            tile(0, 1)
            with act.Fori(1, TILES) as t:
                tile(t, t + 1)

        @block.tensor
        def _(pe):
            def turn(n):
                pe.wait_ge(staged, n)
                nc.tensor.transpose(turn_ps[:, 0:P], xt[:, :], env.ident[:, :]).then_inc(turned, 1)

            def pick_samples(b, n, free):
                pe.wait_ge(reached_ready, n)
                if free is not None:
                    pe.wait_ge(picked_used, free)
                for o in range(CH):
                    last = nc.tensor.matmul(picked[b][:, o // 4, o % 4, 0:WINS + 1], reached[:, b, o, :],
                                            pick[:, :], start=True, stop=True)
                last.then_inc(picked_done, 1)

            def multiply(n, read):
                pe.wait_ge(back, n)
                if read is not None:
                    pe.wait_ge(read_out, read)
                for j, (a, z) in enumerate(((0, 512), (512, width))):
                    last = nc.tensor.matmul(mul_ps[:, j, 0:z - a], x_turned[:, :], mix[:, a:z], start=True, stop=True)
                last.then_inc(multiplied, 1)

            pe.wait_ge(pick_ready, 1)
            turn(1)
            pick_samples(0, 1, None)
            pe.wait_ge(mix_ready, 1)
            multiply(1, None)
            turn(2)
            pick_samples(1, 2, None)
            multiply(2, 1)
            with pe.Fori(1, pairs) as i:
                for b in range(2):
                    turn(i * 2 + b + 1)
                    pick_samples(b, i * 2 + b + 1, i * 2 + b - 1)
                    multiply(i * 2 + b + 1, i * 2 + b)
            turn(TILES)
            pick_samples(0, TILES, TILES - 2)
            multiply(TILES, TILES - 1)

        @block.vector
        def _(dve):
            st = Steps(dve, step)
            nc.vector.memset(x_sb[:, TILES - 1, :], 0.0).then_inc(zeroed, 1)
            nc.vector.memset(shifted[0:1, :], 0.0).then_inc(zeroed, 1)
            st(nc.vector.tensor_reduce(lane[:, :], env.ident[:, :].rearrange("p (o b) -> p b o", b=FEAT), AX.X, ALU.add))
            dve.wait_ge(iotas, 3)
            st(nc.vector.tensor_copy(env.node[:, :], node_i[:, :]))
            st(nc.vector.tensor_scalar(first_t[:, :], tile_base[:, :], -1.0, env.first_dst[:, :], ALU.mult, ALU.add))
            dve.wait_ge(samples_in, 32)
            st(nc.vector.tensor_tensor(pick[:, 0:WINS], samples[:, :], shifted[:, :], ALU.subtract))
            st(nc.vector.memset(pick[:, WINS:WINS + 1], 1.0))
            st.wait()
            dve.sem_inc(pick_ready, 1)

            def reach(b, t):
                nc.vector.tensor_scalar(reached[:, b, :, :], in_tile[:, :, :], first_t[:, bass.ds(t, 1)], None,
                                        ALU.is_ge).then_inc(reached_ready, 1)

            reach(0, 0)
            reach(1, 1)
            dve.wait_ge(loaded, 16 * (CH + 1 + 2))
            st(nc.vector.tensor_tensor(mix[:, :].rearrange("p (k b) -> p k b", b=FEAT),
                                       rep[:, :].unsqueeze(2).to_broadcast([P, TYPES0 * CH, FEAT]),
                                       lane[:, :].unsqueeze(1).to_broadcast([P, TYPES0 * CH, FEAT]), ALU.mult))
            st(nc.vector.tensor_copy(bias_w[:, :].rearrange("p (k b) -> p k b", b=FEAT),
                                     bias_in[:, :].unsqueeze(2).to_broadcast([P, TYPES0 * CH, FEAT])))
            st.wait()
            dve.sem_inc(mix_ready, 1)
            per = 3

            def count(b, t):
                dve.wait_ge(picked_done, t + 1)
                st2 = Steps(dve, tile_step, t * per)
                at = bass.ds(t * CH, CH)
                st2(nc.vector.tensor_tensor(
                    below[:, :, :].rearrange("n (a c) j -> n a c j", a=2), picked[b][:, :, :, 0:WINS],
                    env.node[:, at].rearrange("n (a c) -> n a c", a=2).unsqueeze(3).to_broadcast([P, 2, 4, WINS]),
                    ALU.is_le))
                st2(nc.vector.tensor_copy(env.win_row[:, at].rearrange("n (a c) -> n a c", a=2),
                                          picked[b][:, :, :, WINS]))
                st2.wait()
                dve.sem_inc(picked_used, 1)
                st2(nc.vector.tensor_reduce(win_no[:, at], below[:, :, :], AX.X, ALU.add))
                st2.wait()
                assert st2.n == per

            def messages(b, n, left):
                dve.wait_ge(multiplied, n)
                if left is not None:
                    dve.wait_ge(stored[b], left)
                nc.vector.tensor_tensor(out[:, b, 0:512], mul_ps[:, 0, :], bias_w[:, 0:512], ALU.add)
                nc.vector.tensor_tensor(out[:, b, 512:width], mul_ps[:, 1, 0:width - 512], bias_w[:, 512:width],
                                        ALU.add).then_inc(read_out, 1)

            for b in range(2):
                count(b, b)
                reach(b, b + 2)
                messages(b, b + 1, None)
            with dve.Fori(1, pairs - 1) as i:
                for b in range(2):
                    count(b, i * 2 + b)
                    reach(b, i * 2 + b + 2)
                    messages(b, i * 2 + b + 1, i * 16)
            count(0, TILES - 3)
            reach(0, TILES - 1)
            messages(0, TILES - 2, (pairs - 1) * 16)
            count(1, TILES - 2)
            messages(1, TILES - 1, (pairs - 1) * 16)
            count(0, TILES - 1)
            messages(0, TILES, pairs * 16)

            st3 = Steps(dve, step3)
            st3(nc.vector.tensor_scalar(win_no[:, :], win_no[:, :], -1.0, 0.0, ALU.add, ALU.max))
            st3(nc.vector.tensor_scalar(env.win_row[:, :], env.win_row[:, :], -1.0, float(WINS), ALU.add, ALU.mult))
            st3.wait()
            st3(nc.vector.tensor_tensor(env.win_row[:, :], env.win_row[:, :], win_no[:, :], ALU.add))
            st3.wait()
            st3(nc.vector.tensor_scalar(env.win_idx[:, :], env.win_row[:, :], float(LEAD // WIN), None, ALU.add))
            st3.wait()


def load_x(eng, env, x_sb, landed):
    eng.dma_start(x_sb[:, 0:TILES - 1, :], env.x[0:(TILES - 1) * P * CH, :]
                  .rearrange("(t n o) b -> n t (o b)", n=P, o=CH)).then_inc(landed, 16)
    eng.dma_start(x_sb[0:TAIL, TILES - 1, :], env.x[(TILES - 1) * P * CH:NODES1, :]
                  .rearrange("(n o) b -> n (o b)", o=CH)).then_inc(landed, 16)


def find_last_edges(nc, dve, env, got, cmp, n_le, n_eq, step, done, at):
    st = Steps(dve, step, done)
    want = env.node[:, at].unsqueeze(2).to_broadcast([P, NWIN, WIN])
    for op, to in ((ALU.is_le, n_le), (ALU.is_equal, n_eq)):
        st(nc.vector.tensor_tensor(cmp[:, :, :], got, want, op))
        st.wait()
        st(nc.vector.tensor_reduce(to[:, :], cmp[:, :, :], AX.X, ALU.add))
        st.wait()
    st(nc.vector.tensor_scalar(env.has_edge[:, at], n_eq[:, :], 1.0, None, ALU.min))
    st(nc.vector.scalar_tensor_tensor(n_le[:, :], env.win_row[:, at], float(WIN), n_le[:, :], ALU.mult, ALU.add))
    st.wait()
    st(nc.vector.scalar_tensor_tensor(env.end_idx[:, at], n_le[:, :], -1.0, env.has_edge[:, at], ALU.add, ALU.mult))
    st.wait()
    assert st.n == FIND_STEPS


FIND_STEPS = 7


def fetch(nc, pool, out, table, idx, count, landed):
    for j in range(count):
        pool.indirect_dma_start(out=out[:, j, :], out_offset=None, in_=table,
                                in_offset=bass.IndirectOffsetOnAxis(ap=idx[:, j:j + 1], axis=0)).then_inc(landed, 16)


def stage_ends0(nc, env):
    with ExitStack() as ctx:
        s = Scope(nc, ctx, "e0")
        idx = s.sb("idx", [P, NWIN], I32)
        got = s.sb("got", [P, NWIN, WIN])
        cmp = s.sb("cmp", [P, NWIN, WIN])
        n_le = s.sb("n_le", [P, NWIN])
        n_eq = s.sb("n_eq", [P, NWIN])
        idx_ready, landed, step, found, out, back = map(
            s.sem, ("idx_ready", "landed", "step", "found", "out", "back"))
        block = s.block()

        @block.gpsimd
        def _(pool):
            pool.wait_ge(idx_ready, 3)
            fetch(nc, pool, got, env.dst_rows, idx, NWIN, landed)

        @block.sync
        def _(sp):
            sp.wait_ge(found, 1)
            for to, frm in ((env.end_d, env.end_idx), (env.some_d, env.has_edge)):
                sp.dma_start(to.rearrange("(t n o) -> n t o", n=P, o=CH),
                             frm[:, 0:NWIN].rearrange("n (t o) -> n t o", o=CH)).then_inc(out, 16)
            sp.wait_ge(out, 32)
            for to, frm in ((env.end0, env.end_d), (env.some0, env.some_d)):
                sp.dma_start(to[:, 0:TILES - 1], frm[0:(TILES - 1) * P].rearrange("(t n) -> n t", n=P)).then_inc(back, 16)
                sp.dma_start(to[0:TAIL, TILES - 1:TILES],
                             frm[(TILES - 1) * P:NODES0].rearrange("(n t) -> n t", t=1)).then_inc(back, 16)
            sp.wait_ge(back, 64)

        @block.vector
        def _(dve):
            nc.vector.tensor_copy(idx[:, :], env.win_idx[:, 0:NWIN]).then_inc(idx_ready, 1)
            nc.vector.memset(env.end0[:, :], 0).then_inc(idx_ready, 1)
            nc.vector.memset(env.some0[:, :], 0.0).then_inc(idx_ready, 1)
            dve.wait_ge(landed, 16 * NWIN)
            find_last_edges(nc, dve, env, got[:, :, :], cmp, n_le, n_eq, step, 0, slice(0, NWIN))
            dve.sem_inc(found, 1)


def stage_sum0(nc, env):
    with ExitStack() as ctx:
        s = Scope(nc, ctx, "s0")
        rows = s.sb("rows", [BP, 2, BC, ROW0])
        idx = s.sb("idx", [BP, 2, BC], I32)
        dst = s.sb("dst", [BP, 2, BC + 1])
        keep = s.sb("keep", [BP, BC])
        first = s.sb("first", [BP, BC])
        flag = s.sb("flag", [BP, 2])
        wide = s.sb("wide", [BP, 2, P])
        cont = s.sb("cont", [P, BP])
        through = s.sb("through", [P, BP])
        passed = s.sb("passed", [P, BP])
        last = s.sb("last", [P, BP + 1])
        carry_in = s.sb("carry_in", [P, BP])
        carry_row = s.sb("carry_row", [P, BP])
        carry = s.sb("carry", [BP, P])
        zeros = s.sb("zeros", [P, BLOCK * ROW0 // P // 4])
        got = s.sb("got", [P, TILES, ROW0])
        row_f = s.sb("row_f", [P, TILES])
        row_idx = s.sb("row_idx", [P, TILES], I32)
        mine = s.sb("mine", [P, TILES])
        wide_ps = s.ps("wide_ps", [P, 2, P])
        last_ps = s.ps("last_ps", [P, P])
        carry_ps = s.ps("carry_ps", [P, P])
        wide_ready, wide_turned, scanned, last_turned, carry_ready, carry_back, summed, claimed = map(
            s.sem, ("wide_ready", "wide_turned", "scanned", "last_turned", "carry_ready", "carry_back",
                    "summed", "claimed"))
        start, step, stored, free, rows_known, round_stored, fetched, round_added, round_step = map(
            s.sem, ("start", "step", "stored", "free", "rows_known", "round_stored", "fetched", "round_added",
                    "round_step"))
        free_again = s.sem("free_again")
        loaded = [s.sem(f"loaded{b}") for b in range(2)]
        landed = [s.sem(f"landed{b}") for b in range(2)]
        block = s.block()

        def each_round(eng, before, body, otherwise, after):
            def load(k):
                return eng.value_load(env.block_first[0:1, bass.ds(k, 1)])

            with eng.Fori(0, ROUNDS) as r:
                with eng.If(load(r * PER_ROUND) < NODES0):
                    before(r)
                    with eng.Fori(0, PER_ROUND // 2) as i:
                        for b in range(2):
                            k = r * PER_ROUND + i * 2 + b
                            first_dst = load(k)
                            with eng.If(first_dst < NODES0):
                                body(b, r * (PER_ROUND // 2) + i, k, i * 2 + b)
                            if otherwise is not None:
                                with eng.If(first_dst >= NODES0):
                                    otherwise(k, i * 2 + b)
                    after(r)

        nothing = lambda r: None

        @block.sync
        def _(sp):
            def body(b, i, k, kr):
                sp.wait_ge(free, k + 1)
                at = k * BLOCK
                sp.dma_start(idx[:, b, :], env.idx0_d[bass.ds(at, BLOCK)].rearrange("(p c) -> p c", c=BC)
                             ).then_inc(loaded[b], 16)
                sp.dma_start(dst[:, b, 1:BC + 1], env.dst_d[bass.ds(at + LEAD, BLOCK)]
                             .rearrange("(p c) -> p c", c=BC)).then_inc(loaded[b], 16)
                sp.dma_start(dst[:, b, 0:1], env.dst_d[bass.ds(at + LEAD - 1, BLOCK)]
                             .rearrange("(p c) -> p c", c=BC)[:, 0:1]).then_inc(loaded[b], 16)
            each_round(sp, nothing, body, None, nothing)

        @block.gpsimd
        def _(pool):
            def body(b, i, k, kr):
                pool.wait_ge(loaded[b], (i + 1) * 48)
                pool.sem_inc(claimed, 1)
                fetch(nc, pool, rows[:, b], env.table0, idx[:, b], BC, landed[b])

            def after(r):
                pool.wait_ge(rows_known, r + 1)
                pool.wait_ge(round_stored, r + 1)
                pool.sem_inc(claimed, 1)
                fetch(nc, pool, got, env.sums0, row_idx, TILES, fetched)
                pool.wait_ge(round_added, r + 1)
                pool.sem_inc(claimed, 1)
            each_round(pool, nothing, body, None, after)

        @block.tensor
        def _(pe):
            def body(b, i, k, kr):
                pe.wait_ge(wide_ready, k + 1)
                for j in range(2):
                    mm = nc.tensor.transpose(wide_ps[:, j, 0:BP], wide[:, j, :], env.ident[0:BP, 0:BP])
                mm.then_inc(wide_turned, 1)
                pe.wait_ge(scanned, k + 1)
                nc.tensor.transpose(last_ps[:, 0:BP], rows[:, b, BC - 1, :], env.ident[0:BP, 0:BP]
                                    ).then_inc(last_turned, 1)
                pe.wait_ge(carry_ready, k + 1)
                nc.tensor.transpose(carry_ps[0:BP, :], carry_row[:, :], env.ident[:, :]).then_inc(carry_back, 1)
            each_round(pe, nothing, body, None, nothing)

        @block.scalar
        def _(act):
            act.wait_ge(start, 2)
            act.sem_inc(free, 2)

            def body(b, i, k, kr):
                act.wait_ge(summed, k + 1)
                act.dma_start(env.sums0[bass.ds(kr * BLOCK, BLOCK), :].rearrange("(p c) f -> p c f", c=BC),
                              rows[:, b, :, :]).then_inc(stored, 64)
                act.wait_ge(stored, (k + 1) * 64)
                act.sem_inc(free, 1)

            def otherwise(k, kr):
                part = BLOCK // 4
                for q in range(4):
                    act.dma_start(env.sums0[bass.ds(kr * BLOCK + q * part, part), :].rearrange("e f -> (e f)")
                                  .rearrange("(p c) -> p c", p=P), zeros[:, :]).then_inc(stored, 16)

            def after(r):
                act.wait_ge(stored, (r + 1) * (64 * PER_ROUND))
                act.sem_inc(round_stored, 1)
                act.wait_ge(round_added, r + 1)
                act.sem_inc(free_again, 1)
            each_round(act, nothing, body, otherwise, after)

        @block.vector
        def _(dve):
            nc.vector.memset(last[:, 0:1], 0.0)
            nc.vector.memset(env.layer0[:, :, :], 0.0).then_inc(start, 1)
            nc.vector.memset(zeros[:, :], 0.0).then_inc(start, 1)
            dve.wait_ge(start, 2)
            per_round = 6
            per = 14

            def before(r):
                st = Steps(dve, round_step, r * per_round)
                at, to = env.round_at[:, bass.ds(r, 1)], env.round_at[:, bass.ds(r + 1, 1)]
                st(nc.vector.tensor_scalar(row_f[:, :], env.end0[:, :], at, 0.0, ALU.subtract, ALU.max))
                st(nc.vector.scalar_tensor_tensor(mine[:, :], env.end0[:, :], at, env.some0[:, :], ALU.is_ge, ALU.mult))
                st.wait()
                st(nc.vector.tensor_scalar(row_idx[:, :], row_f[:, :], float(ROUND - 1), None, ALU.min))
                st(nc.vector.scalar_tensor_tensor(mine[:, :], env.end0[:, :], to, mine[:, :], ALU.is_lt, ALU.mult))
                st.wait()
                dve.sem_inc(rows_known, 1)

            def after(r):
                st = Steps(dve, round_step, r * per_round + 4)
                dve.wait_ge(fetched, (r + 1) * (16 * TILES))
                st(nc.vector.tensor_tensor(got[:, :, :], got[:, :, :],
                                           mine[:, :].unsqueeze(2).to_broadcast([P, TILES, ROW0]), ALU.mult))
                st.wait()
                st(nc.vector.tensor_tensor(env.layer0[:, :, :], env.layer0[:, :, :], got[:, :, :], ALU.add))
                st.wait()
                dve.sem_inc(round_added, 1)

            def body(b, i, k, kr):
                st = Steps(dve, step, k * per)
                dve.wait_ge(loaded[b], (i + 1) * 48)
                st(nc.vector.tensor_tensor(keep[:, :], dst[:, b, 1:BC + 1], dst[:, b, 0:BC], ALU.is_equal))
                st(nc.vector.tensor_scalar(first[:, :], dst[:, b, 1:BC + 1], dst[:, b, 1:2], None, ALU.is_equal))
                st(nc.vector.tensor_tensor(flag[:, 1:2], dst[:, b, 1:2], dst[:, b, BC:BC + 1], ALU.is_equal))
                st.wait()
                st(nc.vector.tensor_copy(wide[:, 0, :], keep[:, 0:1].to_broadcast([BP, P])))
                st(nc.vector.tensor_copy(wide[:, 1, :], flag[:, 1:2].to_broadcast([BP, P])))
                st.wait()
                dve.sem_inc(wide_ready, 1)
                dve.wait_ge(wide_turned, k + 1)
                st(nc.vector.tensor_copy(cont[:, :], wide_ps[:, 0, 0:BP]))
                st(nc.vector.tensor_copy(through[:, :], wide_ps[:, 1, 0:BP]))
                st(nc.vector.memset(passed[:, 0:1], 0.0))
                st.wait()
                st(nc.vector.tensor_tensor(passed[:, 1:BP], cont[:, 1:BP], through[:, 0:BP - 1], ALU.mult))
                dve.wait_ge(landed[b], (i + 1) * (16 * BC))
                for f in range(ROW0):
                    one = nc.vector.tensor_tensor_scan(rows[:, b, :, f], keep[:, :], rows[:, b, :, f], 0.0,
                                                       ALU.mult, ALU.add)
                one.then_inc(scanned, 1)
                dve.wait_ge(last_turned, k + 1)
                st(nc.vector.tensor_copy(last[:, 1:BP + 1], last_ps[:, 0:BP]))
                st.wait()
                st(nc.vector.tensor_tensor(carry_in[:, :], cont[:, :], last[:, 0:BP], ALU.mult))
                st.wait()
                nc.vector.tensor_tensor_scan(carry_row[:, :], passed[:, :], carry_in[:, :], 0.0,
                                             ALU.mult, ALU.add).then_inc(carry_ready, 1)
                dve.wait_ge(carry_ready, k + 1)
                st(nc.vector.scalar_tensor_tensor(last[:, 0:1], carry_row[:, BP - 1:BP], through[:, BP - 1:BP],
                                                  last[:, BP:BP + 1], ALU.mult, ALU.add))
                dve.wait_ge(carry_back, k + 1)
                st(nc.vector.tensor_copy(carry[:, :], carry_ps[0:BP, :]))
                st.wait()
                for c in range(BC):
                    one = nc.vector.scalar_tensor_tensor(rows[:, b, c, :], carry[:, :], first[:, c:c + 1],
                                                         rows[:, b, c, :], ALU.mult, ALU.add)
                st(one)
                st.wait()
                dve.sem_inc(summed, 1)
                assert st.n == 14, st.n
            each_round(dve, before, body, None, after)


def layer_norm(nc, st, x, sq, mean, var, slots, act_root):
    stat = lambda t: t.unsqueeze(2).to_broadcast([P, slots, FEAT])
    st(nc.vector.tensor_reduce(mean, x, AX.X, ALU.add))
    st.wait()
    st(nc.vector.tensor_scalar(mean, mean, 1.0 / FEAT, None, ALU.mult))
    st.wait()
    st(nc.vector.tensor_tensor(x, x, stat(mean), ALU.subtract))
    st.wait()
    st(nc.vector.tensor_tensor(sq, x, x, ALU.mult))
    st.wait()
    st(nc.vector.tensor_reduce(var, sq, AX.X, ALU.add))
    st.wait()
    st(nc.vector.tensor_scalar(var, var, 1.0 / FEAT, EPS, ALU.mult, ALU.add))
    st.wait()
    act_root()
    st(nc.vector.reciprocal(var, var))
    st.wait()
    st(nc.vector.tensor_tensor(x, x, stat(var), ALU.mult))
    st.wait()


def stage_x1(nc, env, weights, table, root_out, x1_d):
    slots = TILES * CH
    with ExitStack() as ctx:
        s = Scope(nc, ctx, "x1")
        x_sb = s.sb("x_sb", [P, TILES, ROW0])
        mean = s.sb("mean", [P, slots])
        var = s.sb("var", [P, slots])
        idx = s.sb("idx", [P, 2, NWIN], I32)
        got = s.sb("got", [P, 2, NWIN, WIN])
        cmp = s.sb("cmp", [P, NWIN, WIN])
        n_le = s.sb("n_le", [P, NWIN])
        n_eq = s.sb("n_eq", [P, NWIN])
        loaded, zeroed, step, var_ready, rooted, idx_ready, claimed, find_step, x1_ready, x1_stored = map(
            s.sem, ("loaded", "zeroed", "step", "var_ready", "rooted", "idx_ready", "claimed", "find_step",
                    "x1_ready", "x1_stored"))
        landed = [s.sem(f"landed{b}") for b in range(2)]
        tb = Table(nc, env, s, x_sb, weights, table, root_out)
        block = s.block()

        @block.sync
        def _(sp):
            sp.wait_ge(zeroed, 1)
            load_x(sp, env, x_sb, loaded)
            tb.load_weights(sp)
            sp.wait_ge(x1_ready, 1)
            sp.dma_start(x1_d.rearrange("(t n) f -> n t f", n=P), x_sb[:, :, :]).then_inc(x1_stored, 16)
            tb.sp(sp)
            sp.wait_ge(x1_stored, 16)

        @block.gpsimd
        def _(pool):
            with pool.Fori(0, NWINS // 2) as i:
                for b in range(2):
                    pool.wait_ge(idx_ready, i * 2 + b + 1)
                    pool.sem_inc(claimed, 1)
                    fetch(nc, pool, got[:, b], env.dst_rows, idx[:, b], NWIN, landed[b])

        @block.scalar
        def _(act):
            act.wait_ge(var_ready, 1)
            nc.scalar.activation(var[:, :], var[:, :], ACT.Sqrt).then_inc(rooted, 1)
            tb.act(act)

        @block.tensor
        def _(pe):
            tb.pe(pe)

        @block.vector
        def _(dve):
            st = Steps(dve, step)
            nc.vector.memset(x_sb[:, TILES - 1, :], 0.0).then_inc(zeroed, 1)
            for b in range(2):
                nc.vector.tensor_copy(idx[:, b, :], env.win_idx[:, (b + 1) * NWIN:(b + 2) * NWIN]).then_inc(idx_ready, 1)
            dve.wait_ge(loaded, 32)
            st(nc.vector.tensor_tensor(x_sb[:, :, :], x_sb[:, :, :], env.layer0[:, :, :], ALU.add))
            st.wait()

            def root():
                dve.sem_inc(var_ready, 1)
                dve.wait_ge(rooted, 1)
            layer_norm(nc, st, x_sb[:, :, :].rearrange("p t (o b) -> p (t o) b", b=FEAT),
                       env.layer0[:, :, :].rearrange("p t (o b) -> p (t o) b", b=FEAT),
                       mean[:, :], var[:, :], slots, root)
            dve.sem_inc(x1_ready, 1)
            dve.sem_inc(tb.group_ready, NWINS)
            tb.make_mix(dve)

            def compare(b, i, more):
                w = i * 2 + b + 1
                dve.wait_ge(landed[b], (i + 1) * (16 * NWIN))
                find_last_edges(nc, dve, env, got[:, b, :, :], cmp, n_le, n_eq, find_step,
                                (i * 2 + b) * FIND_STEPS, bass.ds(w * NWIN, NWIN))
                if more:
                    nc.vector.tensor_copy(idx[:, b, :], env.win_idx[:, bass.ds((w + 2) * NWIN, NWIN)]
                                          ).then_inc(idx_ready, 1)
            with dve.Fori(0, NWINS // 2 - 1) as i:
                for b in range(2):
                    compare(b, i, True)
            for b in range(2):
                compare(b, NWINS // 2 - 1, False)


class Norm:

    def __init__(self, nc, env, s):
        self.nc, self.env = nc, env
        s = Scope(nc, s.ctx, s.prefix + "n")
        self.count = s.sb("count", [P, COLS])
        self.rel = s.sb("rel", [P, COLS], BF16)
        self.in_first = s.sb("in_first", [P, COLS], BF16)
        self.in_last = s.sb("in_last", [P, COLS], BF16)
        self.is_end = s.sb("is_end", [P, COLS], BF16)
        self.mine = s.sb("mine", [P, COLS], BF16)
        self.ends = s.sb("ends", [P, 2, RELS])
        self.length = s.sb("length", [P, 1])
        self.carry_in = s.sb("carry_in", [RELS, 2, P])
        self.carry_row = s.sb("carry_row", [RELS, 2, P])
        self.start_row = s.sb("start_row", [RELS, 2, P])
        self.start = s.sb("start", [P, 2, RELS])
        self.ends_ps = s.ps("ends_ps", [RELS, 2, P])
        self.start_ps = s.ps("start_ps", [P, 2, RELS])
        (self.padded, self.type_in, self.dst_in, self.summed, self.turned, self.rows_ready, self.returned,
         self.step, self.ends_step, self.count_step) = map(s.sem, (
             "padded", "type_in", "dst_in", "summed", "turned", "rows_ready", "returned", "nstep", "ends_step",
             "count_step"))

    def sp(self, sp):
        rows, typ = P - 1, self.env.norm[:, :].bitcast(I32)
        split = rows * COLS
        sp.wait_ge(self.padded, 1)
        sp.dma_start(typ[0:rows, :], self.env.type8[0:split].rearrange("(p c) -> p c", p=rows)).then_inc(self.type_in, 16)
        sp.dma_start(typ[rows:P, 0:LAST_VALID],
                     self.env.type8[split:EDGES].rearrange("(p c) -> p c", p=1)).then_inc(self.type_in, 16)
        sp.dma_start(self.count[:, :], self.env.dst_d[LEAD:LEAD + P * COLS].rearrange("(p c) -> p c", c=COLS)
                     ).then_inc(self.dst_in, 16)

    def pe(self, pe):
        pe.wait_ge(self.summed, RELS)
        for j in range(2):
            self.nc.tensor.transpose(self.ends_ps[:, j, :], self.ends[:, j, :],
                                     self.env.ident[:, :]).then_inc(self.turned, 1)
        pe.wait_ge(self.rows_ready, 1)
        for j in range(2):
            self.nc.tensor.transpose(self.start_ps[:, j, :], self.start_row[:, j, :],
                                     self.env.ident[0:RELS, 0:RELS]).then_inc(self.returned, 1)

    def dve(self, dve):
        nc, env = self.nc, self.env
        count, mine = self.count, self.mine
        dst_f = count
        typ = env.norm[:, :].bitcast(I32)
        st = Steps(dve, self.step)
        nc.vector.memset(typ[:, LAST_VALID:], 0).then_inc(self.padded, 1)
        dve.wait_ge(self.type_in, 32)
        st(nc.vector.tensor_copy(self.rel[:, :], typ))
        dve.wait_ge(self.dst_in, 16)
        st(nc.vector.tensor_scalar(self.in_first[:, :], dst_f[:, :], dst_f[:, 0:1], None, ALU.is_equal))
        st(nc.vector.tensor_scalar(self.in_last[:, :], dst_f[:, :], dst_f[:, COLS - 1:COLS], None, ALU.is_equal))
        st(nc.vector.tensor_scalar(self.is_end[:, :], env.keep[:, 1:COLS + 1], -1.0, 1.0, ALU.mult, ALU.add))
        st(nc.vector.memset(self.carry_in[:, :, :], 0.0))
        st(nc.vector.memset(self.start_row[:, :, :], 0.0))
        st.wait()
        st(nc.vector.tensor_reduce(self.length[:, :], self.in_first[:, :], AX.X, ALU.add))
        st(nc.vector.memset(env.norm[:, :], 0.0))
        st.wait()
        st(nc.vector.tensor_tensor(env.fix_idx[:, :], env.fix_base[:, :], self.length[:, :], ALU.add))
        per = 2
        with dve.Fori(0, RELS) as r:
            stl = Steps(dve, self.ends_step, r * per)
            for j, seg in enumerate((self.in_first, self.in_last)):
                stl(nc.vector.scalar_tensor_tensor(mine[:, :], self.rel[:, :], env.rel_id[:, bass.ds(r, 1)], seg[:, :],
                                                   ALU.is_equal, ALU.mult, accum_out=self.ends[:, j, bass.ds(r, 1)]))
                stl.wait()
            dve.sem_inc(self.summed, 1)
            assert stl.n == per
        dve.wait_ge(self.turned, 2)
        cont = env.cont_row[0:RELS, 1:P]
        st(nc.vector.tensor_tensor(self.carry_in[:, 0, 1:P], cont, self.ends_ps[:, 1, 0:P - 1], ALU.mult))
        st(nc.vector.tensor_tensor(self.carry_in[:, 1, 0:P - 1], cont, self.ends_ps[:, 0, 1:P], ALU.mult))
        st.wait()
        st(nc.vector.tensor_tensor_scan(self.carry_row[:, 0, :], env.pass_row[0:RELS, :], self.carry_in[:, 0, :], 0.0,
                                        ALU.mult, ALU.add))
        st(nc.vector.tensor_tensor_scan(self.carry_row[:, 1, ::-1], env.back_row[0:RELS, ::-1],
                                        self.carry_in[:, 1, ::-1], 0.0, ALU.mult, ALU.add))
        st.wait()
        st(nc.vector.tensor_copy(self.start_row[:, 0, :], self.carry_row[:, 0, :]))
        st(nc.vector.tensor_tensor(self.start_row[:, 1, 0:P - 1], self.carry_row[:, 0, 1:P],
                                   self.carry_row[:, 1, 0:P - 1], ALU.add))
        st.wait()
        dve.sem_inc(self.rows_ready, 1)
        dve.wait_ge(self.returned, 2)
        st(nc.vector.tensor_copy(self.start[:, :, :], self.start_ps[:, :, :]))
        st.wait()
        per = 6
        with dve.Fori(0, RELS) as r:
            stl = Steps(dve, self.count_step, r * per)
            at = bass.ds(r, 1)
            stl(nc.vector.tensor_scalar(mine[:, :], self.rel[:, :], env.rel_id[:, at], None, ALU.is_equal))
            stl.wait()
            stl(nc.vector.tensor_tensor_scan(count[:, :], env.keep[:, 0:COLS], mine[:, :], self.start[:, 0, at],
                                             ALU.mult, ALU.add))
            stl.wait()
            stl(nc.vector.tensor_tensor(count[:, :], count[:, :], self.is_end[:, :], ALU.mult))
            stl.wait()
            stl(nc.vector.tensor_tensor_scan(count[:, ::-1], env.keep[:, COLS:0:-1], count[:, ::-1],
                                             self.start[:, 1, at], ALU.mult, ALU.add))
            stl.wait()
            stl(nc.vector.tensor_tensor(count[:, :], count[:, :], mine[:, :], ALU.mult))
            stl.wait()
            stl(nc.vector.tensor_tensor(env.norm[:, :], env.norm[:, :], count[:, :], ALU.add))
            stl.wait()
            assert stl.n == per
        st(nc.vector.tensor_scalar_max(env.norm[:, :], env.norm[:, :], 1.0))
        st.wait()
        st(nc.vector.reciprocal(env.norm[:, :], env.norm[:, :]))
        st.wait()


def stage_sum1(nc, env, name, table, sums, with_norm):
    with ExitStack() as ctx:
        s = Scope(nc, ctx, name)
        rows = s.sb("rows", [P, RING, WIN, FEAT])
        idx = s.sb("idx", [P, RING, WIN], I32)
        so_far = s.sb("so_far", [P, FEAT])
        idx_ready, claimed, summed, step, start = map(s.sem, ("idx_ready", "claimed", "summed", "step", "start"))
        landed = [s.sem(f"landed{b}") for b in range(RING)]
        stored = [s.sem(f"stored{b}") for b in range(RING)]
        norm = Norm(nc, env, s) if with_norm else None
        block = s.block()
        out = sums.rearrange("(p c) f -> p c f", p=P)
        turns = WINS // RING

        @block.gpsimd
        def _(pool):
            with pool.Fori(0, turns) as i:
                for b in range(RING):
                    pool.wait_ge(idx_ready, i * RING + b + 1)
                    pool.sem_inc(claimed, 1)
                    fetch(nc, pool, rows[:, b], table, idx[:, b], WIN, landed[b])

        @block.sync
        def _(sp):
            if norm:
                norm.sp(sp)
            with sp.Fori(0, turns) as i:
                for b in range(RING):
                    sp.wait_ge(summed, i * RING + b + 1)
                    sp.dma_start(out[:, bass.ds((i * RING + b) * WIN, WIN), :], rows[:, b, :, :]).then_inc(stored[b], 16)
            for b in range(RING):
                sp.wait_ge(stored[b], 16 * turns)

        if norm:
            @block.tensor
            def _(pe):
                norm.pe(pe)

        @block.vector
        def _(dve):
            nc.vector.memset(so_far[:, :], 0.0).then_inc(start, 1)
            for b in range(RING):
                nc.vector.tensor_copy(idx[:, b, :], env.idx1[:, b * WIN:(b + 1) * WIN]).then_inc(idx_ready, 1)
            dve.wait_ge(start, 1)
            if norm:
                norm.dve(dve)
            per = 3

            def refill(b, i):
                dve.wait_ge(stored[b], (i + 1) * 16)
                nc.vector.tensor_copy(idx[:, b, :], env.idx1[:, bass.ds(((i + 1) * RING + b) * WIN, WIN)]
                                      ).then_inc(idx_ready, 1)

            def turn(i, more):
                for b in range(RING):
                    w = i * RING + b
                    st = Steps(dve, step, w * per)
                    dve.wait_ge(landed[b], (i + 1) * (16 * WIN))
                    scale = env.norm[:, bass.ds(w * WIN, WIN)].unsqueeze(2).to_broadcast([P, WIN, FEAT])
                    st(nc.vector.tensor_tensor(rows[:, b, :, :], rows[:, b, :, :], scale, ALU.mult))
                    st.wait()
                    for f in range(FEAT):
                        one = nc.vector.tensor_tensor_scan(rows[:, b, :, f], env.keep[:, bass.ds(w * WIN, WIN)],
                                                           rows[:, b, :, f], so_far[:, f:f + 1], ALU.mult, ALU.add)
                    st(one)
                    st.wait()
                    dve.sem_inc(summed, 1)
                    st(nc.vector.tensor_copy(so_far[:, :], rows[:, b, WIN - 1, :]))
                    st.wait()
                    if more and b:
                        refill(b - 1, i)
                    assert st.n == per
                if more:
                    refill(RING - 1, i)
            with dve.Fori(0, turns - 1) as i:
                turn(i, True)
            turn(turns - 1, False)


def stage_nodes1(nc, env, name, sums, root_d, bias, x1_d, table_args):
    slots = TILES * CH
    last_stage = table_args is None
    with ExitStack() as ctx:
        s = Scope(nc, ctx, name)
        root = s.sb("root", [P, TILES, ROW0])
        x1 = s.sb("x1", [P, TILES, ROW0] if last_stage else [P, 1, 1])
        bias_in = s.sb("bias_in", [P, FEAT])
        root_in = s.sem("root_in")
        tb = None if last_stage else Table(nc, env, s, root, *table_args)
        ends = s.sb("ends", [P, 2, FEAT])
        carry_in = s.sb("carry_in", [FEAT, P])
        carry_row = s.sb("carry_row", [FEAT, P])
        idx = s.sb("idx", [P, 2, NWIN], I32)
        got = s.sb("got", [P, 2, NWIN, FEAT])
        big = s.sb("big", [P, slots, FEAT] if last_stage else [P, 1, FEAT])
        stat1 = s.sb("stat1", [P, slots])
        stat2 = s.sb("stat2", [P, slots])
        small_ps = s.ps("small_ps", [P, 2, P]) if last_stage else tb.turn_ps[0][:, 0:2 * P].rearrange(
            "p (a b) -> p a b", a=2)
        last_ps = small_ps[0:FEAT, 0, :]
        carry_ps = small_ps[:, 1, 0:FEAT]
        ends_in, fix_in, turned, carry_ready, carry_back, fixed, patched = map(
            s.sem, ("ends_in", "fix_in", "turned", "carry_ready", "carry_back", "fixed", "patched"))
        idx_ready, claimed, added, step, step2, step3, asked, answered, stored = map(
            s.sem, ("idx_ready", "claimed", "added", "step", "step2", "step3", "asked", "answered", "stored"))
        landed = [s.sem(f"landed{b}") for b in range(2)]
        block = s.block()
        out3 = root[:, :, :].rearrange("p t (o c) -> p (t o) c", c=FEAT)

        @block.sync
        def _(sp):
            sp.dma_start(ends[:, 1, :], sums.rearrange("(p c) f -> p c f", p=P)[:, COLS - 1, :]).then_inc(ends_in, 16)
            sp.dma_start(bias_in[:, :], bias.rearrange("(a c) -> a c", a=1).to_broadcast([P, FEAT])).then_inc(root_in, 16)
            sp.dma_start(root[:, :, :], root_d.rearrange("(t n) f -> n t f", n=P)).then_inc(root_in, 16)
            if last_stage:
                sp.dma_start(x1[:, :, :], x1_d.rearrange("(t n) f -> n t f", n=P)).then_inc(root_in, 16)
            else:
                tb.load_weights(sp)
                tb.sp(sp)
            if last_stage:
                sp.wait_ge(asked, 4)
                sp.dma_start(env.out[0:(TILES - 1) * P * CH, :].rearrange("(t n o) b -> n t (o b)", n=P, o=CH),
                             root[:, 0:TILES - 1, :]).then_inc(stored, 16)
                sp.dma_start(env.out[(TILES - 1) * P * CH:NODES1, :].rearrange("(n o) b -> n (o b)", o=CH),
                             root[0:TAIL, TILES - 1, :]).then_inc(stored, 16)
                sp.wait_ge(stored, 32)

        @block.gpsimd
        def _(pool):
            pool.indirect_dma_start(out=ends[:, 0, :], out_offset=None, in_=sums,
                                    in_offset=bass.IndirectOffsetOnAxis(ap=env.fix_idx[:, 0:1], axis=0)
                                    ).then_inc(fix_in, 16)
            pool.wait_ge(fixed, 1)
            pool.indirect_dma_start(out=sums, out_offset=bass.IndirectOffsetOnAxis(ap=env.fix_idx[:, 0:1], axis=0),
                                    in_=ends[:, 0, :], in_offset=None).then_inc(patched, 16)
            pool.wait_ge(patched, 16)

            def window(b, ready):
                pool.wait_ge(idx_ready, ready)
                pool.sem_inc(claimed, 1)
                for j in range(NWIN):
                    pool.indirect_dma_start(
                        out=got[:, b, j, :], out_offset=None, in_=sums,
                        in_offset=bass.IndirectOffsetOnAxis(ap=idx[:, b, j:j + 1], axis=0)
                    ).then_inc(landed[b], 16)
            window(0, 1)
            with pool.Fori(0, NWINS // 2) as i:
                window(1, i * 2 + 2)
                window(0, i * 2 + 3)

        @block.tensor
        def _(pe):
            pe.wait_ge(ends_in, 16)
            nc.tensor.transpose(last_ps, ends[:, 1, :], env.ident[:, :]).then_inc(turned, 1)
            pe.wait_ge(carry_ready, 1)
            nc.tensor.transpose(carry_ps, carry_row[:, :], env.ident[0:FEAT, 0:FEAT]).then_inc(carry_back, 1)
            if tb:
                tb.pe(pe)

        @block.scalar
        def _(act):
            if tb:
                tb.act(act)
            if last_stage:
                act.wait_ge(asked, 1)
                nc.scalar.activation(big[:, :, :], out3, ACT.Exp).then_inc(answered, 1)
                act.wait_ge(asked, 2)
                nc.scalar.activation(stat1[:, :], stat1[:, :], ACT.Ln).then_inc(answered, 1)
                act.wait_ge(asked, 3)
                nc.scalar.activation(stat2[:, :], stat2[:, :], ACT.Sqrt).then_inc(answered, 1)

        @block.vector
        def _(dve):
            st = Steps(dve, step)
            st(nc.vector.memset(carry_in[:, 0:1], 0.0))
            for b in range(2):
                nc.vector.tensor_copy(idx[:, b, :], env.end_idx[:, b * NWIN:(b + 1) * NWIN]).then_inc(idx_ready, 1)
            dve.wait_ge(turned, 1)
            st(nc.vector.tensor_tensor(carry_in[:, 1:P], env.cont_row[0:FEAT, 1:P], last_ps[:, 0:P - 1], ALU.mult))
            st.wait()
            nc.vector.tensor_tensor_scan(carry_row[:, :], env.pass_row[0:FEAT, :], carry_in[:, :], 0.0,
                                         ALU.mult, ALU.add).then_inc(carry_ready, 1)
            dve.wait_ge(carry_back, 1)
            dve.wait_ge(fix_in, 16)
            nc.vector.tensor_tensor(ends[:, 0, :], ends[:, 0, :], carry_ps, ALU.add).then_inc(fixed, 1)
            if tb:
                tb.make_mix(dve)
            dve.wait_ge(root_in, 48 if last_stage else 32)
            per = 4

            def window(b, w, arrived, more):
                dve.wait_ge(landed[b], arrived)
                st2 = Steps(dve, step2, w * per)
                some = env.has_edge[:, bass.ds(w * NWIN, NWIN)].unsqueeze(2).to_broadcast([P, NWIN, FEAT])
                st2(nc.vector.tensor_tensor(got[:, b, :, :], got[:, b, :, :], some, ALU.mult))
                st2.wait()
                st2(nc.vector.tensor_tensor(got[:, b, :, :], got[:, b, :, :],
                                            bias_in[:, :].unsqueeze(1).to_broadcast([P, NWIN, FEAT]), ALU.add))
                st2.wait()
                to = root[:, bass.ds(w * TPW, TPW), :].rearrange("p t (o c) -> p (t o) c", c=FEAT)
                st2(nc.vector.tensor_tensor(to, to, got[:, b, :, :], ALU.add))
                st2.wait()
                if more:
                    nc.vector.tensor_copy(idx[:, b, :], env.end_idx[:, bass.ds((w + 2) * NWIN, NWIN)]
                                          ).then_inc(idx_ready, 1)
                if last_stage:
                    st2(nc.vector.tensor_reduce(stat1[:, bass.ds(w * NWIN, NWIN)], to, AX.X, ALU.max))
                else:
                    st2(nc.vector.tensor_scalar(to, to, 0.0, None, ALU.max))
                st2.wait()
                if tb:
                    dve.sem_inc(tb.group_ready, 1)
                assert st2.n == per
            full = 16 * NWIN
            with dve.Fori(0, NWINS // 2 - 1) as i:
                for b in range(2):
                    window(b, i * 2 + b, (i + 1) * full, True)
            window(0, NWINS - 3, (NWINS // 2) * full, True)
            window(1, NWINS - 2, (NWINS // 2) * full, False)
            window(0, NWINS - 1, (NWINS // 2 + 1) * full, False)
            if last_stage:
                st3 = Steps(dve, step3)
                stat = lambda t: t.unsqueeze(2).to_broadcast([P, slots, FEAT])
                st3(nc.vector.tensor_tensor(out3, out3, stat(stat1[:, :]), ALU.subtract))
                st3.wait()
                dve.sem_inc(asked, 1)
                dve.wait_ge(answered, 1)
                st3(nc.vector.tensor_reduce(stat1[:, :], big[:, :, :], AX.X, ALU.add))
                st3.wait()
                dve.sem_inc(asked, 1)
                dve.wait_ge(answered, 2)
                st3(nc.vector.tensor_tensor(out3, out3, stat(stat1[:, :]), ALU.subtract))
                st3.wait()
                st3(nc.vector.tensor_tensor(root[:, :, :], root[:, :, :], x1[:, :, :], ALU.add))
                st3.wait()

                def take_root():
                    dve.sem_inc(asked, 1)
                    dve.wait_ge(answered, 3)
                layer_norm(nc, st3, out3, big[:, :, :], stat1[:, :], stat2[:, :], slots, take_root)
                dve.sem_inc(asked, 1)


class Env:
    pass


def gnn_layers(nc, x, src, dst, type6, type8, w0, b0, w1, root1, bias1, w2, root2, bias2, eye, out):
    env = Env()
    env.x, env.src, env.dst, env.type6, env.type8, env.eye, env.out = x, src, dst, type6, type8, eye, out
    env.w0, env.b0 = w0, b0
    dram = lambda name, shape, dt=F32: nc.dram_tensor(name, shape, dt, kind="Internal").ap()
    env.idx0_d = dram("idx0_d", (P * COLS,), I32)
    env.dst_d = dram("dst_d", (LEAD + P * COLS,))
    env.dst_rows = env.dst_d.rearrange("(r c) -> r c", c=WIN)
    env.end_d = dram("end_d", (TPW * P * CH,), I32)
    env.some_d = dram("some_d", (TPW * P * CH,))
    env.table0 = dram("table0", (NODES0 * TYPES0, ROW0))
    env.sums0 = dram("sums0", (ROUND, ROW0))
    table1 = dram("table1", (NODES1 * RELS, FEAT))
    table2 = dram("table2", (NODES1 * RELS, FEAT))
    root1_d = dram("root1_d", (TILES * P, ROW0))
    root2_d = dram("root2_d", (TILES * P, ROW0))
    x1_d = dram("x1_d", (TILES * P, ROW0))
    sums1 = dram("sums1", (P * COLS, FEAT))
    sums2 = dram("sums2", (P * COLS, FEAT))
    slots = TILES * CH
    with ExitStack() as ctx:
        ctx.enter_context(nc.allow_non_contiguous_dma(reason="single columns of the edge list, a few of them"))
        s = Scope(nc, ctx, "all")
        env.ident = s.sb("ident", [P, P])
        env.idx1 = s.sb("idx1", [P, COLS], I32)
        env.keep = s.sb("keep", [P, COLS + 1], BF16)
        env.cont_row = s.sb("cont_row", [P, P])
        env.pass_row = s.sb("pass_row", [P, P])
        env.back_row = s.sb("back_row", [P, P])
        env.fix_idx = s.sb("fix_idx", [P, 1], I32)
        env.fix_base = s.sb("fix_base", [P, 1], I32)
        env.rel_id = s.sb("rel_id", [P, RELS])
        env.end_idx = s.sb("end_idx", [P, slots], I32)
        env.has_edge = s.sb("has_edge", [P, slots])
        with ExitStack() as early:
            e = Scope(nc, early, "early")
            env.block_first = e.sb("block_first", [1, BLOCKS], I32)
            env.first_dst = e.sb("first_dst", [P, 1])
            env.round_at = e.sb("round_at", [P, ROUNDS + 1])
            env.node = e.sb("node", [P, slots])
            env.win_row = e.sb("win_row", [P, slots])
            env.win_idx = e.sb("win_idx", [P, slots], I32)
            env.end0 = e.sb("end0", [P, TILES], I32)
            env.some0 = e.sb("some0", [P, TILES])
            stage_edges(nc, env)
            stage_first(nc, env)
            stage_ends0(nc, env)
            env.layer0 = e.sb("layer0", [P, TILES, ROW0])
            stage_sum0(nc, env)
            stage_x1(nc, env, (w1, root1), table1, root1_d, x1_d)
        env.norm = s.sb("norm", [P, COLS])
        stage_sum1(nc, env, "s1", table1, sums1, True)
        stage_nodes1(nc, env, "n1", sums1, root1_d, bias1, x1_d, ((w2, root2), table2, root2_d))
        stage_sum1(nc, env, "s2", table2, sums2, False)
        stage_nodes1(nc, env, "n2", sums2, root2_d, bias2, x1_d, None)


def kernel(**inputs):
    import numpy as _np
    import concourse.bacc as _bacc
    from concourse import mybir as _mybir
    from concourse.bass_utils import run_bass_kernel_spmd as _run

    nc = _bacc.Bacc("TRN2", target_bir_lowering=False, num_devices=1)
    names = ["x", "src", "dst", "edge_type_6", "edge_type_8", "L0_gnn_W", "L0_gnn_Bv", "L1_gnn_W1",
             "L1_gnn_root1", "L1_gnn_b1", "L1_gnn_W2", "L1_gnn_root2", "L1_gnn_b2", "eye"]
    arrays, args = {}, []
    for name in names:
        a = _np.eye(P, dtype=_np.float32) if name == "eye" else _np.asarray(inputs[name])
        if name == "L0_gnn_W":
            a = a.transpose(2, 0, 1).reshape(CH, TYPES0 * CH)
        a = _np.ascontiguousarray(a)
        arrays[f"in_{name}_dram"] = a
        args.append(nc.dram_tensor(f"in_{name}_dram", a.shape, _mybir.dt.from_np(a.dtype), kind="ExternalInput").ap())
    args.append(nc.dram_tensor("out_0_dram", (NODES1, FEAT), _mybir.dt.float32, kind="ExternalOutput").ap())
    gnn_layers(nc, *args)
    r = _run(nc, [arrays], core_ids=[0])
    return r.results[0]["out_0_dram"]
```

```python
import concourse.bass as bass
from concourse import mybir
from contextlib import ExitStack

F32 = mybir.dt.float32
BF16 = mybir.dt.bfloat16
F16 = mybir.dt.float16
I32 = mybir.dt.int32
ALU = mybir.AluOpType
ACT = mybir.ActivationFunctionType
AX = mybir.AxisListType

P = 128
FEAT = 16
NODES1 = 50000
EDGES = 850000
CH = 8
NODES0 = NODES1 // CH
ROW0 = CH * FEAT
TYPES0 = 5
RELS = 8
EPS = 1e-5

WIN = 82
COLS = 6642
WINS = COLS // WIN
LAST_VALID = EDGES - (P - 1) * COLS
RING = 9
LEAD = WIN

TILES = -(-NODES0 // P)
TAIL = NODES0 - (TILES - 1) * P
NWIN = 56
NWINS = TILES * CH // NWIN
TPW = NWIN // CH
EARLY = 3

BC = 52
BLOCK = P * BC
BLOCKS = -(-EDGES // BLOCK)
PER_ROUND = 18
ROUNDS = -(-BLOCKS // PER_ROUND)
ROUND = PER_ROUND * BLOCK
EXTRA = BLOCKS * BLOCK - P * COLS
assert P * COLS >= EDGES > (P - 1) * COLS and WINS % RING == 0 and EXTRA > 0
assert PER_ROUND % 2 == 0 and (BLOCKS - 1) * BLOCK < EDGES
assert NWINS * NWIN == TILES * CH and NWINS == TPW == 7
assert NODES0 <= TPW * P * CH


class Steps:

    def __init__(self, eng, sem, done=0):
        self.eng, self.sem, self.n, self.done = eng, sem, 0, done

    def __call__(self, ins):
        ins.then_inc(self.sem, 1)
        self.n += 1

    def wait(self):
        self.eng.wait_ge(self.sem, self.done + self.n)


class Scope:

    def __init__(self, nc, ctx, prefix):
        self.nc, self.ctx, self.prefix = nc, ctx, prefix
        self.sems = []
        ctx.callback(self.clear)

    def clear(self):
        if self.sems:
            self.nc.clear_and_free_semaphores(self.sems)
            self.nc.all_engine_barrier()

    def sb(self, name, shape, dt=F32):
        return self.ctx.enter_context(self.nc.sbuf_tensor(f"{self.prefix}_{name}", shape, dt))

    def ps(self, name, shape):
        return self.ctx.enter_context(self.nc.psum_tensor(f"{self.prefix}_{name}", shape, F32))

    def sem(self, name):
        self.sems.append(self.nc.alloc_semaphore(name=f"{self.prefix}_{name}"))
        return self.sems[-1]

    def block(self):
        return self.ctx.enter_context(self.nc.Block())


def stage_edges(nc, env):
    with ExitStack() as ctx:
        s = Scope(nc, ctx, "ed")
        dst_f = s.sb("dst_f", [P, COLS])
        typ = s.sb("typ", [P, COLS], I32)
        typ6 = s.sb("typ6", [P, COLS], I32)
        tmp = s.sb("tmp", [P, COLS], I32)
        before = s.sb("before", [P, 1], I32)
        after = s.sb("after", [P, 1], I32)
        flag = s.sb("flag", [P, 2])
        wide = s.sb("wide", [P, 2, P])
        lead = s.sb("lead", [1, LEAD])
        pad_dst = s.sb("pad_dst", [1, EXTRA])
        pad_idx = s.sb("pad_idx", [1, EXTRA], I32)
        wide_ps = s.ps("wide_ps", [P, 2, P])
        padded, dst_in, type6_in, src_in, type8_in, small_in, dst_used = map(
            s.sem, ("padded", "dst_in", "type6_in", "src_in", "type8_in", "small_in", "dst_used"))
        type6_folded, stored_dst = s.sem("type6_folded"), s.sem("stored_dst")
        flags_done, stored, iotas, idx0_ready, wide_ready, turned, step = map(
            s.sem, ("flags_done", "stored", "iotas", "idx0_ready", "wide_ready", "turned", "step"))
        block = s.block()
        rows = P - 1
        split = rows * COLS

        def load(eng, to, frm, landed):
            eng.dma_start(to[0:rows, :], frm[0:split].rearrange("(p c) -> p c", p=rows)).then_inc(landed, 16)
            eng.dma_start(to[rows:P, 0:LAST_VALID],
                          frm[split:EDGES].rearrange("(p c) -> p c", p=1)).then_inc(landed, 16)

        @block.sync
        def _(sp):
            sp.wait_ge(padded, 3)
            load(sp, typ, env.dst, dst_in)
            load(sp, typ6, env.type6, type6_in)
            load(sp, env.idx1, env.src, src_in)
            sp.wait_ge(dst_used, 1)
            load(sp, typ, env.type8, type8_in)
            sp.wait_ge(idx0_ready, 1)
            sp.dma_start(env.idx0_d[0:P * COLS].rearrange("(p c) -> p c", c=COLS),
                         typ6[:, :]).then_inc(stored, 16)
            sp.wait_ge(stored, 64)

        @block.scalar
        def _(act):
            act.wait_ge(padded, 3)
            act.dma_start(before[1:P, :], env.dst[0:rows * COLS].rearrange("(p c) -> p c", c=COLS)
                          [:, COLS - 1:COLS]).then_inc(small_in, 16)
            act.dma_start(after[0:rows - 1, :], env.dst[COLS:split].rearrange("(p c) -> p c", c=COLS)
                          [:, 0:1]).then_inc(small_in, 16)
            act.dma_start(after[rows - 1:rows, :], env.dst[split:split + 1].rearrange("(p c) -> p c", c=1)
                          ).then_inc(small_in, 16)
            act.dma_start(env.ident[:, :], env.eye).then_inc(small_in, 16)
            act.dma_start(env.block_first[0:1, 1:BLOCKS], env.dst[1:1 + (BLOCKS - 1) * BLOCK]
                          .rearrange("(k e) -> e k", e=BLOCK)[BLOCK - 1:BLOCK, :]).then_inc(small_in, 16)
            act.wait_ge(flags_done, 1)
            act.dma_start(env.dst_d[LEAD:LEAD + P * COLS].rearrange("(p c) -> p c", c=COLS),
                          dst_f[:, :]).then_inc(stored_dst, 16)
            act.dma_start(env.dst_d[0:LEAD].rearrange("(a b) -> a b", a=1), lead[:, :]).then_inc(stored, 16)
            act.dma_start(env.dst_d[LEAD + P * COLS:LEAD + P * COLS + EXTRA].rearrange("(a b) -> a b", a=1),
                          pad_dst[:, :]).then_inc(stored, 16)
            act.dma_start(env.idx0_d[P * COLS:P * COLS + EXTRA].rearrange("(a b) -> a b", a=1),
                          pad_idx[:, :]).then_inc(stored, 16)
            act.wait_ge(small_in, 80)

        @block.gpsimd
        def _(pool):
            nc.gpsimd.iota(env.fix_base[:, :], pattern=[[0, 1]], base=-1, channel_multiplier=COLS).then_inc(iotas, 1)
            nc.gpsimd.iota(env.rel_id[:, :], pattern=[[1, RELS]], base=0, channel_multiplier=0,
                           allow_small_or_imprecise_dtypes=True).then_inc(iotas, 1)
            nc.gpsimd.iota(env.round_at[:, :], pattern=[[ROUND // P, ROUNDS + 1]], base=0, channel_multiplier=0,
                           allow_small_or_imprecise_dtypes=True).then_inc(iotas, 1)
            pool.wait_ge(type6_in, 32)
            nc.gpsimd.tensor_scalar(tmp[:, :], typ6[:, :], 0.0, float(TYPES0), ALU.is_equal, ALU.mult
                                    ).then_inc(type6_folded, 1)
            pool.wait_ge(type6_folded, 1)
            nc.gpsimd.tensor_tensor(tmp[:, :], typ6[:, :], tmp[:, :], ALU.add).then_inc(type6_folded, 1)
            pool.wait_ge(type6_folded, 2)

        @block.tensor
        def _(pe):
            pe.wait_ge(small_in, 80)
            pe.wait_ge(wide_ready, 2)
            for j in range(2):
                nc.tensor.transpose(wide_ps[:, j, :], wide[:, j, :], env.ident[:, :]).then_inc(turned, 1)

        @block.vector
        def _(dve):
            st = Steps(dve, step)
            nc.vector.memset(before[:, :], -1)
            nc.vector.memset(after[:, :], NODES1)
            nc.vector.memset(env.block_first[:, :], NODES1)
            nc.vector.memset(typ[:, LAST_VALID:], NODES1).then_inc(padded, 1)
            nc.vector.memset(typ6[:, LAST_VALID:], 0).then_inc(padded, 1)
            nc.vector.memset(env.idx1[:, LAST_VALID:], 0).then_inc(padded, 1)
            nc.vector.memset(lead[:, :], -1.0)
            nc.vector.memset(pad_dst[:, :], float(NODES1))
            nc.vector.memset(pad_idx[:, :], 0)
            dve.wait_ge(dst_in, 32)
            st(nc.vector.tensor_copy(dst_f[:, :], typ[:, :]))
            st.wait()
            nc.vector.memset(typ[:, LAST_VALID:], 0).then_inc(dst_used, 1)
            dve.sem_inc(flags_done, 1)
            st(nc.vector.tensor_tensor(env.keep[:, 1:COLS], dst_f[:, 1:COLS], dst_f[:, 0:COLS - 1], ALU.is_equal))
            st(nc.vector.memset(env.keep[:, 0:1], 1.0))
            dve.wait_ge(small_in, 80)
            st(nc.vector.memset(env.block_first[:, 0:1], 0))
            st(nc.vector.tensor_tensor(env.keep[:, COLS:COLS + 1], dst_f[:, COLS - 1:COLS], after[:, :], ALU.is_equal))
            st(nc.vector.tensor_tensor(flag[:, 0:1], dst_f[:, 0:1], before[:, :], ALU.is_equal))
            st(nc.vector.tensor_tensor(flag[:, 1:2], dst_f[:, 0:1], dst_f[:, COLS - 1:COLS], ALU.is_equal))
            st(nc.vector.tensor_copy(env.first_dst[:, :], dst_f[:, 0:1]))
            st.wait()
            st(nc.vector.memset(env.first_dst[0:1, :], -1.0))
            for j in range(2):
                nc.vector.tensor_copy(wide[:, j, :], flag[:, j:j + 1].to_broadcast([P, P])).then_inc(wide_ready, 1)
            dve.wait_ge(src_in, 32)
            dve.wait_ge(stored_dst, 16)
            st(nc.vector.tensor_scalar(dst_f[:, :], env.idx1[:, :], float(NODES0 - 1), float(TYPES0), ALU.min, ALU.mult))
            st.wait()
            dve.wait_ge(type6_folded, 2)
            nc.vector.scalar_tensor_tensor(typ6[:, :], dst_f[:, :], -1.0, tmp[:, :], ALU.add, ALU.add
                                           ).then_inc(idx0_ready, 1)
            dve.wait_ge(turned, 2)
            st(nc.vector.tensor_copy(env.cont_row[:, :], wide_ps[:, 0, :]))
            st(nc.vector.memset(env.pass_row[:, :], 0.0))
            st(nc.vector.memset(env.back_row[:, :], 0.0))
            st.wait()
            st(nc.vector.tensor_tensor(env.pass_row[:, 1:P], env.cont_row[:, 1:P], wide_ps[:, 1, 0:P - 1], ALU.mult))
            st(nc.vector.tensor_tensor(env.back_row[:, 0:P - 1], env.cont_row[:, 1:P], wide_ps[:, 1, 1:P], ALU.mult))
            dve.wait_ge(type8_in, 32)
            st(nc.vector.scalar_tensor_tensor(env.idx1[:, :], env.idx1[:, :], float(RELS), typ[:, :],
                                              ALU.mult, ALU.add))
            st.wait()
            dve.wait_ge(iotas, 3)
            st(nc.vector.tensor_scalar(env.round_at[:, :], env.round_at[:, :], float(P), None, ALU.mult))
            st.wait()


class Table:

    def __init__(self, nc, env, s, values, weights, table, root_out):
        self.nc, self.env, self.values, self.root_out = nc, env, values, root_out
        s = Scope(nc, s.ctx, s.prefix + "t")
        self.w, self.root, self.width = weights[0], weights[1], CH * RELS * FEAT
        self.mix = s.sb("mix", [P, self.width + ROW0])
        self.rep = s.sb("rep", [P, (RELS + 1) * FEAT])
        self.slot = s.sb("slot", [P, CH])
        self.xt = s.sb("xt", [P, 2, P])
        self.x_turned = s.sb("x_turned", [P, 2, P])
        self.out = s.sb("out", [P, 2, self.width + ROW0])
        self.turn_ps = [s.ps(f"turn_ps{b}", [P, 512]) for b in range(2)]
        self.mul_ps = [s.ps(f"mul_ps{b}", [P, 3, 512]) for b in range(2)]
        self.flat = table.rearrange("(n r) f -> n (r f)", n=NODES0)
        (self.weights_in, self.mix_ready, self.group_ready, self.staged, self.turned, self.back, self.multiplied,
         self.read_out, self.mix_step) = map(s.sem, (
             "weights_in", "mix_ready", "group_ready", "staged", "turned", "back", "multiplied", "read_out",
             "mix_step"))
        self.stored = [s.sem(f"stored{b}") for b in range(2)]

    def load_weights(self, eng):
        for i in range(CH):
            eng.dma_start(self.rep[i * FEAT:(i + 1) * FEAT, 0:RELS * FEAT].rearrange("b (r c) -> b r c", c=FEAT),
                          self.w.rearrange("r b c -> b r c")).then_inc(self.weights_in, 16)
            eng.dma_start(self.rep[i * FEAT:(i + 1) * FEAT, RELS * FEAT:], self.root).then_inc(self.weights_in, 16)

    def make_mix(self, dve):
        nc, st = self.nc, Steps(dve, self.mix_step)
        st(nc.vector.tensor_reduce(self.slot[:, :], self.env.ident[:, :].rearrange("p (o b) -> p o b", b=FEAT),
                                   AX.X, ALU.add))
        dve.wait_ge(self.weights_in, 16 * 2 * CH)
        st.wait()
        for o in range(CH):
            st(nc.vector.tensor_scalar(self.mix[:, o * P:(o + 1) * P], self.rep[:, 0:P],
                                       self.slot[:, o:o + 1], None, ALU.mult))
            at = self.width + o * FEAT
            st(nc.vector.tensor_scalar(self.mix[:, at:at + FEAT], self.rep[:, P:P + FEAT],
                                       self.slot[:, o:o + 1], None, ALU.mult))
        st.wait()
        dve.sem_inc(self.mix_ready, 1)

    @staticmethod
    def previous(g, j):
        n = g * TPW + j + 1
        back = {0: 1, 1: 3}.get(j, 2)
        return None if isinstance(g, int) and n - back <= 0 else n - back

    @staticmethod
    def uses(g, j):
        return g * (TPW // 2 + 1 - j % 2) + j // 2

    def each_group(self, eng, body):
        body(0)
        with eng.Fori(1, TPW - 1) as g:
            body(g)
        body(TPW - 1)

    def pe(self, pe):
        nc = self.nc
        pe.wait_ge(self.mix_ready, 1)

        def turn(g, j):
            pe.wait_ge(self.staged, g * TPW + j + 1)
            nc.tensor.transpose(self.turn_ps[j % 2][:, 0:P], self.xt[:, j % 2, :],
                                self.env.ident[:, :]).then_inc(self.turned, 1)

        def group(g):
            turn(g, 0)
            for j in range(TPW):
                if j + 1 < TPW:
                    turn(g, j + 1)
                before = self.previous(g, j)
                if before is not None:
                    pe.wait_ge(self.read_out, before)
                pe.wait_ge(self.back, g * TPW + j + 1)
                for k, (a, z) in enumerate(((0, 512), (512, 1024), (1024, 1152))):
                    last = nc.tensor.matmul(self.mul_ps[j % 2][:, k, 0:z - a], self.x_turned[:, j % 2, :],
                                            self.mix[:, a:z], start=True, stop=True)
                last.then_inc(self.multiplied, 1)
        self.each_group(pe, group)

    def act(self, act):
        nc = self.nc

        def stage(g, j):
            nc.scalar.copy(self.xt[:, j % 2, :], self.values[:, self.tile(g, j), :]).then_inc(self.staged, 1)

        def turn_back(g, j):
            act.wait_ge(self.turned, g * TPW + j + 1)
            before = self.previous(g, j)
            if before is not None:
                act.wait_ge(self.multiplied, before)
            nc.scalar.copy(self.x_turned[:, j % 2, :], self.turn_ps[j % 2][:, 0:P]).then_inc(self.back, 1)

        def group(g):
            act.wait_ge(self.group_ready, g + 1)
            stage(g, 0)
            stage(g, 1)
            turn_back(g, 0)
            for j in range(TPW):
                if j + 1 < TPW:
                    turn_back(g, j + 1)
                if j + 2 < TPW:
                    stage(g, j + 2)
                act.wait_ge(self.multiplied, g * TPW + j + 1)
                if not (isinstance(g, int) and self.uses(g, j) == 0):
                    act.wait_ge(self.stored[j % 2], self.uses(g, j) * 32)
                nc.scalar.copy(self.out[:, j % 2, 0:512], self.mul_ps[j % 2][:, 0, :])
                nc.scalar.copy(self.out[:, j % 2, 512:1024], self.mul_ps[j % 2][:, 1, :])
                nc.scalar.copy(self.out[:, j % 2, 1024:], self.mul_ps[j % 2][:, 2, 0:ROW0]
                               ).then_inc(self.read_out, 1)
        self.each_group(act, group)

    @staticmethod
    def tile(g, j):
        return g * TPW + j if isinstance(g, int) else bass.ds(g * TPW + j, 1)

    def sp(self, sp):
        def group(g):
            for j in range(TPW):
                t = g * TPW + j
                end = isinstance(g, int) and t == TILES - 1
                rows = TAIL if end else P
                at = slice(t * P, t * P + rows) if isinstance(g, int) else bass.ds(t * P, P)
                sp.wait_ge(self.read_out, t + 1)
                sp.dma_start(self.flat[at, :], self.out[0:rows, j % 2, 0:self.width]
                             ).then_inc(self.stored[j % 2], 16)
                sp.dma_start(self.root_out[at if not end else slice(t * P, t * P + P), :],
                             self.out[:, j % 2, self.width:]).then_inc(self.stored[j % 2], 16)
        self.each_group(sp, group)
        for b in range(2):
            sp.wait_ge(self.stored[b], 32 * self.uses(TPW, b))


def stage_first(nc, env):
    slots = TILES * CH
    width = TYPES0 * ROW0
    with ExitStack() as ctx:
        s = Scope(nc, ctx, "fi")
        x_sb = s.sb("x_sb", [P, TILES, ROW0])
        mix = s.sb("mix", [P, width])
        rep = s.sb("rep", [P, TYPES0 * CH])
        lane = s.sb("lane", [P, FEAT])
        bias_in = s.sb("bias_in", [P, TYPES0 * CH])
        bias_w = s.sb("bias_w", [P, width])
        xt = s.sb("xt", [P, P])
        x_turned = s.sb("x_turned", [P, P])
        out = s.sb("out", [P, 2, width])
        node_i = s.sb("node_i", [P, slots], I32)
        tile_base = s.sb("tile_base", [P, TILES])
        in_tile = s.sb("in_tile", [P, CH, P], F16)
        first_t = s.sb("first_t", [P, TILES])
        samples = s.sb("samples", [P, WINS])
        shifted = s.sb("shifted", [P, WINS])
        step_f = s.sb("step_f", [P, WINS])
        step_lo = s.sb("step_lo", [P, WINS], I32)
        pick = s.sb("pick", [P, 2, WINS + 1], BF16)
        reached = s.sb("reached", [P, 2, CH, P], BF16)
        below = s.sb("below", [P, CH, WINS])
        win_no = s.sb("win_no", [P, slots])
        got = s.sb("got", [P, EARLY, NWIN, WIN])
        cmp = s.sb("cmp", [P, NWIN, WIN])
        n_le = s.sb("n_le", [P, NWIN])
        n_eq = s.sb("n_eq", [P, NWIN])
        idx_ready, find_step, cleared, ends_out, ends_back = map(
            s.sem, ("idx_ready", "find_step", "cleared", "ends_out", "ends_back"))
        landed = [s.sem(f"landed{w}") for w in range(EARLY)]
        previous, uses = Table.previous, Table.uses
        turn_ps = s.ps("turn_ps", [P, 512])
        mul_ps = s.ps("mul_ps", [P, 2, 512])
        picked = [s.ps(f"picked{b}", [P, 2, 4, P]) for b in range(2)]
        loaded, samples_in, zeroed, mix_ready, staged, turned, back, multiplied, read_out = map(
            s.sem, ("loaded", "samples_in", "zeroed", "mix_ready", "staged", "turned", "back", "multiplied",
                    "read_out"))
        iotas, pick_ready, reached_ready, picked_done, picked_used, step, tile_step = map(
            s.sem, ("iotas", "pick_ready", "reached_ready", "picked_done", "picked_used", "step", "tile_step"))
        stored = [s.sem(f"stored{b}") for b in range(2)]
        block = s.block()
        flat = env.table0.rearrange("(n r) f -> n (r f)", n=NODES0)

        def each_group(eng, body):
            body(0)
            with eng.Fori(1, NWINS - 1) as g:
                body(g)
            body(NWINS - 1)

        @block.sync
        def _(sp):
            src = env.dst_rows[1:1 + P * WINS, 0:1].rearrange("(p j) c -> p (j c)", j=WINS)
            sp.wait_ge(zeroed, 2)
            sp.dma_start(samples[:, :], src).then_inc(samples_in, 16)
            sp.dma_start(shifted[1:P, :], src[0:P - 1, :]).then_inc(samples_in, 16)
            load_x(sp, env, x_sb, loaded)

            def group(g):
                for j in range(TPW):
                    tile = g * TPW + j
                    end = isinstance(g, int) and tile == TILES - 1
                    rows = TAIL if end else P
                    at = slice(tile * P, tile * P + rows) if isinstance(g, int) else bass.ds(tile * P, P)
                    sp.wait_ge(read_out, tile + 1)
                    sp.dma_start(flat[at, :], out[0:rows, j % 2, :]).then_inc(stored[j % 2], 16)
            each_group(sp, group)
            sp.wait_ge(find_step, FIND_STEPS)
            for to, frm in ((env.end_d, env.end_idx), (env.some_d, env.has_edge)):
                sp.dma_start(to.rearrange("(t n o) -> n t o", n=P, o=CH),
                             frm[:, 0:NWIN].rearrange("n (t o) -> n t o", o=CH)).then_inc(ends_out, 16)
            sp.wait_ge(ends_out, 32)
            sp.wait_ge(cleared, 2)
            for to, frm in ((env.end0, env.end_d), (env.some0, env.some_d)):
                sp.dma_start(to[:, 0:TILES - 1], frm[0:(TILES - 1) * P].rearrange("(t n) -> n t", n=P)
                             ).then_inc(ends_back, 16)
                sp.dma_start(to[0:TAIL, TILES - 1:TILES],
                             frm[(TILES - 1) * P:NODES0].rearrange("(n t) -> n t", t=1)).then_inc(ends_back, 16)
            sp.wait_ge(ends_back, 64)
            for b in range(2):
                sp.wait_ge(stored[b], 16 * uses(NWINS, b))

        @block.gpsimd
        def _(pool):
            nc.gpsimd.iota(node_i[:, :], pattern=[[P * CH, TILES], [1, CH]], base=0,
                           channel_multiplier=CH).then_inc(iotas, 1)
            nc.gpsimd.iota(tile_base[:, :], pattern=[[P * CH, TILES]], base=0, channel_multiplier=0,
                           allow_small_or_imprecise_dtypes=True).then_inc(iotas, 1)
            nc.gpsimd.iota(in_tile[:, :, :], pattern=[[1, CH], [CH, P]], base=0, channel_multiplier=0,
                           allow_small_or_imprecise_dtypes=True).then_inc(iotas, 1)
            for w in range(EARLY):
                pool.wait_ge(idx_ready, w + 1)
                fetch(pool, got[:, w], env.dst_rows, env.win_idx[:, w * NWIN:(w + 1) * NWIN], NWIN, landed[w])

        @block.scalar
        def _(act):
            for i in range(CH):
                act.dma_start(rep[i * FEAT:(i + 1) * FEAT, :],
                              env.w0[i:i + 1, :].to_broadcast([FEAT, TYPES0 * CH])).then_inc(loaded, 16)
            act.dma_start(bias_in[:, :], env.b0.rearrange("(a t) o -> a (t o)", a=1)
                          .to_broadcast([P, TYPES0 * CH])).then_inc(loaded, 16)
            act.wait_ge(loaded, 16 * (CH + 1 + 2))

            def tile(t, n):
                if not isinstance(t, int):
                    act.wait_ge(turned, n - 1)
                at = t if isinstance(t, int) else bass.ds(t, 1)
                nc.scalar.copy(xt[:, :], x_sb[:, at, :]).then_inc(staged, 1)
                act.wait_ge(turned, n)
                if not isinstance(t, int):
                    act.wait_ge(multiplied, n - 1)
                nc.scalar.copy(x_turned[:, :], turn_ps[:, 0:P]).then_inc(back, 1)

            tile(0, 1)
            with act.Fori(1, TILES) as t:
                tile(t, t + 1)

        @block.tensor
        def _(pe):
            def turn(n):
                pe.wait_ge(staged, n)
                nc.tensor.transpose(turn_ps[:, 0:P], xt[:, :], env.ident[:, :]).then_inc(turned, 1)

            def pick_samples(g, j):
                pe.wait_ge(reached_ready, g * TPW + j + 1)
                before = previous(g, j)
                if before is not None:
                    pe.wait_ge(picked_used, before)
                b = j % 2
                for o in range(CH):
                    for part in range(2):
                        last = nc.tensor.matmul(picked[b][:, o // 4, o % 4, 0:WINS + 1], reached[:, b, o, :],
                                                pick[:, part, :], start=part == 0, stop=part == 1)
                last.then_inc(picked_done, 1)

            def multiply(g, j):
                n = g * TPW + j + 1
                pe.wait_ge(back, n)
                if not (isinstance(g, int) and n == 1):
                    pe.wait_ge(read_out, n - 1)
                for k, (a, z) in enumerate(((0, 512), (512, width))):
                    last = nc.tensor.matmul(mul_ps[:, k, 0:z - a], x_turned[:, :], mix[:, a:z],
                                            start=True, stop=True)
                last.then_inc(multiplied, 1)

            def group(g):
                for j in range(TPW):
                    turn(g * TPW + j + 1)
                    pick_samples(g, j)
                    multiply(g, j)

            pe.wait_ge(pick_ready, 1)
            pe.wait_ge(mix_ready, 1)
            each_group(pe, group)

        @block.vector
        def _(dve):
            st = Steps(dve, step)
            nc.vector.memset(x_sb[:, TILES - 1, :], 0.0).then_inc(zeroed, 1)
            nc.vector.memset(shifted[0:1, :], 0.0).then_inc(zeroed, 1)
            st(nc.vector.tensor_reduce(lane[:, :], env.ident[:, :].rearrange("p (o b) -> p b o", b=FEAT),
                                       AX.X, ALU.add))
            dve.wait_ge(iotas, 3)
            st(nc.vector.tensor_copy(env.node[:, :], node_i[:, :]))
            nc.vector.memset(env.end0[:, :], 0).then_inc(cleared, 1)
            nc.vector.memset(env.some0[:, :], 0.0).then_inc(cleared, 1)
            st(nc.vector.tensor_scalar(first_t[:, :], tile_base[:, :], -1.0, env.first_dst[:, :], ALU.mult, ALU.add))
            dve.wait_ge(samples_in, 32)
            st(nc.vector.tensor_tensor(step_f[:, :], samples[:, :], shifted[:, :], ALU.subtract))
            st.wait()
            st(nc.vector.tensor_copy(step_lo[:, :], step_f[:, :]))
            st.wait()
            st(nc.vector.tensor_scalar(step_lo[:, :], step_lo[:, :], 255, None, ALU.bitwise_and))
            st.wait()
            st(nc.vector.tensor_copy(pick[:, 0, 0:WINS], step_lo[:, :]))
            st(nc.vector.tensor_tensor(pick[:, 1, 0:WINS], step_f[:, :], step_lo[:, :], ALU.subtract))
            st(nc.vector.memset(pick[:, 0, WINS:WINS + 1], 1.0))
            st(nc.vector.memset(pick[:, 1, WINS:WINS + 1], 0.0))
            st.wait()
            dve.sem_inc(pick_ready, 1)

            dve.wait_ge(loaded, 16 * (CH + 1 + 2))
            st(nc.vector.tensor_tensor(mix[:, :].rearrange("p (k b) -> p k b", b=FEAT),
                                       rep[:, :].unsqueeze(2).to_broadcast([P, TYPES0 * CH, FEAT]),
                                       lane[:, :].unsqueeze(1).to_broadcast([P, TYPES0 * CH, FEAT]), ALU.mult))
            st(nc.vector.tensor_copy(bias_w[:, :].rearrange("p (k b) -> p k b", b=FEAT),
                                     bias_in[:, :].unsqueeze(2).to_broadcast([P, TYPES0 * CH, FEAT])))
            st.wait()
            dve.sem_inc(mix_ready, 1)

            def reach(g, j):
                nc.vector.tensor_scalar(reached[:, j % 2, :, :], in_tile[:, :, :],
                                        first_t[:, bass.ds(g * TPW + j, 1)], None,
                                        ALU.is_ge).then_inc(reached_ready, 1)

            per = 3 * TPW + 4

            def count(g, j):
                tile, b = g * TPW + j, j % 2
                dve.wait_ge(picked_done, tile + 1)
                st2 = Steps(dve, tile_step, g * per + 3 * j)
                at = bass.ds(tile * CH, CH)
                st2(nc.vector.tensor_tensor(
                    below[:, :, :].rearrange("n (a c) j -> n a c j", a=2), picked[b][:, :, :, 0:WINS],
                    env.node[:, at].rearrange("n (a c) -> n a c", a=2).unsqueeze(3).to_broadcast([P, 2, 4, WINS]),
                    ALU.is_le))
                st2(nc.vector.tensor_copy(env.win_row[:, at].rearrange("n (a c) -> n a c", a=2),
                                          picked[b][:, :, :, WINS]))
                st2.wait()
                dve.sem_inc(picked_used, 1)
                st2(nc.vector.tensor_reduce(win_no[:, at], below[:, :, :], AX.X, ALU.add))
                st2.wait()

            def messages(g, j):
                b = j % 2
                dve.wait_ge(multiplied, g * TPW + j + 1)
                if not (isinstance(g, int) and uses(g, j) == 0):
                    dve.wait_ge(stored[b], uses(g, j) * 16)
                nc.vector.tensor_tensor(out[:, b, 0:512], mul_ps[:, 0, :], bias_w[:, 0:512], ALU.add)
                nc.vector.tensor_tensor(out[:, b, 512:width], mul_ps[:, 1, 0:width - 512], bias_w[:, 512:width],
                                        ALU.add).then_inc(read_out, 1)

            def group(g):
                reach(g, 0)
                reach(g, 1)
                for j in range(TPW):
                    count(g, j)
                    if j + 2 < TPW:
                        reach(g, j + 2)
                    messages(g, j)
                st3 = Steps(dve, tile_step, g * per + 3 * TPW)
                at = bass.ds(g * NWIN, NWIN)
                st3(nc.vector.tensor_scalar(win_no[:, at], win_no[:, at], -1.0, 0.0, ALU.add, ALU.max))
                st3(nc.vector.tensor_scalar(env.win_row[:, at], env.win_row[:, at], -1.0, float(WINS),
                                            ALU.add, ALU.mult))
                st3.wait()
                st3(nc.vector.tensor_tensor(env.win_row[:, at], env.win_row[:, at], win_no[:, at], ALU.add))
                st3.wait()
                st3(nc.vector.tensor_scalar(env.win_idx[:, at], env.win_row[:, at], float(LEAD // WIN), None, ALU.add))
                st3.wait()
                dve.sem_inc(idx_ready, 1)
                assert 3 * TPW + st3.n == per
            each_group(dve, group)
            for w in range(EARLY):
                dve.wait_ge(landed[w], 16 * NWIN)
                find_last_edges(nc, dve, env, got[:, w], cmp, n_le, n_eq, find_step, w * FIND_STEPS,
                                slice(w * NWIN, (w + 1) * NWIN))


def load_x(eng, env, x_sb, landed):
    eng.dma_start(x_sb[:, 0:TILES - 1, :], env.x[0:(TILES - 1) * P * CH, :]
                  .rearrange("(t n o) b -> n t (o b)", n=P, o=CH)).then_inc(landed, 16)
    eng.dma_start(x_sb[0:TAIL, TILES - 1, :], env.x[(TILES - 1) * P * CH:NODES1, :]
                  .rearrange("(n o) b -> n (o b)", o=CH)).then_inc(landed, 16)


def find_last_edges(nc, dve, env, got, cmp, n_le, n_eq, step, done, at):
    st = Steps(dve, step, done)
    want = env.node[:, at].unsqueeze(2).to_broadcast([P, NWIN, WIN])
    for op, to in ((ALU.is_le, n_le), (ALU.is_equal, n_eq)):
        st(nc.vector.tensor_tensor(cmp[:, :, :], got, want, op))
        st.wait()
        st(nc.vector.tensor_reduce(to[:, :], cmp[:, :, :], AX.X, ALU.add))
        st.wait()
    st(nc.vector.tensor_scalar(env.has_edge[:, at], n_eq[:, :], 1.0, None, ALU.min))
    st(nc.vector.scalar_tensor_tensor(n_le[:, :], env.win_row[:, at], float(WIN), n_le[:, :], ALU.mult, ALU.add))
    st.wait()
    st(nc.vector.scalar_tensor_tensor(env.end_idx[:, at], n_le[:, :], -1.0, env.has_edge[:, at], ALU.add, ALU.mult))
    st.wait()
    assert st.n == FIND_STEPS


FIND_STEPS = 7


def fetch(pool, out, table, idx, count, landed):
    for j in range(count):
        pool.indirect_dma_start(out=out[:, j, :], out_offset=None, in_=table,
                                in_offset=bass.IndirectOffsetOnAxis(ap=idx[:, j:j + 1], axis=0)).then_inc(landed, 16)


def stage_sum0(nc, env):
    with ExitStack() as ctx:
        s = Scope(nc, ctx, "s0")
        rows = s.sb("rows", [P, 2, BC, ROW0])
        idx = s.sb("idx", [P, 2, BC], I32)
        dst = s.sb("dst", [P, 2, BC + 1])
        keep = s.sb("keep", [P, BC])
        first = s.sb("first", [P, BC])
        flag = s.sb("flag", [P, 2])
        wide = s.sb("wide", [P, 2, P])
        cont = s.sb("cont", [P, P])
        through = s.sb("through", [P, P])
        passed = s.sb("passed", [P, P])
        last = s.sb("last", [P, P + 1])
        carry_in = s.sb("carry_in", [P, P])
        carry_row = s.sb("carry_row", [P, P])
        carry = s.sb("carry", [P, P])
        zeros = s.sb("zeros", [P, BLOCK * ROW0 // P // 4])
        got = s.sb("got", [P, TILES, ROW0])
        row_f = s.sb("row_f", [P, TILES])
        row_idx = s.sb("row_idx", [P, TILES], I32)
        mine = s.sb("mine", [P, TILES])
        wide_ps = s.ps("wide_ps", [P, 2, P])
        last_ps = s.ps("last_ps", [P, P])
        carry_ps = s.ps("carry_ps", [P, P])
        wide_ready, wide_turned, scanned, last_turned, carry_ready, carry_back, summed, claimed = map(
            s.sem, ("wide_ready", "wide_turned", "scanned", "last_turned", "carry_ready", "carry_back",
                    "summed", "claimed"))
        start, step, stored, free, rows_known, round_stored, fetched, round_added, round_step = map(
            s.sem, ("start", "step", "stored", "free", "rows_known", "round_stored", "fetched", "round_added",
                    "round_step"))
        table_free, zeroed = s.sem("table_free"), s.sem("zeroed")
        loaded = [s.sem(f"loaded{b}") for b in range(2)]
        landed = [s.sem(f"landed{b}") for b in range(2)]
        block = s.block()

        def each_round(eng, before, body, after):
            def load(k):
                return eng.value_load(env.block_first[0:1, bass.ds(k, 1)])

            with eng.Fori(0, ROUNDS) as r:
                with eng.If(load(r * PER_ROUND) < NODES0):
                    before(r)
                    with eng.Fori(0, PER_ROUND // 2) as i:
                        for b in range(2):
                            k = r * PER_ROUND + i * 2 + b
                            with eng.If(load(k) < NODES0):
                                body(b, r * (PER_ROUND // 2) + i, k, i * 2 + b)
                    after(r)

        nothing = lambda r: None

        @block.sync
        def _(sp):
            def body(b, i, k, kr):
                sp.wait_ge(free, k + 1)
                at = k * BLOCK
                sp.dma_start(idx[:, b, :], env.idx0_d[bass.ds(at, BLOCK)].rearrange("(p c) -> p c", c=BC)
                             ).then_inc(loaded[b], 16)
                sp.dma_start(dst[:, b, 1:BC + 1], env.dst_d[bass.ds(at + LEAD, BLOCK)]
                             .rearrange("(p c) -> p c", c=BC)).then_inc(loaded[b], 16)
                sp.dma_start(dst[:, b, 0:1], env.dst_d[bass.ds(at + LEAD - 1, BLOCK)]
                             .rearrange("(p c) -> p c", c=BC)[:, 0:1]).then_inc(loaded[b], 16)
            each_round(sp, nothing, body, nothing)

        @block.gpsimd
        def _(pool):
            def body(b, i, k, kr):
                pool.wait_ge(loaded[b], (i + 1) * 48)
                pool.sem_inc(claimed, 1)
                fetch(pool, rows[:, b], env.table0, idx[:, b], BC, landed[b])

            def after(r):
                pool.wait_ge(rows_known, r + 1)
                pool.wait_ge(round_stored, r + 1)
                pool.sem_inc(claimed, 1)
                fetch(pool, got, env.sums0, row_idx, TILES, fetched)
                pool.wait_ge(round_added, r + 1)
                pool.sem_inc(claimed, 1)
            each_round(pool, nothing, body, after)

        @block.tensor
        def _(pe):
            def body(b, i, k, kr):
                pe.wait_ge(wide_ready, k + 1)
                for j in range(2):
                    mm = nc.tensor.transpose(wide_ps[:, j, 0:P], wide[:, j, :], env.ident[0:P, 0:P])
                mm.then_inc(wide_turned, 1)
                pe.wait_ge(scanned, k + 1)
                nc.tensor.transpose(last_ps[:, 0:P], rows[:, b, BC - 1, :], env.ident[0:P, 0:P]
                                    ).then_inc(last_turned, 1)
                pe.wait_ge(carry_ready, k + 1)
                nc.tensor.transpose(carry_ps[0:P, :], carry_row[:, :], env.ident[:, :]).then_inc(carry_back, 1)
            each_round(pe, nothing, body, nothing)

        @block.scalar
        def _(act):
            act.wait_ge(start, 2)
            act.sem_inc(free, 2)

            def body(b, i, k, kr):
                act.wait_ge(summed, k + 1)
                act.dma_start(env.sums0[bass.ds(kr * BLOCK, BLOCK), :].rearrange("(p c) f -> p c f", c=BC),
                              rows[:, b, :, :]).then_inc(stored, 16)
                act.wait_ge(stored, (k + 1) * 16)
                act.sem_inc(free, 1)

            def zero_rest(r):
                part = BLOCK // 4
                with act.Fori(0, PER_ROUND) as kr:
                    first_dst = act.value_load(env.block_first[0:1, bass.ds(r * PER_ROUND + kr, 1)])
                    with act.If(first_dst >= NODES0):
                        for q in range(4):
                            act.dma_start(env.sums0[bass.ds(kr * BLOCK + q * part, part), :]
                                          .rearrange("e f -> (e f)").rearrange("(p c) -> p c", p=P),
                                          zeros[:, :]).then_inc(zeroed, 16)
                    with act.If(first_dst < NODES0):
                        act.sem_inc(zeroed, 64)

            def after(r):
                act.wait_ge(zeroed, (r + 1) * (64 * PER_ROUND))
                act.sem_inc(round_stored, 1)
                act.wait_ge(round_added, r + 1)
                act.sem_inc(table_free, 1)
            each_round(act, zero_rest, body, after)

        @block.vector
        def _(dve):
            nc.vector.memset(last[:, 0:1], 0.0)
            nc.vector.memset(env.layer0[:, :, :], 0.0).then_inc(start, 1)
            nc.vector.memset(zeros[:, :], 0.0).then_inc(start, 1)
            dve.wait_ge(start, 2)
            per_round = 6
            per = 14

            def before(r):
                st = Steps(dve, round_step, r * per_round)
                at, to = env.round_at[:, bass.ds(r, 1)], env.round_at[:, bass.ds(r + 1, 1)]
                st(nc.vector.tensor_scalar(row_f[:, :], env.end0[:, :], at, 0.0, ALU.subtract, ALU.max))
                st(nc.vector.scalar_tensor_tensor(mine[:, :], env.end0[:, :], at, env.some0[:, :], ALU.is_ge, ALU.mult))
                st.wait()
                st(nc.vector.tensor_scalar(row_idx[:, :], row_f[:, :], float(ROUND - 1), None, ALU.min))
                st(nc.vector.scalar_tensor_tensor(mine[:, :], env.end0[:, :], to, mine[:, :], ALU.is_lt, ALU.mult))
                st.wait()
                dve.sem_inc(rows_known, 1)

            def after(r):
                st = Steps(dve, round_step, r * per_round + 4)
                dve.wait_ge(fetched, (r + 1) * (16 * TILES))
                st(nc.vector.tensor_tensor(got[:, :, :], got[:, :, :],
                                           mine[:, :].unsqueeze(2).to_broadcast([P, TILES, ROW0]), ALU.mult))
                st.wait()
                st(nc.vector.tensor_tensor(env.layer0[:, :, :], env.layer0[:, :, :], got[:, :, :], ALU.add))
                st.wait()
                dve.sem_inc(round_added, 1)

            def body(b, i, k, kr):
                st = Steps(dve, step, k * per)
                dve.wait_ge(loaded[b], (i + 1) * 48)
                st(nc.vector.tensor_tensor(keep[:, :], dst[:, b, 1:BC + 1], dst[:, b, 0:BC], ALU.is_equal))
                st(nc.vector.tensor_scalar(first[:, :], dst[:, b, 1:BC + 1], dst[:, b, 1:2], None, ALU.is_equal))
                st(nc.vector.tensor_tensor(flag[:, 1:2], dst[:, b, 1:2], dst[:, b, BC:BC + 1], ALU.is_equal))
                st.wait()
                st(nc.vector.tensor_copy(wide[:, 0, :], keep[:, 0:1].to_broadcast([P, P])))
                st(nc.vector.tensor_copy(wide[:, 1, :], flag[:, 1:2].to_broadcast([P, P])))
                st.wait()
                dve.sem_inc(wide_ready, 1)
                dve.wait_ge(wide_turned, k + 1)
                st(nc.vector.tensor_copy(cont[:, :], wide_ps[:, 0, 0:P]))
                st(nc.vector.tensor_copy(through[:, :], wide_ps[:, 1, 0:P]))
                st(nc.vector.memset(passed[:, 0:1], 0.0))
                st.wait()
                st(nc.vector.tensor_tensor(passed[:, 1:P], cont[:, 1:P], through[:, 0:P - 1], ALU.mult))
                dve.wait_ge(landed[b], (i + 1) * (16 * BC))
                for f in range(ROW0):
                    one = nc.vector.tensor_tensor_scan(rows[:, b, :, f], keep[:, :], rows[:, b, :, f], 0.0,
                                                       ALU.mult, ALU.add)
                one.then_inc(scanned, 1)
                dve.wait_ge(last_turned, k + 1)
                st(nc.vector.tensor_copy(last[:, 1:P + 1], last_ps[:, 0:P]))
                st.wait()
                st(nc.vector.tensor_tensor(carry_in[:, :], cont[:, :], last[:, 0:P], ALU.mult))
                st.wait()
                nc.vector.tensor_tensor_scan(carry_row[:, :], passed[:, :], carry_in[:, :], 0.0,
                                             ALU.mult, ALU.add).then_inc(carry_ready, 1)
                dve.wait_ge(carry_ready, k + 1)
                st(nc.vector.scalar_tensor_tensor(last[:, 0:1], carry_row[:, P - 1:P], through[:, P - 1:P],
                                                  last[:, P:P + 1], ALU.mult, ALU.add))
                dve.wait_ge(carry_back, k + 1)
                st(nc.vector.tensor_copy(carry[:, :], carry_ps[0:P, :]))
                st.wait()
                for c in range(BC):
                    one = nc.vector.scalar_tensor_tensor(rows[:, b, c, :], carry[:, :], first[:, c:c + 1],
                                                         rows[:, b, c, :], ALU.mult, ALU.add)
                st(one)
                st.wait()
                dve.sem_inc(summed, 1)
                assert st.n == 14, st.n
            each_round(dve, before, body, after)


def layer_norm(nc, st, x, sq, mean, var, slots, act_root):
    stat = lambda t: t.unsqueeze(2).to_broadcast([P, slots, FEAT])
    st(nc.vector.tensor_reduce(mean, x, AX.X, ALU.add))
    st.wait()
    st(nc.vector.tensor_scalar(mean, mean, 1.0 / FEAT, None, ALU.mult))
    st.wait()
    st(nc.vector.tensor_tensor(x, x, stat(mean), ALU.subtract))
    st.wait()
    st(nc.vector.tensor_tensor(sq, x, x, ALU.mult))
    st.wait()
    st(nc.vector.tensor_reduce(var, sq, AX.X, ALU.add))
    st.wait()
    st(nc.vector.tensor_scalar(var, var, 1.0 / FEAT, EPS, ALU.mult, ALU.add))
    st.wait()
    act_root()
    st(nc.vector.reciprocal(var, var))
    st.wait()
    st(nc.vector.tensor_tensor(x, x, stat(var), ALU.mult))
    st.wait()


def stage_x1(nc, env, weights, table, root_out, x1_d):
    slots = TILES * CH
    with ExitStack() as ctx:
        s = Scope(nc, ctx, "x1")
        x_sb = s.sb("x_sb", [P, TILES, ROW0])
        mean = s.sb("mean", [P, slots])
        var = s.sb("var", [P, slots])
        idx = s.sb("idx", [P, 2, NWIN], I32)
        got = s.sb("got", [P, 2, NWIN, WIN])
        cmp = s.sb("cmp", [P, NWIN, WIN])
        n_le = s.sb("n_le", [P, NWIN])
        n_eq = s.sb("n_eq", [P, NWIN])
        loaded, zeroed, step, var_ready, rooted, idx_ready, claimed, find_step, x1_ready, x1_stored = map(
            s.sem, ("loaded", "zeroed", "step", "var_ready", "rooted", "idx_ready", "claimed", "find_step",
                    "x1_ready", "x1_stored"))
        landed = [s.sem(f"landed{b}") for b in range(2)]
        late = NWINS - EARLY
        assert late % 2 == 0
        tb = Table(nc, env, s, x_sb, weights, table, root_out)
        block = s.block()

        @block.sync
        def _(sp):
            sp.wait_ge(zeroed, 1)
            load_x(sp, env, x_sb, loaded)
            tb.load_weights(sp)
            sp.wait_ge(x1_ready, 1)
            sp.dma_start(x1_d.rearrange("(t n) f -> n t f", n=P), x_sb[:, :, :]).then_inc(x1_stored, 16)
            tb.sp(sp)
            sp.wait_ge(x1_stored, 16)

        @block.gpsimd
        def _(pool):
            def window(b, n):
                pool.wait_ge(idx_ready, n)
                pool.sem_inc(claimed, 1)
                fetch(pool, got[:, b], env.dst_rows, idx[:, b], NWIN, landed[b])
            with pool.Fori(0, late // 2) as i:
                for b in range(2):
                    window(b, i * 2 + b + 1)

        @block.scalar
        def _(act):
            act.wait_ge(var_ready, 1)
            nc.scalar.activation(var[:, :], var[:, :], ACT.Sqrt).then_inc(rooted, 1)
            tb.act(act)

        @block.tensor
        def _(pe):
            tb.pe(pe)

        @block.vector
        def _(dve):
            st = Steps(dve, step)
            nc.vector.memset(x_sb[:, TILES - 1, :], 0.0).then_inc(zeroed, 1)
            for b in range(2):
                nc.vector.tensor_copy(idx[:, b, :], env.win_idx[:, (EARLY + b) * NWIN:(EARLY + b + 1) * NWIN]
                                      ).then_inc(idx_ready, 1)
            dve.wait_ge(loaded, 32)
            st(nc.vector.tensor_tensor(x_sb[:, :, :], x_sb[:, :, :], env.layer0[:, :, :], ALU.add))
            st.wait()

            def root():
                dve.sem_inc(var_ready, 1)
                dve.wait_ge(rooted, 1)
            layer_norm(nc, st, x_sb[:, :, :].rearrange("p t (o b) -> p (t o) b", b=FEAT),
                       env.layer0[:, :, :].rearrange("p t (o b) -> p (t o) b", b=FEAT),
                       mean[:, :], var[:, :], slots, root)
            dve.sem_inc(x1_ready, 1)
            dve.sem_inc(tb.group_ready, NWINS)
            tb.make_mix(dve)

            def compare(b, i, more):
                w = i * 2 + b + EARLY
                dve.wait_ge(landed[b], (i + 1) * (16 * NWIN))
                find_last_edges(nc, dve, env, got[:, b, :, :], cmp, n_le, n_eq, find_step,
                                (i * 2 + b) * FIND_STEPS, bass.ds(w * NWIN, NWIN))
                if more:
                    nc.vector.tensor_copy(idx[:, b, :], env.win_idx[:, bass.ds((w + 2) * NWIN, NWIN)]
                                          ).then_inc(idx_ready, 1)
            with dve.Fori(0, late // 2 - 1) as i:
                for b in range(2):
                    compare(b, i, True)
            for b in range(2):
                compare(b, late // 2 - 1, False)


class Norm:

    def __init__(self, nc, env, s):
        self.nc, self.env = nc, env
        s = Scope(nc, s.ctx, s.prefix + "n")
        self.count = s.sb("count", [P, COLS])
        self.rel = s.sb("rel", [P, COLS], BF16)
        self.in_first = s.sb("in_first", [P, COLS], BF16)
        self.in_last = s.sb("in_last", [P, COLS], BF16)
        self.is_end = self.in_first
        self.mine = s.sb("mine", [P, COLS], BF16)
        self.ends = s.sb("ends", [P, 2, RELS])
        self.length = s.sb("length", [P, 1])
        self.carry_in = s.sb("carry_in", [RELS, 2, P])
        self.carry_row = s.sb("carry_row", [RELS, 2, P])
        self.start_row = s.sb("start_row", [RELS, 2, P])
        self.start = s.sb("start", [P, 2, RELS])
        self.ends_ps = s.ps("ends_ps", [RELS, 2, P])
        self.start_ps = s.ps("start_ps", [P, 2, RELS])
        (self.padded, self.type_in, self.dst_in, self.summed, self.turned, self.rows_ready, self.returned,
         self.step, self.ends_step, self.count_step) = map(s.sem, (
             "padded", "type_in", "dst_in", "summed", "turned", "rows_ready", "returned", "nstep", "ends_step",
             "count_step"))

    def sp(self, sp):
        rows, typ = P - 1, self.env.norm[:, :].bitcast(I32)
        split = rows * COLS
        sp.wait_ge(self.padded, 1)
        sp.dma_start(typ[0:rows, :], self.env.type8[0:split].rearrange("(p c) -> p c", p=rows)
                     ).then_inc(self.type_in, 16)
        sp.dma_start(typ[rows:P, 0:LAST_VALID],
                     self.env.type8[split:EDGES].rearrange("(p c) -> p c", p=1)).then_inc(self.type_in, 16)
        sp.dma_start(self.count[:, :], self.env.dst_d[LEAD:LEAD + P * COLS].rearrange("(p c) -> p c", c=COLS)
                     ).then_inc(self.dst_in, 16)

    def pe(self, pe):
        pe.wait_ge(self.summed, RELS)
        for j in range(2):
            self.nc.tensor.transpose(self.ends_ps[:, j, :], self.ends[:, j, :],
                                     self.env.ident[:, :]).then_inc(self.turned, 1)
        pe.wait_ge(self.rows_ready, 1)
        for j in range(2):
            self.nc.tensor.transpose(self.start_ps[:, j, :], self.start_row[:, j, :],
                                     self.env.ident[0:RELS, 0:RELS]).then_inc(self.returned, 1)

    def dve(self, dve):
        nc, env = self.nc, self.env
        count, mine = self.count, self.mine
        dst_f = count
        typ = env.norm[:, :].bitcast(I32)
        st = Steps(dve, self.step)
        nc.vector.memset(typ[:, LAST_VALID:], 0).then_inc(self.padded, 1)
        dve.wait_ge(self.type_in, 32)
        st(nc.vector.tensor_copy(self.rel[:, :], typ))
        dve.wait_ge(self.dst_in, 16)
        st(nc.vector.tensor_scalar(self.in_first[:, :], dst_f[:, :], dst_f[:, 0:1], None, ALU.is_equal))
        st(nc.vector.tensor_scalar(self.in_last[:, :], dst_f[:, :], dst_f[:, COLS - 1:COLS], None, ALU.is_equal))
        st(nc.vector.memset(self.carry_in[:, :, :], 0.0))
        st(nc.vector.memset(self.start_row[:, :, :], 0.0))
        st.wait()
        st(nc.vector.tensor_reduce(self.length[:, :], self.in_first[:, :], AX.X, ALU.add))
        st(nc.vector.memset(env.norm[:, :], 0.0))
        st.wait()
        st(nc.vector.tensor_tensor(env.fix_idx[:, :], env.fix_base[:, :], self.length[:, :], ALU.add))
        per = 2
        with dve.Fori(0, RELS) as r:
            stl = Steps(dve, self.ends_step, r * per)
            for j, seg in enumerate((self.in_first, self.in_last)):
                stl(nc.vector.scalar_tensor_tensor(mine[:, :], self.rel[:, :], env.rel_id[:, bass.ds(r, 1)], seg[:, :],
                                                   ALU.is_equal, ALU.mult, accum_out=self.ends[:, j, bass.ds(r, 1)]))
                stl.wait()
            dve.sem_inc(self.summed, 1)
            assert stl.n == per
        st(nc.vector.tensor_scalar(self.is_end[:, :], env.keep[:, 1:COLS + 1], -1.0, 1.0, ALU.mult, ALU.add))
        dve.wait_ge(self.turned, 2)
        cont = env.cont_row[0:RELS, 1:P]
        st(nc.vector.tensor_tensor(self.carry_in[:, 0, 1:P], cont, self.ends_ps[:, 1, 0:P - 1], ALU.mult))
        st(nc.vector.tensor_tensor(self.carry_in[:, 1, 0:P - 1], cont, self.ends_ps[:, 0, 1:P], ALU.mult))
        st.wait()
        st(nc.vector.tensor_tensor_scan(self.carry_row[:, 0, :], env.pass_row[0:RELS, :], self.carry_in[:, 0, :], 0.0,
                                        ALU.mult, ALU.add))
        st(nc.vector.tensor_tensor_scan(self.carry_row[:, 1, ::-1], env.back_row[0:RELS, ::-1],
                                        self.carry_in[:, 1, ::-1], 0.0, ALU.mult, ALU.add))
        st.wait()
        st(nc.vector.tensor_copy(self.start_row[:, 0, :], self.carry_row[:, 0, :]))
        st(nc.vector.tensor_tensor(self.start_row[:, 1, 0:P - 1], self.carry_row[:, 0, 1:P],
                                   self.carry_row[:, 1, 0:P - 1], ALU.add))
        st.wait()
        dve.sem_inc(self.rows_ready, 1)
        dve.wait_ge(self.returned, 2)
        st(nc.vector.tensor_copy(self.start[:, :, :], self.start_ps[:, :, :]))
        st.wait()
        per = 6
        with dve.Fori(0, RELS) as r:
            stl = Steps(dve, self.count_step, r * per)
            at = bass.ds(r, 1)
            stl(nc.vector.tensor_scalar(mine[:, :], self.rel[:, :], env.rel_id[:, at], None, ALU.is_equal))
            stl.wait()
            stl(nc.vector.tensor_tensor_scan(count[:, :], env.keep[:, 0:COLS], mine[:, :], self.start[:, 0, at],
                                             ALU.mult, ALU.add))
            stl.wait()
            stl(nc.vector.tensor_tensor(count[:, :], count[:, :], self.is_end[:, :], ALU.mult))
            stl.wait()
            stl(nc.vector.tensor_tensor_scan(count[:, ::-1], env.keep[:, COLS:0:-1], count[:, ::-1],
                                             self.start[:, 1, at], ALU.mult, ALU.add))
            stl.wait()
            stl(nc.vector.tensor_tensor(count[:, :], count[:, :], mine[:, :], ALU.mult))
            stl.wait()
            stl(nc.vector.tensor_tensor(env.norm[:, :], env.norm[:, :], count[:, :], ALU.add))
            stl.wait()
            assert stl.n == per
        st(nc.vector.tensor_scalar_max(env.norm[:, :], env.norm[:, :], 1.0))
        st.wait()
        st(nc.vector.reciprocal(env.norm[:, :], env.norm[:, :]))
        st.wait()


def stage_sum1(nc, env, name, table, sums, with_norm):
    with ExitStack() as ctx:
        s = Scope(nc, ctx, name)
        rows = s.sb("rows", [P, RING, WIN, FEAT])
        idx = s.sb("idx", [P, RING, WIN], I32)
        so_far = s.sb("so_far", [P, FEAT])
        idx_ready, claimed, summed, step, start = map(s.sem, ("idx_ready", "claimed", "summed", "step", "start"))
        landed = [s.sem(f"landed{b}") for b in range(RING)]
        stored = [s.sem(f"stored{b}") for b in range(RING)]
        norm = Norm(nc, env, s) if with_norm else None
        block = s.block()
        out = sums.rearrange("(p c) f -> p c f", p=P)
        turns = WINS // RING

        @block.gpsimd
        def _(pool):
            with pool.Fori(0, turns) as i:
                for b in range(RING):
                    pool.wait_ge(idx_ready, i * RING + b + 1)
                    pool.sem_inc(claimed, 1)
                    fetch(pool, rows[:, b], table, idx[:, b], WIN, landed[b])

        @block.sync
        def _(sp):
            if norm:
                norm.sp(sp)
            with sp.Fori(0, turns) as i:
                for b in range(RING):
                    sp.wait_ge(summed, i * RING + b + 1)
                    sp.dma_start(out[:, bass.ds((i * RING + b) * WIN, WIN), :], rows[:, b, :, :]
                                 ).then_inc(stored[b], 16)
            for b in range(RING):
                sp.wait_ge(stored[b], 16 * turns)

        if norm:
            @block.tensor
            def _(pe):
                norm.pe(pe)

        @block.vector
        def _(dve):
            nc.vector.memset(so_far[:, :], 0.0).then_inc(start, 1)
            for b in range(RING):
                nc.vector.tensor_copy(idx[:, b, :], env.idx1[:, b * WIN:(b + 1) * WIN]).then_inc(idx_ready, 1)
            dve.wait_ge(start, 1)
            if norm:
                norm.dve(dve)
            per = 3

            def refill(b, i):
                dve.wait_ge(stored[b], (i + 1) * 16)
                nc.vector.tensor_copy(idx[:, b, :], env.idx1[:, bass.ds(((i + 1) * RING + b) * WIN, WIN)]
                                      ).then_inc(idx_ready, 1)

            def turn(i, more):
                for b in range(RING):
                    w = i * RING + b
                    st = Steps(dve, step, w * per)
                    dve.wait_ge(landed[b], (i + 1) * (16 * WIN))
                    scale = env.norm[:, bass.ds(w * WIN, WIN)].unsqueeze(2).to_broadcast([P, WIN, FEAT])
                    st(nc.vector.tensor_tensor(rows[:, b, :, :], rows[:, b, :, :], scale, ALU.mult))
                    st.wait()
                    for f in range(FEAT):
                        one = nc.vector.tensor_tensor_scan(rows[:, b, :, f], env.keep[:, bass.ds(w * WIN, WIN)],
                                                           rows[:, b, :, f], so_far[:, f:f + 1], ALU.mult, ALU.add)
                    st(one)
                    st.wait()
                    dve.sem_inc(summed, 1)
                    st(nc.vector.tensor_copy(so_far[:, :], rows[:, b, WIN - 1, :]))
                    st.wait()
                    if more and b:
                        refill(b - 1, i)
                    assert st.n == per
                if more:
                    refill(RING - 1, i)
            with dve.Fori(0, turns - 1) as i:
                turn(i, True)
            turn(turns - 1, False)


def stage_nodes1(nc, env, name, sums, root_d, bias, x1_d, table_args):
    last_stage = table_args is None
    with ExitStack() as ctx:
        s = Scope(nc, ctx, name)
        root = s.sb("root", [P, TILES, ROW0])
        x1 = s.sb("x1", [P, TILES, ROW0] if last_stage else [P, 1, 1])
        bias_in = s.sb("bias_in", [P, FEAT])
        root_in = s.sem("root_in")
        tb = None if last_stage else Table(nc, env, s, root, *table_args)
        ends = s.sb("ends", [P, 2, FEAT])
        carry_in = s.sb("carry_in", [FEAT, P])
        carry_row = s.sb("carry_row", [FEAT, P])
        idx = s.sb("idx", [P, 2, NWIN], I32)
        got = s.sb("got", [P, 2, NWIN, FEAT])
        big = s.sb("big", [P, NWIN, FEAT])
        here = s.sb("here", [P, NWIN, FEAT])
        stat1 = s.sb("stat1", [P, NWIN])
        stat2 = s.sb("stat2", [P, NWIN])
        small_ps = s.ps("small_ps", [P, 2, P]) if last_stage else tb.turn_ps[0][:, 0:2 * P].rearrange(
            "p (a b) -> p a b", a=2)
        last_ps = small_ps[0:FEAT, 0, :]
        carry_ps = small_ps[:, 1, 0:FEAT]
        ends_in, fix_in, turned, carry_ready, carry_back, fixed, patched = map(
            s.sem, ("ends_in", "fix_in", "turned", "carry_ready", "carry_back", "fixed", "patched"))
        idx_ready, claimed, step, step2, asked, answered, finished, stored = map(
            s.sem, ("idx_ready", "claimed", "step", "step2", "asked", "answered", "finished", "stored"))
        landed = [s.sem(f"landed{b}") for b in range(2)]
        block = s.block()

        @block.sync
        def _(sp):
            sp.dma_start(ends[:, 1, :], sums.rearrange("(p c) f -> p c f", p=P)[:, COLS - 1, :]
                         ).then_inc(ends_in, 16)
            sp.dma_start(bias_in[:, :], bias.rearrange("(a c) -> a c", a=1).to_broadcast([P, FEAT])
                         ).then_inc(root_in, 16)
            sp.dma_start(root[:, :, :], root_d.rearrange("(t n) f -> n t f", n=P)).then_inc(root_in, 16)
            if last_stage:
                sp.dma_start(x1[:, :, :], x1_d.rearrange("(t n) f -> n t f", n=P)).then_inc(root_in, 16)
            else:
                tb.load_weights(sp)
                tb.sp(sp)
            if last_stage:
                part = TPW * P * CH
                with sp.Fori(0, NWINS - 1) as w:
                    sp.wait_ge(finished, w + 1)
                    sp.dma_start(env.out[bass.ds(w * part, part), :].rearrange("(t n o) b -> n t (o b)", n=P, o=CH),
                                 root[:, bass.ds(w * TPW, TPW), :]).then_inc(stored, 16)
                sp.wait_ge(finished, NWINS)
                sp.dma_start(env.out[(NWINS - 1) * part:(TILES - 1) * P * CH, :]
                             .rearrange("(t n o) b -> n t (o b)", n=P, o=CH),
                             root[:, (NWINS - 1) * TPW:TILES - 1, :]).then_inc(stored, 16)
                sp.dma_start(env.out[(TILES - 1) * P * CH:NODES1, :].rearrange("(n o) b -> n (o b)", o=CH),
                             root[0:TAIL, TILES - 1, :]).then_inc(stored, 16)
                sp.wait_ge(stored, 16 * (NWINS + 1))

        @block.gpsimd
        def _(pool):
            pool.indirect_dma_start(out=ends[:, 0, :], out_offset=None, in_=sums,
                                    in_offset=bass.IndirectOffsetOnAxis(ap=env.fix_idx[:, 0:1], axis=0)
                                    ).then_inc(fix_in, 16)
            pool.wait_ge(fixed, 1)
            pool.indirect_dma_start(out=sums, out_offset=bass.IndirectOffsetOnAxis(ap=env.fix_idx[:, 0:1], axis=0),
                                    in_=ends[:, 0, :], in_offset=None).then_inc(patched, 16)
            pool.wait_ge(patched, 16)

            def window(b, ready):
                pool.wait_ge(idx_ready, ready)
                pool.sem_inc(claimed, 1)
                fetch(pool, got[:, b], sums, idx[:, b], NWIN, landed[b])
            window(0, 1)
            with pool.Fori(0, NWINS // 2) as i:
                window(1, i * 2 + 2)
                window(0, i * 2 + 3)

        @block.tensor
        def _(pe):
            pe.wait_ge(ends_in, 16)
            nc.tensor.transpose(last_ps, ends[:, 1, :], env.ident[:, :]).then_inc(turned, 1)
            pe.wait_ge(carry_ready, 1)
            nc.tensor.transpose(carry_ps, carry_row[:, :], env.ident[0:FEAT, 0:FEAT]).then_inc(carry_back, 1)
            if tb:
                tb.pe(pe)

        @block.scalar
        def _(act):
            if tb:
                tb.act(act)
            if last_stage:
                with act.Fori(0, NWINS) as w:
                    act.wait_ge(asked, w * 3 + 1)
                    nc.scalar.activation(big[:, :, :], here[:, :, :], ACT.Exp).then_inc(answered, 1)
                    act.wait_ge(asked, w * 3 + 2)
                    nc.scalar.activation(stat1[:, :], stat1[:, :], ACT.Ln).then_inc(answered, 1)
                    act.wait_ge(asked, w * 3 + 3)
                    nc.scalar.activation(stat2[:, :], stat2[:, :], ACT.Sqrt).then_inc(answered, 1)

        @block.vector
        def _(dve):
            st = Steps(dve, step)
            st(nc.vector.memset(carry_in[:, 0:1], 0.0))
            for b in range(2):
                nc.vector.tensor_copy(idx[:, b, :], env.end_idx[:, b * NWIN:(b + 1) * NWIN]).then_inc(idx_ready, 1)
            dve.wait_ge(turned, 1)
            st(nc.vector.tensor_tensor(carry_in[:, 1:P], env.cont_row[0:FEAT, 1:P], last_ps[:, 0:P - 1], ALU.mult))
            st.wait()
            nc.vector.tensor_tensor_scan(carry_row[:, :], env.pass_row[0:FEAT, :], carry_in[:, :], 0.0,
                                         ALU.mult, ALU.add).then_inc(carry_ready, 1)
            dve.wait_ge(carry_back, 1)
            dve.wait_ge(fix_in, 16)
            nc.vector.tensor_tensor(ends[:, 0, :], ends[:, 0, :], carry_ps, ALU.add).then_inc(fixed, 1)
            if tb:
                tb.make_mix(dve)
            dve.wait_ge(root_in, 48 if last_stage else 32)
            per = 17 if last_stage else 4
            windowed = lambda buf, w: buf[:, bass.ds(w * TPW, TPW), :].rearrange("p t (o c) -> p (t o) c", c=FEAT)

            def output(st2, w, to):
                stat = lambda v: v.unsqueeze(2).to_broadcast([P, NWIN, FEAT])

                def ask(n):
                    dve.sem_inc(asked, 1)
                    dve.wait_ge(answered, w * 3 + n)
                st2(nc.vector.tensor_reduce(stat1[:, :], here[:, :, :], AX.X, ALU.max))
                st2.wait()
                st2(nc.vector.tensor_tensor(here[:, :, :], here[:, :, :], stat(stat1[:, :]), ALU.subtract))
                st2.wait()
                ask(1)
                st2(nc.vector.tensor_reduce(stat1[:, :], big[:, :, :], AX.X, ALU.add))
                st2.wait()
                ask(2)
                st2(nc.vector.tensor_tensor(here[:, :, :], here[:, :, :], stat(stat1[:, :]), ALU.subtract))
                st2.wait()
                st2(nc.vector.tensor_tensor(here[:, :, :], here[:, :, :], windowed(x1, w), ALU.add))
                st2.wait()
                layer_norm(nc, st2, here[:, :, :], big[:, :, :], stat1[:, :], stat2[:, :], NWIN, lambda: ask(3))
                st2(nc.vector.tensor_scalar(to, here[:, :, :], 1.0, None, ALU.mult))
                st2.wait()
                dve.sem_inc(finished, 1)

            def window(b, w, arrived, more):
                dve.wait_ge(landed[b], arrived)
                st2 = Steps(dve, step2, w * per)
                some = env.has_edge[:, bass.ds(w * NWIN, NWIN)].unsqueeze(2).to_broadcast([P, NWIN, FEAT])
                st2(nc.vector.tensor_tensor(got[:, b, :, :], got[:, b, :, :], some, ALU.mult))
                st2.wait()
                st2(nc.vector.tensor_tensor(got[:, b, :, :], got[:, b, :, :],
                                            bias_in[:, :].unsqueeze(1).to_broadcast([P, NWIN, FEAT]), ALU.add))
                st2.wait()
                to = windowed(root, w)
                st2(nc.vector.tensor_tensor(here[:, :, :] if last_stage else to, to, got[:, b, :, :], ALU.add))
                st2.wait()
                if more:
                    nc.vector.tensor_copy(idx[:, b, :], env.end_idx[:, bass.ds((w + 2) * NWIN, NWIN)]
                                          ).then_inc(idx_ready, 1)
                if last_stage:
                    output(st2, w, to)
                else:
                    st2(nc.vector.tensor_scalar(to, to, 0.0, None, ALU.max))
                    st2.wait()
                    dve.sem_inc(tb.group_ready, 1)
                assert st2.n == per, st2.n
            full = 16 * NWIN
            with dve.Fori(0, NWINS // 2 - 1) as i:
                for b in range(2):
                    window(b, i * 2 + b, (i + 1) * full, True)
            window(0, NWINS - 3, (NWINS // 2) * full, True)
            window(1, NWINS - 2, (NWINS // 2) * full, False)
            window(0, NWINS - 1, (NWINS // 2 + 1) * full, False)


class Env:
    pass


def gnn_layers(nc, x, src, dst, type6, type8, w0, b0, w1, root1, bias1, w2, root2, bias2, eye, out):
    env = Env()
    env.x, env.src, env.dst, env.type6, env.type8, env.eye, env.out = x, src, dst, type6, type8, eye, out
    env.w0, env.b0 = w0, b0
    dram = lambda name, shape, dt=F32: nc.dram_tensor(name, shape, dt, kind="Internal").ap()
    env.idx0_d = dram("idx0_d", (ROUNDS * ROUND,), I32)
    env.dst_d = dram("dst_d", (LEAD + ROUNDS * ROUND,))
    env.dst_rows = env.dst_d[0:LEAD + P * COLS].rearrange("(r c) -> r c", c=WIN)
    env.end_d = dram("end_d", (TPW * P * CH,), I32)
    env.some_d = dram("some_d", (TPW * P * CH,))
    env.table0 = dram("table0", (NODES0 * TYPES0, ROW0))
    env.sums0 = dram("sums0", (ROUND, ROW0))
    table1 = dram("table1", (NODES1 * RELS, FEAT))
    table2 = dram("table2", (NODES1 * RELS, FEAT))
    root1_d = dram("root1_d", (TILES * P, ROW0))
    root2_d = dram("root2_d", (TILES * P, ROW0))
    x1_d = dram("x1_d", (TILES * P, ROW0))
    sums1 = dram("sums1", (P * COLS, FEAT))
    sums2 = dram("sums2", (P * COLS, FEAT))
    slots = TILES * CH
    with ExitStack() as ctx:
        ctx.enter_context(nc.allow_non_contiguous_dma(reason="single columns of the edge list, a few of them"))
        s = Scope(nc, ctx, "all")
        env.ident = s.sb("ident", [P, P])
        env.idx1 = s.sb("idx1", [P, COLS], I32)
        env.keep = s.sb("keep", [P, COLS + 1], BF16)
        env.cont_row = s.sb("cont_row", [P, P])
        env.pass_row = s.sb("pass_row", [P, P])
        env.back_row = s.sb("back_row", [P, P])
        env.fix_idx = s.sb("fix_idx", [P, 1], I32)
        env.fix_base = s.sb("fix_base", [P, 1], I32)
        env.rel_id = s.sb("rel_id", [P, RELS])
        env.end_idx = s.sb("end_idx", [P, slots], I32)
        env.has_edge = s.sb("has_edge", [P, slots])
        with ExitStack() as early:
            e = Scope(nc, early, "early")
            env.block_first = e.sb("block_first", [1, ROUNDS * PER_ROUND], I32)
            env.first_dst = e.sb("first_dst", [P, 1])
            env.round_at = e.sb("round_at", [P, ROUNDS + 1])
            env.node = e.sb("node", [P, slots])
            env.win_row = e.sb("win_row", [P, slots])
            env.win_idx = e.sb("win_idx", [P, slots], I32)
            env.end0 = e.sb("end0", [P, TILES], I32)
            env.some0 = e.sb("some0", [P, TILES])
            stage_edges(nc, env)
            stage_first(nc, env)
            env.layer0 = e.sb("layer0", [P, TILES, ROW0])
            stage_sum0(nc, env)
            stage_x1(nc, env, (w1, root1), table1, root1_d, x1_d)
        env.norm = s.sb("norm", [P, COLS])
        stage_sum1(nc, env, "s1", table1, sums1, True)
        stage_nodes1(nc, env, "n1", sums1, root1_d, bias1, x1_d, ((w2, root2), table2, root2_d))
        stage_sum1(nc, env, "s2", table2, sums2, False)
        stage_nodes1(nc, env, "n2", sums2, root2_d, bias2, x1_d, None)


def kernel(**inputs):
    import numpy as _np
    import concourse.bacc as _bacc
    from concourse import mybir as _mybir
    from concourse.bass_utils import run_bass_kernel_spmd as _run

    nc = _bacc.Bacc("TRN2", target_bir_lowering=False, num_devices=1)
    names = ["x", "src", "dst", "edge_type_6", "edge_type_8", "L0_gnn_W", "L0_gnn_Bv", "L1_gnn_W1",
             "L1_gnn_root1", "L1_gnn_b1", "L1_gnn_W2", "L1_gnn_root2", "L1_gnn_b2", "eye"]
    arrays, args = {}, []
    for name in names:
        a = _np.eye(P, dtype=_np.float32) if name == "eye" else _np.asarray(inputs[name])
        if name == "L0_gnn_W":
            a = a.transpose(2, 0, 1).reshape(CH, TYPES0 * CH)
        a = _np.ascontiguousarray(a)
        arrays[f"in_{name}_dram"] = a
        args.append(nc.dram_tensor(f"in_{name}_dram", a.shape, _mybir.dt.from_np(a.dtype), kind="ExternalInput").ap())
    args.append(nc.dram_tensor("out_0_dram", (NODES1, FEAT), _mybir.dt.float32, kind="ExternalOutput").ap())
    gnn_layers(nc, *args)
    r = _run(nc, [arrays], core_ids=[0])
    return r.results[0]["out_0_dram"]
```
